# Optimizing a Trainium2 kernel written in Bass

```python
import numpy as np
import jax
import jax.numpy as jnp

def _softmax(x, axis=-1):
    return jax.nn.softmax(x, axis=axis)

def _gelu(x):
    return jax.nn.gelu(x, approximate=True)

def _silu(x):
    return jax.nn.silu(x)

def _sigmoid(x):
    return jax.nn.sigmoid(x)

def _layernorm(x, axis=-1, eps=1e-05):
    m = jnp.mean(x, axis=axis, keepdims=True)
    v = jnp.var(x, axis=axis, keepdims=True)
    return (x - m) / jnp.sqrt(v + eps)

def _scatter_add(tgt, idx, src, axis=0):
    return tgt.at[idx].add(src)

def _segment_sum(src, seg, n):
    return jax.ops.segment_sum(src, seg, n)
kernel_name = 'mk_xattn_ffn_d2_seqx_r8_13cc3f'

def setup_inputs(seed: int=0):
    np.random.seed(seed)
    _w = jnp.asarray

    def _rec_inputs():
        import jax
        import jax.numpy as jnp
        _rk = jax.random.key(seed)
        x = -0.0002928 + 1 * jax.random.normal(jax.random.fold_in(_rk, 1), (16, 128, 256), jnp.float32)
        _lenS = 128 - jax.random.randint(jax.random.fold_in(_rk, 7), (16,), 0, max(1, 128 // 4) + 1, jnp.int32)
        _lenS2 = 128 - jax.random.randint(jax.random.fold_in(_rk, 8), (16,), 0, max(1, 128 // 4) + 1, jnp.int32)
        _ctx_512P = jax.random.normal(jax.random.fold_in(_rk, 11), (16, 16, 64), jnp.float32)
        _ctx_512c = jax.random.dirichlet(jax.random.fold_in(_rk, 511), 0.3 * jnp.ones((16,), jnp.float32), (16, 128))
        _ctx_512t = jnp.einsum('bsk,bkd->bsd', _ctx_512c, _ctx_512P)
        _ctx_512t = _ctx_512t * jax.lax.rsqrt(jnp.mean(jnp.square(_ctx_512t)) + 1e-12) * 0.953939
        ctx_512 = 0.000227908 + 0.99994 * (_ctx_512t + 0.3 * jax.random.normal(jax.random.fold_in(_rk, 611), (16, 128, 64), jnp.float32))
        return (x, ctx_512)
    x, ctx_512 = _rec_inputs()

    def _L0_xattn_setup():
        import jax, jax.numpy as jnp
        import numpy as np
        B, S, L = (2, 128, 128)
        DIM_Q, H, K, D_C, D_CQ, R = (256, 16, 128, 64, 192, 64)

        def _rope_tables(length, dim):
            inv = 1.0 / 10000.0 ** (jnp.arange(0, dim, 2, dtype=jnp.float32) / dim)
            f = jnp.arange(length, dtype=jnp.float32)[:, None] * inv[None, :]
            sin = jnp.repeat(jnp.sin(f), 2, axis=-1)
            cos = jnp.repeat(jnp.cos(f), 2, axis=-1)
            return (sin, cos)

        def _rotate_half(x):
            half = x.shape[-1] // 2
            return jnp.concatenate([-x[..., half:], x[..., :half]], axis=-1)

        def _apply_rope(x, sin, cos):
            return x * cos + _rotate_half(x) * sin
        key = jax.random.key(seed)
        ks = jax.random.split(key, 8)
        return {'hidden_q': jax.random.normal(ks[0], (B, S, DIM_Q), jnp.float32), 'kv_c': jax.random.normal(ks[1], (B, L, D_C), jnp.float32), 'Wq': jax.random.normal(ks[2], (H * K, DIM_Q), jnp.float32) / np.sqrt(DIM_Q).astype(np.float32), 'w_kc_q': jax.random.normal(ks[3], (H, K, D_CQ), jnp.float32) / np.sqrt(K).astype(np.float32), 'w_kc_kv': jax.random.normal(ks[4], (H, K, D_C), jnp.float32) / np.sqrt(K).astype(np.float32), 'W_qr': jax.random.normal(ks[5], (H, D_CQ, R), jnp.float32) / np.float32(np.sqrt(D_CQ) * np.sqrt(R)), 'W_kr': jax.random.normal(ks[6], (H, D_C, R), jnp.float32) / np.sqrt(D_C).astype(np.float32), 'Wo': jax.random.normal(ks[7], (DIM_Q, H * K), jnp.float32) / np.sqrt(H * K).astype(np.float32)}
    _L0_xattn_all = _L0_xattn_setup()
    _L0_xattn_in = {k: v for k, v in _L0_xattn_all.items() if k in ('Wq', 'w_kc_q', 'w_kc_kv', 'W_qr', 'W_kr', 'Wo')}
    del _L0_xattn_all

    def _L0_ffn_setup():
        import jax, jax.numpy as jnp
        import numpy as np
        NUM_EXPERTS = 8
        HIDDEN = 256
        INTER = 256
        TOP_K = 2
        key = jax.random.key(seed)
        ks = jax.random.split(key, 7)
        hidden_states = jax.random.normal(ks[0], (4, 256, HIDDEN), dtype=jnp.float32)
        gate_w = jax.random.normal(ks[1], (HIDDEN, NUM_EXPERTS), dtype=jnp.float32) * 0.02
        fc1_w = jax.random.normal(ks[2], (NUM_EXPERTS, HIDDEN, INTER), dtype=jnp.float32) * 0.02
        fc1_b = jnp.zeros((NUM_EXPERTS, INTER), dtype=jnp.float32)
        fc2_w = jax.random.normal(ks[3], (NUM_EXPERTS, INTER, HIDDEN), dtype=jnp.float32) * 0.02
        fc2_b = jnp.zeros((NUM_EXPERTS, HIDDEN), dtype=jnp.float32)
        alpha = jax.random.normal(ks[4], (NUM_EXPERTS,), dtype=jnp.float32)
        return {'hidden_states': hidden_states, 'gate_w': gate_w, 'fc1_w': fc1_w, 'fc1_b': fc1_b, 'fc2_w': fc2_w, 'fc2_b': fc2_b, 'alpha': alpha}
    _L0_ffn_all = _L0_ffn_setup()
    _L0_ffn_in = {k: v for k, v in _L0_ffn_all.items() if k in ('gate_w', 'fc1_w', 'fc1_b', 'fc2_w', 'fc2_b', 'alpha')}
    del _L0_ffn_all

    def _L1_xattn_setup():
        import jax, jax.numpy as jnp
        import numpy as np
        B, S, H, NH, L = (2, 256, 256, 16, 64)
        HD = H // NH
        key = jax.random.key(seed)
        k1, k2, k3, k4, k5 = jax.random.split(key, 5)
        scale = 0.02
        return {'q': jax.random.normal(k1, (B, S, H), dtype=jnp.float32), 'latent_kv': jax.random.normal(k2, (B, S, L), dtype=jnp.float32), 'Wq': jax.random.normal(k3, (H, H), dtype=jnp.float32) * scale, 'Wkv_expand': jax.random.normal(k4, (2 * H, L), dtype=jnp.float32) * scale, 'Wout': jax.random.normal(k5, (H, H), dtype=jnp.float32) * scale}
    _L1_xattn_all = _L1_xattn_setup()
    _L1_xattn_in = {k: v for k, v in _L1_xattn_all.items() if k in ('Wq', 'Wkv_expand', 'Wout')}
    del _L1_xattn_all

    def _L1_ffn_setup():
        import jax, jax.numpy as jnp
        import numpy as np
        FP8_MAX = 448.0
        GLOBAL_DIV = 448.0 * 6.0

        def _fp8(x):
            return x.astype(jnp.float8_e4m3fn).astype(jnp.float32)

        def _reorder_quantize_x(x, idx):
            scale = jnp.max(jnp.abs(x)) / GLOBAL_DIV
            xr = (x / scale)[:, idx]
            scale_x = jnp.max(jnp.abs(xr), axis=1, keepdims=True) / FP8_MAX
            qx = _fp8(xr / scale_x)
            return (qx, scale_x, scale)

        def _qlinear(qx, scale_x, scale, W, idx, out_idx=None):
            Wr = W[:, idx]
            w_scale = jnp.max(jnp.abs(Wr), axis=1, keepdims=True) / FP8_MAX
            qw = _fp8(Wr / w_scale)
            y = qx * scale_x @ (qw * w_scale).T * scale
            if out_idx is not None:
                y = y[:, out_idx]
            return y
        key = jax.random.key(seed)
        ks = jax.random.split(key, 6)
        B, S, H, I = (2, 128, 256, 704)
        return {'x': jax.random.normal(ks[0], (B, S, H), jnp.float32), 'w_gate': jax.random.normal(ks[1], (I, H), jnp.float32) * 0.02, 'w_up': jax.random.normal(ks[2], (I, H), jnp.float32) * 0.02, 'w_down': jax.random.normal(ks[3], (H, I), jnp.float32) * 0.02, 'up_reorder_index': jax.random.permutation(ks[4], jnp.arange(H, dtype=jnp.int64)), 'down_reorder_index': jax.random.permutation(ks[5], jnp.arange(I, dtype=jnp.int64))}
    _L1_ffn_all = _L1_ffn_setup()
    _L1_ffn_in = {k: v for k, v in _L1_ffn_all.items() if k in ('w_gate', 'w_up', 'w_down', 'up_reorder_index', 'down_reorder_index')}
    del _L1_ffn_all
    return {'x': x, 'ctx_512': ctx_512, 'L0_xattn_Wq': _L0_xattn_in['Wq'], 'L0_xattn_w_kc_q': _L0_xattn_in['w_kc_q'], 'L0_xattn_w_kc_kv': _L0_xattn_in['w_kc_kv'], 'L0_xattn_W_qr': _L0_xattn_in['W_qr'], 'L0_xattn_W_kr': _L0_xattn_in['W_kr'], 'L0_xattn_Wo': _L0_xattn_in['Wo'], 'L0_ffn_gate_w': _L0_ffn_in['gate_w'], 'L0_ffn_fc1_w': _L0_ffn_in['fc1_w'], 'L0_ffn_fc1_b': _L0_ffn_in['fc1_b'], 'L0_ffn_fc2_w': _L0_ffn_in['fc2_w'], 'L0_ffn_fc2_b': _L0_ffn_in['fc2_b'], 'L0_ffn_alpha': _L0_ffn_in['alpha'], 'L1_xattn_Wq': _L1_xattn_in['Wq'], 'L1_xattn_Wkv_expand': _L1_xattn_in['Wkv_expand'], 'L1_xattn_Wout': _L1_xattn_in['Wout'], 'L1_ffn_w_gate': _L1_ffn_in['w_gate'], 'L1_ffn_w_up': _L1_ffn_in['w_up'], 'L1_ffn_w_down': _L1_ffn_in['w_down'], 'L1_ffn_up_reorder_index': _L1_ffn_in['up_reorder_index'], 'L1_ffn_down_reorder_index': _L1_ffn_in['down_reorder_index']}

def reference(x, ctx_512, L0_xattn_Wq, L0_xattn_w_kc_q, L0_xattn_w_kc_kv, L0_xattn_W_qr, L0_xattn_W_kr, L0_xattn_Wo, L0_ffn_gate_w, L0_ffn_fc1_w, L0_ffn_fc1_b, L0_ffn_fc2_w, L0_ffn_fc2_b, L0_ffn_alpha, L1_xattn_Wq, L1_xattn_Wkv_expand, L1_xattn_Wout, L1_ffn_w_gate, L1_ffn_w_up, L1_ffn_w_down, L1_ffn_up_reorder_index, L1_ffn_down_reorder_index):
    import jax
    import jax.numpy as jnp

    def _L0_xattn_ref(hidden_q, kv_c, Wq, w_kc_q, w_kc_kv, W_qr, W_kr, Wo):
        import jax, jax.numpy as jnp
        import numpy as np
        B, S, L = (2, 128, 128)
        DIM_Q, H, K, D_C, D_CQ, R = (256, 16, 128, 64, 192, 64)

        def _rope_tables(length, dim):
            inv = 1.0 / 10000.0 ** (jnp.arange(0, dim, 2, dtype=jnp.float32) / dim)
            f = jnp.arange(length, dtype=jnp.float32)[:, None] * inv[None, :]
            sin = jnp.repeat(jnp.sin(f), 2, axis=-1)
            cos = jnp.repeat(jnp.cos(f), 2, axis=-1)
            return (sin, cos)

        def _rotate_half(x):
            half = x.shape[-1] // 2
            return jnp.concatenate([-x[..., half:], x[..., :half]], axis=-1)

        def _apply_rope(x, sin, cos):
            return x * cos + _rotate_half(x) * sin
        Bv, Sv, _ = hidden_q.shape
        _, Lv, _ = kv_c.shape
        q_hk = (hidden_q @ Wq.T).reshape(Bv, Sv, H, K)
        q_big = jnp.einsum('bshk,hkq->bshq', q_hk, w_kc_q)
        sin_q, cos_q = _rope_tables(Sv, D_CQ)
        q_big = _apply_rope(q_big, sin_q[None, :, None, :], cos_q[None, :, None, :])
        sin_k, cos_k = _rope_tables(Lv, D_C)
        kv_r = _apply_rope(kv_c, sin_k[None], cos_k[None])
        q_r = jnp.einsum('bshq,hqr->bhsr', q_big, W_qr)
        k_r = jnp.einsum('bld,hdr->bhlr', kv_r, W_kr)
        scores = jnp.einsum('bhsr,bhlr->bhsl', q_r, k_r)
        attn = jax.nn.softmax(scores, axis=-1)
        ctx_c = jnp.einsum('bhsl,bld->bhsd', attn, kv_r)
        ctx_lat = jnp.einsum('bhsd,hkd->bhsk', ctx_c, w_kc_kv)
        ctx = ctx_lat.transpose(0, 2, 1, 3).reshape(Bv, Sv, H * K)
        return ctx @ Wo.T

    def _L0_ffn_ref(hidden_states, gate_w, fc1_w, fc1_b, fc2_w, fc2_b, alpha):
        import jax, jax.numpy as jnp
        import numpy as np
        NUM_EXPERTS = 8
        HIDDEN = 256
        INTER = 256
        TOP_K = 2
        B, S, H = hidden_states.shape
        x = hidden_states.reshape(-1, H)
        probs = jax.nn.softmax(x @ gate_w, axis=-1)
        gate_score, gate_idx = jax.lax.top_k(probs, TOP_K)
        gate_score = gate_score / jnp.sum(gate_score, axis=-1, keepdims=True)
        onehot = jax.nn.one_hot(gate_idx, NUM_EXPERTS, dtype=x.dtype)
        combine = jnp.einsum('tk,tke->te', gate_score, onehot) * alpha[None, :]
        h = jnp.einsum('th,ehi->eti', x, fc1_w) + fc1_b[:, None, :]
        h = jax.nn.gelu(h, approximate=False)
        y = jnp.einsum('eti,eih->eth', h, fc2_w) + fc2_b[:, None, :]
        out = jnp.einsum('eth,te->th', y, combine)
        return out.reshape(B, S, H)

    def _L1_xattn_ref(q, latent_kv, Wq, Wkv_expand, Wout):
        import jax, jax.numpy as jnp
        import numpy as np
        B, S, H, NH, L = (2, 256, 256, 16, 64)
        HD = H // NH
        b, sq, _ = q.shape
        sk = latent_kv.shape[1]
        qp = q @ Wq.T
        kv = latent_kv @ Wkv_expand.T
        k, v = jnp.split(kv, 2, axis=-1)
        qh = qp.reshape(b, sq, NH, HD).transpose(0, 2, 1, 3)
        kh = k.reshape(b, sk, NH, HD).transpose(0, 2, 1, 3)
        vh = v.reshape(b, sk, NH, HD).transpose(0, 2, 1, 3)
        inv_sqrt_d = 1.0 / jnp.sqrt(jnp.float32(HD))
        scores = jnp.einsum('bhqd,bhkd->bhqk', qh, kh) * inv_sqrt_d
        causal = jnp.tril(jnp.ones((sq, sk), dtype=bool))
        scores = jnp.where(causal, scores, jnp.finfo(scores.dtype).min)
        attn = jax.nn.softmax(scores, axis=-1)
        out = jnp.einsum('bhqk,bhkd->bhqd', attn, vh)
        out = out.transpose(0, 2, 1, 3).reshape(b, sq, H)
        return out @ Wout.T

    def _L1_ffn_ref(x, w_gate, w_up, w_down, up_reorder_index, down_reorder_index):
        import jax, jax.numpy as jnp
        import numpy as np
        FP8_MAX = 448.0
        GLOBAL_DIV = 448.0 * 6.0

        def _fp8(x):
            return x.astype(jnp.float8_e4m3fn).astype(jnp.float32)

        def _reorder_quantize_x(x, idx):
            scale = jnp.max(jnp.abs(x)) / GLOBAL_DIV
            xr = (x / scale)[:, idx]
            scale_x = jnp.max(jnp.abs(xr), axis=1, keepdims=True) / FP8_MAX
            qx = _fp8(xr / scale_x)
            return (qx, scale_x, scale)

        def _qlinear(qx, scale_x, scale, W, idx, out_idx=None):
            Wr = W[:, idx]
            w_scale = jnp.max(jnp.abs(Wr), axis=1, keepdims=True) / FP8_MAX
            qw = _fp8(Wr / w_scale)
            y = qx * scale_x @ (qw * w_scale).T * scale
            if out_idx is not None:
                y = y[:, out_idx]
            return y
        B, S, H = x.shape
        xf = x.reshape(B * S, H)
        qx, sx, sc = _reorder_quantize_x(xf, up_reorder_index)
        g = _qlinear(qx, sx, sc, w_gate, up_reorder_index, out_idx=down_reorder_index)
        u = _qlinear(qx, sx, sc, w_up, up_reorder_index, out_idx=down_reorder_index)
        t = jax.nn.silu(g) * u
        qt, st, sct = _reorder_quantize_x(t, down_reorder_index)
        y = _qlinear(qt, st, sct, w_down, down_reorder_index)
        return y.reshape(B, S, H)
    x = x + _L0_xattn_ref(_layernorm(x, axis=-1), ctx_512, L0_xattn_Wq, L0_xattn_w_kc_q, L0_xattn_w_kc_kv, L0_xattn_W_qr, L0_xattn_W_kr, L0_xattn_Wo)
    x = x + _L0_ffn_ref(_layernorm(x, axis=-1), L0_ffn_gate_w, L0_ffn_fc1_w, L0_ffn_fc1_b, L0_ffn_fc2_w, L0_ffn_fc2_b, L0_ffn_alpha)
    x = x + _L1_xattn_ref(_layernorm(x, axis=-1), ctx_512, L1_xattn_Wq, L1_xattn_Wkv_expand, L1_xattn_Wout)
    x = x + _L1_ffn_ref(_layernorm(x, axis=-1), L1_ffn_w_gate, L1_ffn_w_up, L1_ffn_w_down, L1_ffn_up_reorder_index, L1_ffn_down_reorder_index)
    return x

_drawn_inputs = setup_inputs


def setup_inputs(seed=0):
    import zlib

    import numpy as np

    out = dict(_drawn_inputs(seed))
    spreads = {'L0_ffn_fc1_b': (0.0, 0.612), 'L0_ffn_fc2_b': (0.0, 0.1)}
    factors = {'L1_xattn_Wq': 64.0}
    for name, (base, spread) in spreads.items():
        noise = np.random.default_rng([zlib.crc32(name.encode()), seed]).standard_normal(out[name].shape)
        drawn = base * np.exp(spread * noise) if base else spread * noise
        out[name] = jnp.asarray(drawn.astype(out[name].dtype))
    for name, factor in factors.items():
        out[name] = (out[name] * factor).astype(out[name].dtype)
    return out
```

```python
from contextlib import ExitStack

import numpy as np

import concourse.bass as bass
from concourse import mybir

ALU = mybir.AluOpType
ACT = mybir.ActivationFunctionType
AX = mybir.AxisListType
F32 = mybir.dt.float32
BF16 = mybir.dt.bfloat16
U32 = mybir.dt.uint32

P = 128
NB = 16
D = 256
DC = D // P
DCTX = 64
H0, K0, DQ0, R0 = 16, 128, 192, 64
HALF = DQ0 // 2
NPAIR = H0 // 2
NE, TOPK = 8, 2
INTER = 256
IC = INTER // P
H1, HD1 = 16, 16
V1 = HD1 + 1
FF = 704
FCH = [(c * P, min(P, FF - c * P)) for c in range(-(-FF // P))]
FP8_MAX = 448.0
LN_EPS = 1e-5
MASKED = -3.0e38

GB = 2
GT = GB * P
NG = NB // GB
GB2 = 4
T2 = GB2 * P
NG2 = NB // GB2
SIGN_EXP = 0x7F800000


def build(nc, a, out):
    with ExitStack() as ctx:
        def sb(name, shape, dt=F32):
            return ctx.enter_context(nc.sbuf_tensor(name, shape, dt))

        def sem(name):
            return ctx.enter_context(nc.semaphore(name))

        x = sb("x", [P, NB, D])
        xnT = sb("xnT", [P, 2, DC, NB * P])
        raw = sb("raw", [P, 16384])
        work = sb("work", [P, 7168])
        wc = sb("wc", [P, DC, H0, DQ0])
        wc_flat = wc[:].rearrange("p c h q -> p (c h q)")
        wqk = sb("wqk", [HALF, H0, 2, R0])
        wvo = sb("wvo", [P, NPAIR, D])
        kvaug = sb("kvaug", [P, NB, DCTX + 1])
        kvT = sb("kvT", [P, NB * P])
        ctxT = sb("ctxT", [DCTX, NB * P])
        rope_c = sb("rope_c", [HALF, 2, GB, P])
        rope_s = sb("rope_s", [HALF, 2, GB, P])
        ident = sb("ident", [P, P])
        identb = sb("identb", [P, P], BF16)
        mask = sb("mask", [P, 4, P], BF16)
        mv = sb("mv", [P, NB, 2])
        st6 = sb("st6", [P, NB, 6])
        rstd = sb("rstd", [P, NB])
        unread = sb("unread", [P, 1])
        epst = sb("epst", [P, NB])
        veps = sb("veps", [P, NB])
        mhalf = sb("mhalf", [P, NB])
        logits = sb("logits", [P, NB, NE])

        gatew = sb("gatew", [P, DC, NE])

        def carve(region, at, parts, shape, dt=F32):
            n = int(np.prod(shape))
            if dt == BF16:
                v = region[0:parts, at:at + (n + 1) // 2].bitcast(BF16)
                v = v[:, 0:n]
            else:
                v = region[0:parts, at:at + n]
            names = "abcd"[:len(shape)]
            if len(shape) > 1:
                v = v.rearrange(f"p ({' '.join(names)}) -> p {' '.join(names)}",
                                **{k: s for k, s in zip(names[1:], shape[1:])})
            return v

        r_wq = carve(raw, 0, P, [H0, D])
        r_wkcq = carve(raw, 4096, P, [H0, DQ0])
        r_wqrT = carve(raw, 7168, R0, [H0, DQ0])
        r_wkrT = carve(raw, 10240, R0, [H0, DCTX])
        r_wkckv = carve(raw, 11264, P, [H0, DCTX])
        r_woT = carve(raw, 12288, P, [H0, D])
        xn_all = carve(work, 0, P, [NB, D])
        ctx_n = carve(work, 4096, P, [NB, DCTX])
        kvd = carve(work, 5120, P, [NB, 2, DCTX])
        ropek_c = sb("ropek_c", [P, DCTX])
        ropek_s = sb("ropek_s", [P, DCTX])
        t1 = carve(raw, 8192, HALF, [2, 512])
        t2 = carve(raw, 9216, HALF, [2, 512])
        roped = carve(raw, 10240, HALF, [2, 2, 512])
        qT = carve(raw, 12288, P, [2, GT])
        kvTg = carve(raw, 12800, P, [GT])
        prob = carve(raw, 13056, P, [2, 4, P])
        probT = carve(raw, 14080, P, [2, 4, P])
        ctxh = carve(raw, 15104, P, [2, GB, P])
        nmax = carve(raw, 15616, P, [2, 4])
        rsum = carve(raw, 15624, P, [2, 4])
        xn2 = carve(work, 0, P, [GB, D])
        ctxhT = carve(work, 512, P, [NPAIR, GT])
        xgT = carve(work, 2560, P, [DC, GT])
        fc1 = carve(raw, 0, P, [NE, DC, INTER])
        fc2 = carve(raw, 4096, P, [NE, IC, D])

        hT = carve(raw, 8192, P, [2, IC, T2])
        xn4 = carve(raw, 10240, P, [GB2, D])
        combT = carve(raw, 11264, NE, [T2])
        combg = carve(raw, 11776, P, [GB2, NE])
        expl = carve(work, 0, P, [NB, NE])
        above = carve(work, 128, P, [NB, NE, NE])
        tied = carve(work, 1152, P, [NB, NE, NE])
        rank = carve(work, 2176, P, [NB, NE])
        lmax = carve(work, 2304, P, [NB])
        comb = carve(work, 2432, P, [NB, NE])
        before = carve(work, 2560, P, [NE, NE])
        alpha = carve(work, 2624, P, [NE])
        fc1b = carve(work, 2632, P, [NE, IC])
        fc2b = carve(work, 2656, NE, [D])
        wq1 = carve(raw, 0, P, [DC, D])
        wqm = carve(raw, 512, P, [DC, DC, 2, P])
        wkv1 = carve(raw, 1536, DCTX, [2 * D])
        wout1 = carve(raw, 2048, P, [DC, D])
        vaug = carve(raw, 2560, P, [NB, H1, V1])
        q3 = carve(raw, 6912, P, [2, 2, DC, GT])
        k3 = carve(raw, 8960, P, [2, DC, GT])
        prob3 = carve(raw, 9984, P, [4, 4, P])
        probT3 = carve(raw, 12032, P, [2, 4, P])
        ctx3 = carve(raw, 13056, P, [D])
        ctx3T = carve(raw, 13312, P, [DC, P])
        nmax3 = carve(raw, 13568, P, [4, 4])
        rsum3 = carve(raw, 13584, P, [H1])
        NF = len(FCH)
        idx_a = sb("idx_a", [P, NF - 1], mybir.dt.int32)
        idx_b = sb("idx_b", [FCH[-1][1], 1], mybir.dt.int32)
        wgu_n = carve(raw, 0, P, [2 * NF, D])
        wd_n = carve(raw, 3072, P, [DC, FF])
        w_all = carve(raw, 0, P, [4480])
        v_all = carve(raw, 4480, P, [4480])
        m_all = carve(wc_flat, 0, P, [4480])
        wgu_q = carve(raw, 8960, P, [2 * NF, D], BF16)
        wd_q = carve(raw, 10496, P, [DC, FF], BF16)
        wguT = carve(raw, 11200, P, [DC, 2 * FF], BF16)
        wdT = carve(raw, 12608, P, [NF, D], BF16)
        wsb = carve(work, 0, P, [2 * FF])
        wsdb = carve(work, 1408, P, [D])
        diag = carve(work, 1664, P, [2 * NF + DC, P])
        ones = carve(work, 3456, P, [P])
        ws = carve(work, 3584, P, [2 * NF + DC])
        wr = carve(work, 3600, P, [2 * NF + DC])
        xn5 = carve(raw, 0, P, [D])
        v5 = carve(raw, 256, P, [D])
        m5 = carve(raw, 512, P, [D])
        qx = carve(raw, 768, P, [D], BF16)
        qxT = carve(raw, 896, P, [2, DC, P], BF16)
        tg = carve(raw, 1152, P, [FF])
        tu = carve(raw, 1856, P, [FF])
        tsl = carve(raw, 2560, P, [FF])
        tt = carve(raw, 3264, P, [FF])
        tv = carve(raw, 3968, P, [FF])
        tm = carve(raw, 4672, P, [FF])
        qt = carve(raw, 5376, P, [2, FF], BF16)
        qtT = carve(raw, 6080, P, [2, NF, P], BF16)
        yt = carve(raw, 6848, P, [D])
        sx = carve(raw, 7104, P, [8, 2])
        st5 = carve(raw, 7168, P, [8])
        mv5 = carve(raw, 7176, P, [2])
        ve5 = carve(raw, 7180, P, [2])

        ps = ctx.enter_context(nc.psum_tensor("ps", [P, 8, 512], F32))

        def bank(i):
            return ps[:, i, :]

        def bank16(i):
            return ps[:, i, :].bitcast(BF16)

        ld_x, ld_w, ld_c, ld_f = sem("ld_x"), sem("ld_w"), sem("ld_c"), sem("ld_f")
        ld_f1 = sem("ld_f1")
        phase_end = sem("phase_end")
        stored = sem("stored")
        dve_step = sem("dve_step")
        act_step = sem("act_step")
        pool_step = sem("pool_step")
        ln_stats, ln_rstd = sem("ln_stats"), sem("ln_rstd")
        kv_ready = sem("kv_ready")
        xn_ready = sem("xn_ready")
        norm_r, ln_a = sem("norm_r"), sem("ln_a")
        prep_mm, prep_act, prep_dve = sem("prep_mm"), sem("prep_act"), sem("prep_dve")
        q_mm, q_scaled, q_roped = sem("q_mm"), sem("q_scaled"), sem("q_roped")
        b_mm, b_out = sem("b_mm"), sem("b_out")
        kv_copied = sem("kv_copied")
        s_mm, s_max, s_exp = sem("s_mm"), sem("s_max"), sem("s_exp")
        t_mm, t_out = sem("t_mm"), sem("t_out")
        o_mm, o_out = sem("o_mm"), sem("o_out")
        u_mm, u_out = sem("u_mm"), sem("u_out")
        y_mm, y_add = sem("y_mm"), sem("y_add")
        l_stats, l_rstd, l_xn, l_mm, l_out = (sem("l_stats"), sem("l_rstd"), sem("l_xn"), sem("l_mm"),
                                              sem("l_out"))
        g_mm, g_out = sem("g_mm"), sem("g_out")

        ld_2, ld_3, ld_i, ld_g = sem("ld_2"), sem("ld_3"), sem("ld_i"), sem("ld_g")
        ld_d = sem("ld_d")
        gate_exp, gate_max, comb_ready = sem("gate_exp"), sem("gate_max"), sem("comb_ready")
        h_mm, h_out, f_mm, f_acc, f_cp = sem("h_mm"), sem("h_out"), sem("f_mm"), sem("f_acc"), sem("f_cp")
        n_a, n_stats, n_eps, n_rstd, n_xn, n_mm, n_out = (sem("n_a"), sem("n_stats"), sem("n_eps"), sem("n_rstd"),
                                                          sem("n_xn"), sem("n_mm"), sem("n_out"))
        w3_ready, v3_mm, v3_out = sem("w3_ready"), sem("v3_mm"), sem("v3_out")
        pj_mm, pj_out = sem("pj_mm"), sem("pj_out")
        s3_mm, s3_max, s3_exp, t3_mm, t3_out = (sem("s3_mm"), sem("s3_max"), sem("s3_exp"), sem("t3_mm"),
                                                sem("t3_out"))
        o3_mm, o3_r, o3_out, u3_mm, u3_out, y3_mm, y3_add = (sem("o3_mm"), sem("o3_r"), sem("o3_out"),
                                                             sem("u3_mm"), sem("u3_out"), sem("y3_mm"),
                                                             sem("y3_add"))
        pad_set = sem("pad_set")
        w4_quant, w4_diag, w4_mm, w4_out = sem("w4_quant"), sem("w4_diag"), sem("w4_mm"), sem("w4_out")
        x5, t5 = sem("x5"), sem("t5")
        x5_stats, x5_eps, x5_rstd, x5_q, x5_mm, x5_out = (sem("x5_stats"), sem("x5_eps"), sem("x5_rstd"),
                                                          sem("x5_q"), sem("x5_mm"), sem("x5_out"))
        gu_mm, g_scaled, gu_read, silu_out, t5_q, t5_mm, t5_out, y5_mm, y5_read, x5_done = (
            sem("gu_mm"), sem("g_scaled"), sem("gu_read"), sem("silu_out"), sem("t5_q"), sem("t5_mm"),
            sem("t5_out"), sem("y5_mm"), sem("y5_read"), sem("x5_done"))

        counts = {}

        def wait(eng, s, v):
            if isinstance(v, int) and v <= 0:
                return
            eng.wait_ge(s, v)

        def wait_apart(eng, s, v):
            if isinstance(v, int):
                eng.wait_ge(s, v)
                return
            eng.wait_ge(s, v)
            nc.vector.memset(unread[:], 0.0)

        def then_next(eng, ins, s, key):
            counts[key] = counts.get(key, 0) + 1
            ins.then_inc(s, 1)
            eng.wait_ge(s, counts[key])

        def barrier(eng, n, engines=5):
            eng.drain().then_inc(phase_end, 1)
            eng.wait_ge(phase_end, engines * n)

        def stage(g, i, lag, steps, groups=NG):
            if isinstance(g, int):
                f = g * steps + i - lag
                if f < 0 or f >= groups * steps:
                    return None
                return f // steps, f % steps
            back = -((i - lag) // steps)
            return g - back, (i - lag) % steps

        def pipeline(eng, groups, steps, body):
            for i in range(steps):
                body(0, i)
            with eng.Fori(1, groups) as g:
                for i in range(steps):
                    body(g, i)
            for i in range(steps):
                body(groups, i)

        B_LAG, S_LAG, T_LAG, O_LAG, U_LAG = 1, 2, 3, 4, 5
        Y_AT, L_AT, G_AT = 5, 6, 7
        STEPS2, BIAS_AT, LN_AT = NE + 2, NE, NE + 1
        STEPS3, NG3 = 16, 4
        S3, T3, O3, U3, Y3 = 4, 6, 8, 9, 10
        STEPS4, NG4 = 4, 4
        QB, BB, SB, TB, OB, MB = (0, 1), 2, 3, 5, 6, 7

        CONSTS = [("ctx", ctx_n), ("ctxT", ctxT[:]), ("ropek_c", ropek_c[:]), ("ropek_s", ropek_s[:]),
                  ("ident", ident[:]), ("rope_c", rope_c[:]), ("rope_s", rope_s[:]),
                  ("L0_ffn_gate_w", gatew[:]), ("identb", identb[:]), ("mask", mask[:])]
        N_CONST = len(CONSTS)

        block = ctx.enter_context(nc.Block())

        @block.sync
        def _(sp):
            sp.dma_start(x[:], a["x"]).then_inc(ld_x, 16)
            sp.dma_start(r_wq, a["L0_xattn_Wq"]).then_inc(ld_w, 16)
            sp.dma_start(r_wkcq, a["L0_xattn_w_kc_q"]).then_inc(ld_w, 16)
            sp.dma_start(r_wqrT, a["L0_xattn_W_qr"]).then_inc(ld_w, 16)
            sp.dma_start(r_wkrT, a["L0_xattn_W_kr"]).then_inc(ld_w, 16)
            sp.dma_start(r_wkckv, a["L0_xattn_w_kc_kv"]).then_inc(ld_w, 16)
            sp.dma_start(r_woT, a["L0_xattn_Wo"]).then_inc(ld_w, 16)
            sp.dma_start(idx_a[:], a["idx_a"]).then_inc(ld_i, 16)
            sp.dma_start(idx_b[:], a["idx_b"]).then_inc(ld_i, 16)
            barrier(sp, 1)
            sp.dma_start(fc1, a["L0_ffn_fc1_w"]).then_inc(ld_f1, 16)
            sp.dma_start(fc2, a["L0_ffn_fc2_w"]).then_inc(ld_f1, 16)
            barrier(sp, 2)
            for name, dst in (("before", before), ("L0_ffn_alpha", alpha), ("L0_ffn_fc1_b", fc1b),
                              ("L0_ffn_fc2_b", fc2b)):
                sp.dma_start(dst, a[name]).then_inc(ld_2, 16)
            barrier(sp, 3)
            for name, dst in (("L1_xattn_Wq", wq1), ("L1_xattn_Wkv", wkv1), ("L1_xattn_Wout", wout1)):
                sp.dma_start(dst, a[name]).then_inc(ld_3, 16)
            barrier(sp, 4)
            sp.dma_start(wd_n, a["L1_ffn_w_down"]).then_inc(ld_d, 16)
            barrier(sp, 5)
            with sp.Fori(0, NG4) as g:
                sp.wait_ge(x5_done, (g + 1) * STEPS4)
                sp.dma_start(out[:, bass.ds(g * STEPS4, STEPS4), :],
                             x[:, bass.ds(g * STEPS4, STEPS4), :]).then_inc(stored, 16)
            sp.wait_ge(stored, 16 * NG4)

        PREP_WC, PREP_QK, PREP_VO, PREP_KV, PREP_LN = H0, H0 // 4, NPAIR // 2, NB // 4, NB // 2
        PREP = PREP_WC + PREP_QK + PREP_VO + PREP_KV + PREP_LN

        def prep_out(n):
            b = bank(n % 8)
            if n < PREP_WC:
                return b[:, 0:DC * DQ0].rearrange("p (c q) -> p c q", c=DC), wc[:, :, n, :]
            n -= PREP_WC
            if n < PREP_QK:
                return (b[0:HALF, :].rearrange("p (h a d) -> p h a d", h=4, a=2), wqk[:, 4 * n:4 * n + 4])
            n -= PREP_QK
            if n < PREP_VO:
                return b.rearrange("p (h o) -> p h o", h=2), wvo[:, 2 * n:2 * n + 2, :]
            n -= PREP_VO
            if n < PREP_KV:
                return b, kvT[:, 512 * n:512 * n + 512]
            n -= PREP_KV
            return (b.rearrange("p (c t) -> p c t", c=DC), xnT[:, 1, :, GT * n:GT * n + GT])

        @block.tensor
        def _(pe):
            mm = nc.tensor.matmul
            pe.wait_ge(ld_c, 16 * N_CONST)
            pe.wait_ge(ld_w, 16 * 6)
            for n in range(PREP):
                if n >= 8:
                    pe.wait_ge(prep_dve if n % 2 else prep_act, (n - 8) // 2 + 1)
                to, _ = prep_out(n)
                if n < PREP_WC:
                    for c in range(DC):
                        last = mm(to[:, c, :], r_wq[:, n, c * P:(c + 1) * P], r_wkcq[:, n, :])
                elif n < PREP_WC + PREP_QK:
                    for k in range(4):
                        h = 4 * (n - PREP_WC) + k
                        for half in range(2):
                            last = mm(to[:, k, half, :], r_wqrT[:, h, half * HALF:(half + 1) * HALF],
                                      r_wkrT[:, h, :])
                elif n < PREP_WC + PREP_QK + PREP_VO:
                    for k in range(2):
                        for odd in range(2):
                            h = 4 * (n - PREP_WC - PREP_QK) + 2 * k + odd
                            last = mm(to[64 * odd:64 * odd + 64, k, :], r_wkckv[:, h, :], r_woT[:, h, :])
                elif n < PREP - PREP_LN:
                    for k in range(4):
                        b = 4 * (n - PREP_WC - PREP_QK - PREP_VO) + k
                        pe.wait_ge(kv_ready, 2)
                        last = nc.tensor.transpose(to[:, k * P:(k + 1) * P],
                                                   kvd[:, b].rearrange("p a d -> p (a d)"), ident[:])
                else:
                    g = n - (PREP - PREP_LN)
                    pe.wait_ge(xn_ready, GB * (g + 1))
                    for k in range(GB):
                        for c in range(DC):
                            last = nc.tensor.transpose(to[:, c, k * P:(k + 1) * P],
                                                       xn_all[:, GB * g + k, c * P:(c + 1) * P], ident[:])
                last.then_inc(prep_mm, 1)
            barrier(pe, 1)

            def query(g, i, h):
                s = stage(g, i, 0, NPAIR)
                if s is None:
                    return
                grp, p = s
                f = NPAIR * grp + p
                wait(pe, q_scaled, 2 * f + h - 1)
                o = bank(QB[h])[0:HALF, :]
                for half in range(2):
                    for c in range(DC):
                        last = mm(o[:, half * GT:(half + 1) * GT],
                                  wc[:, c, 2 * p + h, half * HALF:(half + 1) * HALF],
                                  xnT[:, 1, c, bass.ds(grp * GT, GT)], start=(c == 0), stop=(c == DC - 1))
                last.then_inc(q_mm, 1)

            def to_rank(g, i):
                s = stage(g, i, B_LAG, NPAIR)
                if s is None:
                    return
                grp, p = s
                f = NPAIR * grp + p
                pe.wait_ge(q_roped, 2 * f + 2)
                wait(pe, b_out, f)
                for h in range(2):
                    for half in range(2):
                        last = mm(bank(BB)[64 * h:64 * h + 64, 0:GT], wqk[:, 2 * p + h, half, :],
                                  roped[:, p % 2, h, half * GT:(half + 1) * GT],
                                  start=(half == 0), stop=(half == 1))
                last.then_inc(b_mm, 1)

            def scores(g, i):
                s = stage(g, i, S_LAG, NPAIR)
                if s is None:
                    return
                grp, p = s
                f = NPAIR * grp + p
                pe.wait_ge(b_out, f + 1)
                if p == 0:
                    pe.wait_ge(kv_copied, grp + 1)
                wait(pe, s_exp, f)
                for h in range(2):
                    for b in range(GB):
                        last = mm(bank(SB + h)[:, b * P:(b + 1) * P],
                                  qT[64 * h:64 * h + 64, p % 2, b * P:(b + 1) * P],
                                  kvTg[64 * h:64 * h + 64, b * P:(b + 1) * P])
                last.then_inc(s_mm, 1)

            def transpose_p(g, i):
                s = stage(g, i, T_LAG, NPAIR)
                if s is None:
                    return
                grp, p = s
                f = NPAIR * grp + p
                pe.wait_ge(s_exp, f + 1)
                wait(pe, t_out, f)
                for k in range(4):
                    last = nc.tensor.transpose(bank(TB)[:, k * P:(k + 1) * P], prob[:, p % 2, k, :], ident[:])
                last.then_inc(t_mm, 1)

            def mix(g, i):
                s = stage(g, i, O_LAG, NPAIR)
                if s is None:
                    return
                grp, p = s
                f = NPAIR * grp + p
                pe.wait_ge(t_out, f + 1)
                wait(pe, o_out, f)
                for h in range(2):
                    for b in range(GB):
                        k = 2 * h + b
                        last = mm(bank(OB)[:, k * (DCTX + 1):(k + 1) * (DCTX + 1)], probT[:, p % 2, k, :],
                                  kvaug[:, bass.ds(grp * GB + b, 1), :].rearrange("p a d -> p (a d)"))
                last.then_inc(o_mm, 1)

            def transpose_c(g, i):
                s = stage(g, i, U_LAG, NPAIR)
                if s is None:
                    return
                grp, p = s
                f = NPAIR * grp + p
                pe.wait_ge(o_out, f + 1)
                wait(pe, u_out, f)
                if p == 0:
                    wait(pe, y_add, grp)
                if p == 1:
                    wait(pe, l_out, grp)
                if p == 2:
                    wait(pe, g_out, grp)
                for b in range(GB):
                    last = nc.tensor.transpose(bank(MB)[:, b * P:(b + 1) * P], ctxh[:, p % 2, b, :], ident[:])
                last.then_inc(u_mm, 1)

            def close_group(g, i):
                s = stage(g, 0, 1, NPAIR)
                if s is None or i not in (Y_AT, L_AT, G_AT):
                    return
                grp = s[0]
                more = not isinstance(g, int) or g < NG
                if i == Y_AT:
                    pe.wait_ge(u_out, NPAIR * (grp + 1))
                    for b in range(GB):
                        for p in range(NPAIR):
                            last = mm(bank(MB)[:, b * D:(b + 1) * D], ctxhT[:, p, b * P:(b + 1) * P],
                                      wvo[:, p, :], start=(p == 0), stop=(p == NPAIR - 1))
                    last.then_inc(y_mm, 1)
                if i == L_AT:
                    pe.wait_ge(l_xn, grp + 1)
                    pe.wait_ge(u_out, NPAIR * (grp + 1) + more)
                    pe.wait_ge(y_add, grp + 1)
                    for b in range(GB):
                        for c in range(DC):
                            last = nc.tensor.transpose(bank(MB)[:, c * GT + b * P:c * GT + (b + 1) * P],
                                                       xn2[:, b, c * P:(c + 1) * P], ident[:])
                    last.then_inc(l_mm, 1)
                if i == G_AT:
                    pe.wait_ge(l_out, grp + 1)
                    pe.wait_ge(u_out, NPAIR * (grp + 1) + 2 * more)
                    for b in range(GB):
                        for c in range(DC):
                            last = mm(bank(MB)[:, b * NE:(b + 1) * NE], xgT[:, c, b * P:(b + 1) * P],
                                      gatew[:, c, :], start=(c == 0), stop=(c == DC - 1))
                    last.then_inc(g_mm, 1)

            def body(g, i):
                query(g, i, 0)
                scores(g, i)
                close_group(g, i)
                query(g, i, 1)
                transpose_p(g, i)
                mix(g, i)
                transpose_c(g, i)
                to_rank(g, i)

            pipeline(pe, NG, NPAIR, body)
            barrier(pe, 2)

            pe.wait_ge(ld_f1, 32)
            pe.wait_ge(ld_2, 64)

            def up(g, i):
                s = stage(g, i, 0, STEPS2, NG2)
                if s is None or i > BIAS_AT:
                    return
                grp, e = s
                n = (NE + 1) * grp + e
                wait(pe, h_out, n if e < 2 else n - 1)
                if e == BIAS_AT:
                    pe.wait_ge(f_cp, grp + 1)
                    for b in range(GB2):
                        last = nc.tensor.transpose(bank(0)[0:NE, b * P:(b + 1) * P], combg[:, b, :], ident[:])
                else:
                    for m in range(IC):
                        for c in range(DC):
                            last = mm(bank(2 * (e % 2) + m), fc1[:, e, c, m * P:(m + 1) * P],
                                      xnT[:, 0, c, bass.ds(grp * T2, T2)], start=(c == 0), stop=(c == DC - 1))
                last.then_inc(h_mm, 1)

            def down(g, i):
                s = stage(g, i, 1, STEPS2, NG2)
                if s is None or s[1] > BIAS_AT:
                    return
                grp, e = s
                n = (NE + 1) * grp + e
                pe.wait_ge(h_out, n + 1)
                wait(pe, f_acc, n - (0 if e == 0 else 1))
                for b in range(GB2):
                    o = bank(4 + 2 * (e % 2) + b // 2)[:, (b % 2) * D:(b % 2 + 1) * D]
                    if e == BIAS_AT:
                        last = mm(o, combT[:, b * P:(b + 1) * P], fc2b)
                    else:
                        for m in range(IC):
                            last = mm(o, hT[:, e % 2, m, b * P:(b + 1) * P], fc2[:, e, m, :],
                                      start=(m == 0), stop=(m == IC - 1))
                last.then_inc(f_mm, 1)

            def next_x(g, i):
                s = stage(g, 0, 1, STEPS2, NG2)
                if s is None or i != LN_AT:
                    return
                grp = s[0]
                pe.wait_ge(n_xn, grp + 1)
                if not isinstance(g, int) or g < NG2:
                    pe.wait_ge(h_out, (NE + 1) * (grp + 1) + NE)
                else:
                    pe.wait_ge(n_out, grp)
                for c in range(DC):
                    for b in range(GB2):
                        last = nc.tensor.transpose(bank(2 + c)[:, b * P:(b + 1) * P],
                                                   xn4[:, b, c * P:(c + 1) * P], ident[:])
                last.then_inc(n_mm, 1)

            def body2(g, i):
                up(g, i)
                next_x(g, i)
                down(g, i)

            pipeline(pe, NG2, STEPS2, body2)
            barrier(pe, 3)

            pe.wait_ge(ld_3, 48)
            for n in range(NB // 2):
                wait(pe, v3_out, n - 7)
                for b in range(2):
                    last = mm(bank(n % 8)[:, b * D:(b + 1) * D], ctxT[:, (2 * n + b) * P:(2 * n + b + 1) * P],
                              wkv1[:, D:2 * D])
                last.then_inc(v3_mm, 1)
            pe.wait_ge(w3_ready, 1)
            pe.wait_ge(v3_out, NB // 2)

            def project(g, i):
                s = stage(g, i, 0, STEPS3, NG3)
                if s is None or i % 8 > 2:
                    return
                grp, u = s[0], i % 8
                half = 2 * grp + i // 8
                wait(pe, pj_out, 3 * half + u)
                tok = bass.ds(half * GT, GT)
                for ct in range(DC):
                    o = bank(6)[:, ct * GT:(ct + 1) * GT]
                    if u == 2:
                        last = mm(o, wkv1[:, ct * P:(ct + 1) * P], ctxT[:, tok])
                    else:
                        for c in range(DC):
                            last = mm(o, wqm[:, c, ct, u, :], xnT[:, 1, c, tok], start=(c == 0), stop=(c == DC - 1))
                last.then_inc(pj_mm, 1)

            def scores3(g, i):
                s = stage(g, i, S3, STEPS3, NG3)
                if s is None:
                    return
                grp, k = s
                f, half, b, w = STEPS3 * grp + k, 2 * grp + k // 8, k // 4 % 2, k % 4
                if k % 8 == 0:
                    pe.wait_ge(pj_out, 3 * half + 3)
                wait(pe, s3_exp, f - 3)
                mm(bank(w), identb[:], mask[:].rearrange("p k l -> p (k l)"), start=True, stop=False)
                r = slice(32 * w, 32 * w + 32)
                t = slice(b * P, (b + 1) * P)
                for ct in range(DC):
                    for e in range(2):
                        o = 2 * ct + e
                        last = mm(bank(w)[:, o * P:(o + 1) * P], q3[r, k // 8, e, ct, t], k3[r, k // 8, ct, t],
                                  start=False, stop=(o == 3))
                last.then_inc(s3_mm, 1)

            def transpose3(g, i):
                s = stage(g, i, T3, STEPS3, NG3)
                if s is None:
                    return
                grp, k = s
                f = STEPS3 * grp + k
                pe.wait_ge(s3_exp, f + 1)
                wait(pe, t3_out, f)
                for o in range(4):
                    last = nc.tensor.transpose(bank(4)[:, o * P:(o + 1) * P], prob3[:, k % 4, o, :], ident[:])
                last.then_inc(t3_mm, 1)

            def mix3(g, i):
                s = stage(g, i, O3, STEPS3, NG3)
                if s is None:
                    return
                grp, k = s
                f, b, w = STEPS3 * grp + k, 4 * grp + k // 4, k % 4
                pe.wait_ge(t3_out, f + 1)
                if w == 0:
                    wait(pe, o3_out, b)
                for ct in range(DC):
                    for e in range(2):
                        h = 8 * ct + 2 * w + e
                        last = mm(bank(5)[:, h * V1:(h + 1) * V1], probT3[:, k % 2, 2 * ct + e, :],
                                  vaug[:, bass.ds(b, 1), h, :].rearrange("p a d -> p (a d)"))
                last.then_inc(o3_mm, 1)

            def project_out(g, i):
                s = stage(g, i, U3, STEPS3, NG3)
                if s is not None and s[1] % 4 == 3:
                    b = 4 * s[0] + s[1] // 4
                    pe.wait_ge(o3_out, b + 1)
                    wait(pe, y3_add, b)
                    for c in range(DC):
                        last = nc.tensor.transpose(bank(7)[:, c * P:(c + 1) * P], ctx3[:, c * P:(c + 1) * P], ident[:])
                    last.then_inc(u3_mm, 1)
                s = stage(g, i, Y3, STEPS3, NG3)
                if s is not None and s[1] % 4 == 3:
                    b = 4 * s[0] + s[1] // 4
                    pe.wait_ge(u3_out, b + 1)
                    for c in range(DC):
                        last = mm(bank(7)[:, D:2 * D], ctx3T[:, c, :], wout1[:, c, :],
                                  start=(c == 0), stop=(c == DC - 1))
                    last.then_inc(y3_mm, 1)

            def body3(g, i):
                project(g, i)
                scores3(g, i)
                mix3(g, i)
                transpose3(g, i)
                project_out(g, i)

            pipeline(pe, NG3, STEPS3, body3)
            barrier(pe, 4)

            pe.wait_ge(w4_quant, 1)
            for j in range(2):
                for hc in range(DC):
                    for k, (at, n) in enumerate(FCH):
                        last = nc.tensor.transpose(bank16(2 * j + hc)[:, at:at + n],
                                                   wgu_q[0:n, NF * j + k, hc * P:(hc + 1) * P], identb[0:n, 0:n])
            for k, (at, n) in enumerate(FCH):
                for c in range(DC):
                    last = nc.tensor.transpose(bank16(4 + k // 4)[0:n, (k % 4) * D + c * P:(k % 4) * D + (c + 1) * P],
                                               wd_q[:, c, at:at + n], identb[:])
            last.then_inc(w4_mm, 1)
            pe.wait_ge(w4_diag, 1)
            for c in range(DC):
                last = mm(bank(6)[:, c * P:(c + 1) * P], ones, diag[:, 2 * NF + c, :])
            last.then_inc(w4_mm, 1)
            pe.wait_ge(w4_out, 1)
            for j in range(2):
                for k, (at, n) in enumerate(FCH):
                    bk, col = 2 * j + k // 4, at % 512
                    last = mm(bank(bk)[:, col:col + n], ones[0:n, :], diag[0:n, NF * j + k, 0:n])
            last.then_inc(w4_mm, 1)
            barrier(pe, 5)

            def x_turned(g, i):
                s = stage(g, i, 1, STEPS4, NG4)
                if s is None:
                    return
                grp, k = s
                f = STEPS4 * grp + k
                pe.wait_ge(x5_q, f + 1)
                wait(pe, x5_out, f)
                for c in range(DC):
                    last = nc.tensor.transpose(bank16(4)[:, c * P:(c + 1) * P], qx[:, c * P:(c + 1) * P], identb[:])
                last.then_inc(x5_mm, 1)

            def gate_up(g, i):
                s = stage(g, i, 1, STEPS4, NG4)
                if s is None:
                    return
                grp, k = s
                f = STEPS4 * grp + k
                pe.wait_ge(x5_out, f + 1)
                wait(pe, gu_read, f)
                for o in range(4):
                    for c in range(DC):
                        last = mm(bank(o)[:, 0:FF // 2], qxT[:, k % 2, c, :],
                                  wguT[:, c, o * (FF // 2):(o + 1) * (FF // 2)], start=(c == 0), stop=(c == DC - 1))
                last.then_inc(gu_mm, 1)

            def t_turned(g, i):
                s = stage(g, i, 2, STEPS4, NG4)
                if s is None:
                    return
                grp, k = s
                f = STEPS4 * grp + k
                pe.wait_ge(t5_q, f + 1)
                wait(pe, t5_out, f)
                for c, (at, n) in enumerate(FCH):
                    last = nc.tensor.transpose(bank16(5)[0:n, c * P:(c + 1) * P], qt[:, k % 2, at:at + n], identb[:])
                last.then_inc(t5_mm, 1)

            def y_down(g, i):
                s = stage(g, i, 2, STEPS4, NG4)
                if s is None:
                    return
                grp, k = s
                f = STEPS4 * grp + k
                pe.wait_ge(t5_out, f + 1)
                wait(pe, y5_read, f)
                for c, (at, n) in enumerate(FCH):
                    last = mm(bank(6)[:, 0:D], qtT[0:n, k % 2, c, :], wdT[0:n, c, :],
                              start=(c == 0), stop=(c == NF - 1))
                last.then_inc(y5_mm, 1)

            def body4(g, i):
                x_turned(g, i)
                gate_up(g, i)
                t_turned(g, i)
                y_down(g, i)

            pipeline(pe, NG4, STEPS4, body4)

        @block.scalar
        def _(act):
            def copy(o, i):
                return nc.scalar.activation(o, i, ACT.Copy)

            for name, dst in CONSTS:
                act.dma_start(dst, a[name]).then_inc(ld_c, 16)
            for n in range(0, PREP, 2):
                act.wait_ge(prep_mm, n + 1)
                src, dst = prep_out(n)
                copy(dst, src).then_inc(prep_act, 1)
            barrier(act, 1)

            def exps(g, i):
                s = stage(g, i, S_LAG, NPAIR)
                if s is None:
                    return
                grp, p = s
                f = NPAIR * grp + p
                act.wait_ge(s_max, f + 1)
                wait(act, t_mm, f - 1)
                for k in range(4):
                    last = nc.scalar.activation(prob[:, p % 2, k, :],
                                                bank(SB + k // 2)[:, (k % 2) * P:(k % 2 + 1) * P],
                                                ACT.Exp, bias=nmax[:, p % 2, k:k + 1])
                last.then_inc(s_exp, 1)

            def probs_out(g, i):
                s = stage(g, i, T_LAG, NPAIR)
                if s is None:
                    return
                grp, p = s
                f = NPAIR * grp + p
                act.wait_ge(t_mm, f + 1)
                wait(act, o_mm, f - 1)
                copy(probT[:, p % 2].rearrange("p k t -> p (k t)"), bank(TB)).then_inc(t_out, 1)

            def ctx_out(g, i):
                s = stage(g, i, U_LAG, NPAIR)
                if s is None:
                    return
                grp, p = s
                f = NPAIR * grp + p
                act.wait_ge(u_mm, f + 1)
                if p == 0:
                    wait(act, y_mm, grp)
                copy(ctxhT[:, p, :], bank(MB)[:, 0:GT]).then_inc(u_out, 1)

            def close_group(g, i):
                s = stage(g, 0, 1, NPAIR)
                if s is None:
                    return
                grp = s[0]
                if i == L_AT:
                    act.wait_ge(l_mm, grp + 1)
                    src = bank(MB).rearrange("p (c t) -> p c t", c=DC)
                    copy(xgT[:, :, :], src)
                    copy(xnT[:, 0, :, bass.ds(grp * GT, GT)], src).then_inc(l_out, 1)
                if i == G_AT:
                    act.wait_ge(g_mm, grp + 1)
                    copy(logits[:, bass.ds(grp * GB, GB), :],
                         bank(MB)[:, 0:GB * NE].rearrange("p (b e) -> p b e", b=GB)).then_inc(g_out, 1)

            def q_out(g, i):
                s = stage(g, i, B_LAG, NPAIR)
                if s is None:
                    return
                grp, p = s
                f = NPAIR * grp + p
                act.wait_ge(b_mm, f + 1)
                wait(act, s_mm, f - 1)
                copy(qT[:, p % 2, :], bank(BB)[:, 0:GT]).then_inc(b_out, 1)

            def group_kv(g, i):
                s = stage(g, i, S_LAG, NPAIR)
                if s is None or s[1] != 0:
                    return
                grp = s[0]
                wait(act, s_mm, NPAIR * grp)
                copy(kvTg, kvT[:, bass.ds(grp * GT, GT)]).then_inc(kv_copied, 1)

            def body(g, i):
                group_kv(g, i)
                exps(g, i)
                close_group(g, i)
                probs_out(g, i)
                ctx_out(g, i)
                q_out(g, i)

            pipeline(act, NG, NPAIR, body)
            barrier(act, 2)

            act.wait_ge(gate_max, 1)
            nc.scalar.activation(expl, expl, ACT.Exp).then_inc(gate_exp, 1)
            act.wait_ge(ld_2, 64)

            def gelu(g, i):
                s = stage(g, i, 0, STEPS2, NG2)
                if s is None or i > BIAS_AT:
                    return
                grp, e = s
                n = (NE + 1) * grp + e
                act.wait_ge(h_mm, n + 1)
                if e == BIAS_AT:
                    wait(act, f_mm, n - NE)
                    copy(combT, bank(0)[0:NE, :]).then_inc(h_out, 1)
                    return
                wait(act, f_mm, n - 1 if e >= 2 else n - 2)
                for m in range(IC):
                    last = nc.scalar.activation(hT[:, e % 2, m, :], bank(2 * (e % 2) + m), ACT.Gelu,
                                                bias=fc1b[:, e, m:m + 1])
                last.then_inc(h_out, 1)

            def next_x(g, i):
                s = stage(g, 0, 1, STEPS2, NG2)
                if s is None or i != LN_AT:
                    return
                grp = s[0]
                act.wait_ge(n_mm, grp + 1)
                for c in range(DC):
                    last = copy(xnT[:, 1, c, bass.ds(grp * T2, T2)], bank(2 + c))
                last.then_inc(n_out, 1)

            def body2(g, i):
                gelu(g, i)
                next_x(g, i)

            pipeline(act, NG2, STEPS2, body2)
            barrier(act, 3)

            act.wait_ge(w3_ready, 1)
            for n in range(NB // 2):
                act.wait_ge(v3_mm, n + 1)
                for b in range(2):
                    last = copy(vaug[:, 2 * n + b, :, 0:HD1],
                                bank(n % 8)[:, b * D:(b + 1) * D].rearrange("p (h d) -> p h d", h=H1))
                last.then_inc(v3_out, 1)

            def project(g, i):
                s = stage(g, i, 0, STEPS3, NG3)
                if s is None or i % 8 > 2:
                    return
                grp, u = s[0], i % 8
                half = 2 * grp + i // 8
                act.wait_ge(pj_mm, 3 * half + u + 1)
                wait(act, s3_mm, 8 * (half - 1))
                dst = k3[:, i // 8] if u == 2 else q3[:, i // 8, u]
                copy(dst.rearrange("p c t -> p (c t)"), bank(6)).then_inc(pj_out, 1)

            def exps3(g, i):
                s = stage(g, i, S3, STEPS3, NG3)
                if s is None:
                    return
                grp, k = s
                f = STEPS3 * grp + k
                act.wait_ge(s3_max, f + 1)
                wait(act, t3_mm, f - 3)
                for o in range(4):
                    last = nc.scalar.activation(prob3[:, k % 4, o, :], bank(k % 4)[:, o * P:(o + 1) * P],
                                                ACT.Exp, bias=nmax3[:, k % 4, o:o + 1])
                last.then_inc(s3_exp, 1)

            def ctx_out3(g, i):
                s = stage(g, i, U3, STEPS3, NG3)
                if s is None or s[1] % 4 != 3:
                    return
                b = 4 * s[0] + s[1] // 4
                act.wait_ge(u3_mm, b + 1)
                wait(act, y3_mm, b)
                copy(ctx3T.rearrange("p c t -> p (c t)"), bank(7)[:, 0:D]).then_inc(u3_out, 1)

            def body3(g, i):
                project(g, i)
                exps3(g, i)
                ctx_out3(g, i)

            pipeline(act, NG3, STEPS3, body3)
            barrier(act, 4)

            act.wait_ge(w4_mm, 1)
            for j in range(2):
                for hc in range(DC):
                    last = copy(wguT[:, hc, j * FF:(j + 1) * FF], bank16(2 * j + hc)[:, 0:FF])
            last.then_inc(w4_out, 1)
            for c in range(NF):
                n = FCH[c][1]
                copy(wdT[0:n, c, :], bank16(4 + c // 4)[0:n, (c % 4) * D:(c % 4 + 1) * D])
            act.wait_ge(w4_mm, 2)
            copy(wsdb, bank(6)[:, 0:D])
            act.wait_ge(w4_mm, 3)
            for j in range(2):
                copy(wsb[:, j * FF:j * FF + 512], bank(2 * j))
                copy(wsb[:, j * FF + 512:(j + 1) * FF], bank(2 * j + 1)[:, 0:FF - 512])
            barrier(act, 5)

            def x_turned(g, i):
                s = stage(g, i, 1, STEPS4, NG4)
                if s is None:
                    return
                grp, k = s
                f = STEPS4 * grp + k
                act.wait_ge(x5_mm, f + 1)
                wait(act, gu_mm, f - 1)
                copy(qxT[:, k % 2].rearrange("p c t -> p (c t)"), bank16(4)[:, 0:D]).then_inc(x5_out, 1)

            def silu(g, i):
                s = stage(g, i, 1, STEPS4, NG4)
                if s is None:
                    return
                grp, k = s
                f = STEPS4 * grp + k
                act.wait_ge(g_scaled, f + 1)
                nc.scalar.activation(tsl, tg, ACT.Silu, scale=sx[:, k, 0:1]).then_inc(silu_out, 1)

            def t_turned(g, i):
                s = stage(g, i, 2, STEPS4, NG4)
                if s is None:
                    return
                grp, k = s
                f = STEPS4 * grp + k
                act.wait_ge(t5_mm, f + 1)
                wait(act, y5_mm, f - 1)
                last_n = FCH[-1][1]
                copy(qtT[:, k % 2, 0:NF - 1, :].rearrange("p c t -> p (c t)"), bank16(5)[:, 0:(NF - 1) * P])
                copy(qtT[0:last_n, k % 2, NF - 1, :], bank16(5)[0:last_n, (NF - 1) * P:NF * P]).then_inc(t5_out, 1)

            def body4(g, i):
                x_turned(g, i)
                silu(g, i)
                t_turned(g, i)

            pipeline(act, NG4, STEPS4, body4)

        @block.vector
        def _(dve):
            V = nc.vector

            def step(ins):
                then_next(dve, ins, dve_step, "dve")

            V.memset(mhalf[:], -0.5)
            V.memset(epst[:], LN_EPS)
            V.memset(kvaug[:, :, DCTX:DCTX + 1], 1.0)
            dve.wait_ge(ld_x, 16)
            for b in range(NB):
                V.bn_stats(st6[:, b, :], x[:, b, :])
            step(V.memset(veps[:], 0.0))
            for b in range(NB):
                last = V.bn_aggr(mv[:, b, :], st6[:, b, :])
            step(last)
            V.tensor_scalar(veps[:], mv[:, :, 1], LN_EPS, None, ALU.add).then_inc(ln_stats, 1)
            dve.wait_ge(ld_c, 16 * N_CONST)
            hc = DCTX // 2
            cb = ropek_c[:].unsqueeze(1).to_broadcast([P, NB, DCTX])
            tmp = kvd[:, :, 1, :]
            V.tensor_tensor(kvaug[:, :, 0:DCTX], ctx_n, cb, ALU.mult)
            V.tensor_tensor(tmp[:, :, 0:hc], ctx_n[:, :, hc:DCTX],
                            ropek_s[:, 0:hc].unsqueeze(1).to_broadcast([P, NB, hc]), ALU.mult)
            step(V.tensor_tensor(tmp[:, :, hc:DCTX], ctx_n[:, :, 0:hc],
                                 ropek_s[:, hc:DCTX].unsqueeze(1).to_broadcast([P, NB, hc]), ALU.mult))
            step(V.tensor_tensor(kvaug[:, :, 0:DCTX], kvaug[:, :, 0:DCTX], tmp, ALU.add))
            V.tensor_copy(kvd[:, :, 0, :], kvaug[:, :, 0:DCTX]).then_inc(kv_ready, 1)
            V.tensor_copy(kvd[:, :, 1, :], kvaug[:, :, 0:DCTX]).then_inc(kv_ready, 1)
            dve.wait_ge(ln_rstd, 1)
            for b in range(NB):
                V.tensor_scalar(xn_all[:, b, :], x[:, b, :], mv[:, b, 0:1], rstd[:, b:b + 1],
                                ALU.subtract, ALU.mult).then_inc(xn_ready, 1)
            for n in range(1, PREP, 2):
                dve.wait_ge(prep_mm, n + 1)
                src, dst = prep_out(n)
                V.tensor_copy(dst, src).then_inc(prep_dve, 1)
            barrier(dve, 1)

            rc = rope_c[:].rearrange("p a b t -> p (a b t)")
            rs = rope_s[:].rearrange("p a b t -> p (a b t)")

            def rope(g, i, h):
                s = stage(g, i, 0, NPAIR)
                if s is None:
                    return
                grp, p = s
                f = NPAIR * grp + p
                dve.wait_ge(q_mm, 2 * f + h + 1)
                wait(dve, q_roped, 2 * f + h - 1)
                q = bank(QB[h])[0:HALF, :]
                V.tensor_tensor(t1[:, h, :], q, rc, ALU.mult)
                V.tensor_tensor(t2[:, h, :], q, rs, ALU.mult).then_inc(q_scaled, 1)

            def row_max(g, i):
                s = stage(g, i, S_LAG, NPAIR)
                if s is None:
                    return
                grp, p = s
                f = NPAIR * grp + p
                dve.wait_ge(s_mm, f + 1)
                wait(dve, s_exp, f - 1)
                V.tensor_reduce(nmax[:, p % 2, :].rearrange("p (h b) -> p h b", h=2),
                                ps[:, SB:SB + 2, 0:GT].rearrange("p h (b l) -> p h b l", b=GB),
                                AX.X, ALU.max, negate=True).then_inc(s_max, 1)

            def normalise(g, i):
                s = stage(g, i, O_LAG, NPAIR)
                if s is None:
                    return
                grp, p = s
                f = NPAIR * grp + p
                dve.wait_ge(o_mm, f + 1)
                wait(dve, u_mm, f - 1)
                o = bank(OB)[:, 0:4 * (DCTX + 1)].rearrange("p (k d) -> p k d", k=4)
                V.reciprocal(rsum[:, p % 2, :], o[:, :, DCTX]).then_inc(norm_r, 1)
                dve.wait_ge(norm_r, f + 1)
                for h in range(2):
                    last = V.tensor_tensor(ctxh[:, p % 2, :, 64 * h:64 * h + 64], o[:, 2 * h:2 * h + 2, 0:DCTX],
                                           rsum[:, p % 2, 2 * h:2 * h + 2].unsqueeze(2)
                                           .to_broadcast([P, GB, DCTX]), ALU.mult)
                last.then_inc(o_out, 1)

            def close_group(g, i):
                s = stage(g, 0, 1, NPAIR)
                if s is None or i != Y_AT:
                    return
                grp = s[0]
                dve.wait_ge(y_mm, grp + 1)
                xg = x[:, bass.ds(grp * GB, GB), :]
                V.tensor_tensor(xg, xg, bank(MB).rearrange("p (b d) -> p b d", b=GB), ALU.add).then_inc(y_add, 1)
                wait_apart(dve, y_add, grp + 1)
                layernorm(grp, 1)

            def layernorm(grp, phase):
                for b in range(GB):
                    last = V.bn_stats(st6[:, b, :], x[:, bass.ds(grp * GB + b, 1), :].rearrange("p a d -> p (a d)"))
                last.then_inc(ln_a, 1)
                wait_apart(dve, ln_a, grp + 1)
                for b in range(GB):
                    last = V.bn_aggr(mv[:, b, :], st6[:, b, :])
                last.then_inc(l_stats, 1)
                dve.wait_ge(l_rstd, grp + 1)
                for b in range(GB):
                    last = V.tensor_scalar(xn2[:, b, :], x[:, bass.ds(grp * GB + b, 1), :]
                                           .rearrange("p a d -> p (a d)"), mv[:, b, 0:1], rstd[:, b:b + 1],
                                           ALU.subtract, ALU.mult)
                last.then_inc(l_xn, 1)

            def body(g, i):
                rope(g, i, 0)
                row_max(g, i)
                rope(g, i, 1)
                normalise(g, i)
                close_group(g, i)

            pipeline(dve, NG, NPAIR, body)
            barrier(dve, 2)

            dve.wait_ge(ld_2, 64)
            step(V.tensor_reduce(lmax, logits[:], AX.X, ALU.max))
            V.tensor_tensor(expl, logits[:], lmax.unsqueeze(2).to_broadcast([P, NB, NE]),
                            ALU.subtract).then_inc(gate_max, 1)
            dve.wait_ge(gate_exp, 1)
            every = [P, NB, NE, NE]
            mine = expl.unsqueeze(3).to_broadcast(every)
            other = expl.unsqueeze(2).to_broadcast(every)
            V.tensor_tensor(above, other, mine, ALU.is_gt)
            step(V.tensor_tensor(tied, other, mine, ALU.is_equal))
            step(V.tensor_tensor(tied, tied, before.unsqueeze(1).to_broadcast(every), ALU.mult))
            step(V.tensor_tensor(above, above, tied, ALU.add))
            step(V.tensor_reduce(rank, above, AX.X, ALU.add))
            step(V.tensor_scalar(rank, rank, TOPK - 0.5, None, ALU.is_lt))
            step(V.tensor_tensor(rank, rank, expl, ALU.mult))
            step(V.tensor_reduce(lmax, rank, AX.X, ALU.add))
            step(V.reciprocal(lmax, lmax))
            step(V.tensor_tensor(rank, rank, lmax.unsqueeze(2).to_broadcast([P, NB, NE]), ALU.mult))
            V.tensor_tensor(comb, rank, alpha.unsqueeze(1).to_broadcast([P, NB, NE]), ALU.mult)\
                .then_inc(comb_ready, 1)
            dve.wait_ge(comb_ready, 1)

            def group_comb(g, i):
                s = stage(g, i, 0, STEPS2, NG2)
                if s is None or i != 1:
                    return
                grp = s[0]
                wait(dve, h_mm, (NE + 1) * grp)
                wait(dve, f_acc, (NE + 1) * grp)
                V.tensor_copy(combg, comb[:, bass.ds(grp * GB2, GB2), :]).then_inc(f_cp, 1)

            def accumulate(g, i):
                s = stage(g, i, 1, STEPS2, NG2)
                if s is None or s[1] > BIAS_AT:
                    return
                grp, e = s
                n = (NE + 1) * grp + e
                dve.wait_ge(f_mm, n + 1)
                wait(dve, f_acc, n)
                if e == 0:
                    dve.wait_ge(f_cp, grp + 1)
                for b in range(GB2):
                    xb = x[:, bass.ds(grp * GB2 + b, 1), :].rearrange("p a d -> p (a d)")
                    y = bank(4 + 2 * (e % 2) + b // 2)[:, (b % 2) * D:(b % 2 + 1) * D]
                    if e == BIAS_AT:
                        last = V.tensor_tensor(xb, xb, y, ALU.add)
                    else:
                        last = V.scalar_tensor_tensor(xb, y, combg[:, b, e:e + 1], xb, ALU.mult, ALU.add)
                last.then_inc(f_acc, 1)

            def layernorm2(g, i):
                s = stage(g, 0, 1, STEPS2, NG2)
                if s is None or i != 1:
                    return
                grp = s[0]
                wait_apart(dve, f_acc, (NE + 1) * (grp + 1))
                for b in range(GB2):
                    last = V.bn_stats(st6[:, b, :], x[:, bass.ds(grp * GB2 + b, 1), :].rearrange("p a d -> p (a d)"))
                last.then_inc(n_a, 1)
                wait_apart(dve, n_a, grp + 1)
                for b in range(GB2):
                    last = V.bn_aggr(mv[:, b, :], st6[:, b, :])
                last.then_inc(n_stats, 1)
                dve.wait_ge(n_rstd, grp + 1)
                for b in range(GB2):
                    last = V.tensor_scalar(xn4[:, b, :], x[:, bass.ds(grp * GB2 + b, 1), :]
                                           .rearrange("p a d -> p (a d)"), mv[:, b, 0:1], rstd[:, b:b + 1],
                                           ALU.subtract, ALU.mult)
                last.then_inc(n_xn, 1)

            def body2(g, i):
                group_comb(g, i)
                layernorm2(g, i)
                accumulate(g, i)

            pipeline(dve, NG2, STEPS2, body2)
            barrier(dve, 3)

            V.memset(vaug, 1.0)
            step(V.memset(wqm, 0.0))
            dve.wait_ge(ld_3, 48)
            for c in range(DC):
                for ct in range(DC):
                    for e in range(2):
                        pick = wqm[:, c, ct, e, :].rearrange("p (w e d) -> p w e d", w=4, e=2)[:, :, e, :]
                        src = wq1[:, c, ct * P:(ct + 1) * P].rearrange("p (w e d) -> p w e d", w=4, e=2)[:, :, e, :]
                        last = V.tensor_scalar(pick, src, float(HD1) ** -0.5, None, ALU.mult)
            last.then_inc(w3_ready, 1)

            def row_max3(g, i):
                s = stage(g, i, S3, STEPS3, NG3)
                if s is None:
                    return
                grp, k = s
                f = STEPS3 * grp + k
                dve.wait_ge(s3_mm, f + 1)
                wait(dve, s3_exp, f - 3)
                V.tensor_reduce(nmax3[:, k % 4, :], bank(k % 4).rearrange("p (o l) -> p o l", o=4),
                                AX.X, ALU.max, negate=True).then_inc(s3_max, 1)

            def probs_out3(g, i):
                s = stage(g, i, T3, STEPS3, NG3)
                if s is None:
                    return
                grp, k = s
                f = STEPS3 * grp + k
                dve.wait_ge(t3_mm, f + 1)
                wait(dve, o3_mm, f - 1)
                V.tensor_copy(probT3[:, k % 2].rearrange("p o t -> p (o t)"), bank(4)).then_inc(t3_out, 1)

            def normalise3(g, i):
                s = stage(g, i, O3, STEPS3, NG3)
                if s is None or s[1] % 4 != 3:
                    return
                b = 4 * s[0] + s[1] // 4
                dve.wait_ge(o3_mm, 4 * (b + 1))
                wait(dve, u3_mm, b)
                o = bank(5)[:, 0:H1 * V1].rearrange("p (h d) -> p h d", h=H1)
                V.reciprocal(rsum3, o[:, :, HD1]).then_inc(o3_r, 1)
                dve.wait_ge(o3_r, b + 1)
                V.tensor_tensor(ctx3.rearrange("p (h d) -> p h d", h=H1), o[:, :, 0:HD1],
                                rsum3.unsqueeze(2).to_broadcast([P, H1, HD1]), ALU.mult).then_inc(o3_out, 1)

            def add3(g, i):
                s = stage(g, i, Y3, STEPS3, NG3)
                if s is None or s[1] % 4 != 3:
                    return
                b = 4 * s[0] + s[1] // 4
                dve.wait_ge(y3_mm, b + 1)
                xb = x[:, bass.ds(b, 1), :].rearrange("p a d -> p (a d)")
                V.tensor_tensor(xb, xb, bank(7)[:, D:2 * D], ALU.add).then_inc(y3_add, 1)

            def body3(g, i):
                row_max3(g, i)
                normalise3(g, i)
                probs_out3(g, i)
                add3(g, i)

            pipeline(dve, NG3, STEPS3, body3)
            barrier(dve, 4)

            def fp8(v, m, q):
                step(V.tensor_scalar(m.bitcast(U32), v.bitcast(U32), SIGN_EXP, None, ALU.bitwise_and))
                step(V.tensor_scalar(m, m, 2.0 ** -6, 1.5 * 2.0 ** 20, ALU.max, ALU.mult))
                step(V.tensor_tensor(v, v, m, ALU.add))
                return V.tensor_tensor(q, v, m, ALU.subtract)

            V.memset(ones, 1.0)
            for j in range(2):
                last = V.memset(wgu_n[FCH[-1][1]:P, NF * j + NF - 1, :], 1.0)
            last.then_inc(pad_set, 1)
            dve.wait_ge(ld_g, 16 * 2 * NF)
            dve.wait_ge(ld_d, 16)
            dve.wait_ge(pad_set, 1)
            V.tensor_reduce(ws[:, 0:2 * NF], wgu_n, AX.X, ALU.max, apply_absolute_value=True)
            step(V.tensor_reduce(ws[:, 2 * NF:], wd_n, AX.X, ALU.max, apply_absolute_value=True))
            step(V.tensor_scalar(ws, ws, 1.0 / FP8_MAX, None, ALU.mult))
            step(V.reciprocal(wr, ws))
            V.tensor_tensor(v_all[:, 0:2 * NF * D].rearrange("p (k d) -> p k d", d=D), wgu_n,
                            wr[:, 0:2 * NF].unsqueeze(2).to_broadcast([P, 2 * NF, D]), ALU.mult)
            step(V.tensor_tensor(v_all[:, 2 * NF * D:].rearrange("p (k f) -> p k f", f=FF), wd_n,
                                 wr[:, 2 * NF:].unsqueeze(2).to_broadcast([P, DC, FF]), ALU.mult))
            wq_all = raw[:, 8960:8960 + 2240].bitcast(BF16)
            fp8(v_all, m_all, wq_all).then_inc(w4_quant, 1)
            for k in range(2 * NF + DC):
                last = V.tensor_scalar(diag[:, k, :], ident[:], ws[:, k:k + 1], None, ALU.mult)
            last.then_inc(w4_diag, 1)
            barrier(dve, 5)

            def chain(s, f, total):
                done = [0]

                def link(ins, then=dve.wait_ge):
                    done[0] += 1
                    ins.then_inc(s, 1)
                    then(s, f * total + done[0])
                return link

            def quantise(v, tmp, m, q, s_r, link, before_q):
                link(V.tensor_reduce(s_r[:, 0:1], v, AX.X, ALU.max, apply_absolute_value=True))
                link(V.tensor_scalar(s_r[:, 0:1], s_r[:, 0:1], 1.0 / FP8_MAX, None, ALU.mult))
                link(V.reciprocal(s_r[:, 1:2], s_r[:, 0:1]))
                link(V.tensor_scalar(tmp, v, s_r[:, 1:2], None, ALU.mult))
                link(V.tensor_scalar(m.bitcast(U32), tmp.bitcast(U32), SIGN_EXP, None, ALU.bitwise_and))
                link(V.tensor_scalar(m, m, 2.0 ** -6, 1.5 * 2.0 ** 20, ALU.max, ALU.mult))
                link(V.tensor_tensor(tmp, tmp, m, ALU.add))
                before_q()
                return V.tensor_tensor(q, tmp, m, ALU.subtract)

            def seq(f):
                return x[:, bass.ds(f, 1), :].rearrange("p a d -> p (a d)")

            def quant_x(g, i):
                s = stage(g, i, 0, STEPS4, NG4)
                if s is None:
                    return
                grp, k = s
                f = STEPS4 * grp + k
                link = chain(x5, f, 9)
                link(V.bn_stats(st5[:, 0:6], seq(f)), lambda sm, v: wait_apart(dve, sm, v))
                V.bn_aggr(mv5, st5[:, 0:6]).then_inc(x5_stats, 1)
                dve.wait_ge(x5_rstd, f + 1)
                link(V.tensor_scalar(xn5, seq(f), mv5[:, 0:1], ve5[:, 1:2], ALU.subtract, ALU.mult))
                quantise(xn5, v5, m5, qx, sx[:, k, :], link,
                         lambda: wait(dve, x5_mm, f)).then_inc(x5_q, 1)

            def gated(g, i):
                s = stage(g, i, 1, STEPS4, NG4)
                if s is None:
                    return
                grp, k = s
                f = STEPS4 * grp + k
                link = chain(t5, f, 8)
                dve.wait_ge(gu_mm, f + 1)
                two = {"k": 2}
                V.tensor_tensor(tg.rearrange("p (k n) -> p k n", **two), ps[:, 0:2, 0:FF // 2],
                                wsb[:, 0:FF].rearrange("p (k n) -> p k n", **two), ALU.mult).then_inc(g_scaled, 1)
                V.tensor_tensor(tu.rearrange("p (k n) -> p k n", **two), ps[:, 2:4, 0:FF // 2],
                                wsb[:, FF:2 * FF].rearrange("p (k n) -> p k n", **two), ALU.mult).then_inc(gu_read, 1)
                dve.wait_ge(gu_read, f + 1)
                dve.wait_ge(silu_out, f + 1)
                link(V.scalar_tensor_tensor(tt, tu, sx[:, k, 0:1], tsl, ALU.mult, ALU.mult))
                quantise(tt, tv, tm, qt[:, k % 2, :], sx[:, STEPS4 + k, :], link,
                         lambda: wait(dve, t5_mm, f - 1)).then_inc(t5_q, 1)

            def add_ffn(g, i):
                s = stage(g, i, 2, STEPS4, NG4)
                if s is None:
                    return
                grp, k = s
                f = STEPS4 * grp + k
                dve.wait_ge(y5_mm, f + 1)
                wait(dve, x5_done, f)
                V.scalar_tensor_tensor(yt, bank(6)[:, 0:D], sx[:, STEPS4 + k, 0:1], wsdb,
                                       ALU.mult, ALU.mult).then_inc(y5_read, 1)
                dve.wait_ge(y5_read, f + 1)
                V.tensor_tensor(seq(f), seq(f), yt, ALU.add).then_inc(x5_done, 1)

            def body4(g, i):
                quant_x(g, i)
                gated(g, i)
                add_ffn(g, i)

            pipeline(dve, NG4, STEPS4, body4)

        @block.gpsimd
        def _(pool):
            G = nc.gpsimd
            pool.wait_ge(ln_stats, 1)
            G.tensor_tensor(rstd[:], veps[:], mhalf[:], ALU.pow).then_inc(ln_rstd, 1)
            barrier(pool, 1)

            def add_rope(g, i, h):
                s = stage(g, i, 0, NPAIR)
                if s is None:
                    return
                grp, p = s
                f = NPAIR * grp + p
                pool.wait_ge(q_scaled, 2 * f + h + 1)
                wait(pool, b_mm, f - 1)
                for half in range(2):
                    lo, other = half * GT, (1 - half) * GT
                    last = G.tensor_tensor(roped[:, p % 2, h, lo:lo + GT], t1[:, h, lo:lo + GT],
                                           t2[:, h, other:other + GT], ALU.add)
                last.then_inc(q_roped, 1)

            def rsqrt_var(g, i):
                s = stage(g, 0, 1, NPAIR)
                if s is None or i != Y_AT:
                    return
                grp = s[0]
                wait(pool, l_stats, grp + 1)
                G.tensor_tensor(veps[:, 0:GB], mv[:, 0:GB, 1], epst[:, 0:GB], ALU.add).then_inc(pool_step, 1)
                pool.wait_ge(pool_step, grp + 1)
                G.tensor_tensor(rstd[:, 0:GB], veps[:, 0:GB], mhalf[:, 0:GB], ALU.pow).then_inc(l_rstd, 1)

            def body(g, i):
                add_rope(g, i, 0)
                rsqrt_var(g, i)
                add_rope(g, i, 1)

            pipeline(pool, NG, NPAIR, body)
            barrier(pool, 2)

            def rsqrt2(g, i):
                s = stage(g, 0, 1, STEPS2, NG2)
                if s is None or i != 1:
                    return
                grp = s[0]
                wait(pool, n_stats, grp + 1)
                G.tensor_tensor(veps[:, 0:GB2], mv[:, 0:GB2, 1], epst[:, 0:GB2], ALU.add).then_inc(n_eps, 1)
                pool.wait_ge(n_eps, grp + 1)
                G.tensor_tensor(rstd[:, 0:GB2], veps[:, 0:GB2], mhalf[:, 0:GB2], ALU.pow).then_inc(n_rstd, 1)

            pipeline(pool, NG2, STEPS2, rsqrt2)
            barrier(pool, 3)
            barrier(pool, 4)

            pool.wait_ge(ld_i, 32)
            for j, name in enumerate(("L1_ffn_w_gate", "L1_ffn_w_up")):
                for k, (at, n) in enumerate(FCH):
                    ix = idx_a[:, k:k + 1] if k < NF - 1 else idx_b[:]
                    if k == NF - 1:
                        pool.wait_ge(pad_set, 1)
                    G.indirect_dma_start(
                        out=wgu_n[0:n, NF * j + k, :], out_offset=None, in_=a[name],
                        in_offset=bass.IndirectOffsetOnAxis(ap=ix.bitcast(U32), axis=0)).then_inc(ld_g, 16)
            barrier(pool, 5)

            def rsqrt4(g, i):
                s = stage(g, i, 0, STEPS4, NG4)
                if s is None:
                    return
                f = STEPS4 * s[0] + s[1]
                wait(pool, x5_stats, f + 1)
                G.tensor_tensor(ve5[:, 0:1], mv5[:, 1:2], epst[:, 0:1], ALU.add).then_inc(x5_eps, 1)
                pool.wait_ge(x5_eps, f + 1)
                G.tensor_tensor(ve5[:, 1:2], ve5[:, 0:1], mhalf[:, 0:1], ALU.pow).then_inc(x5_rstd, 1)

            pipeline(pool, NG4, STEPS4, rsqrt4)


def rope_tables(length, dim):
    f32 = np.float32
    inv = (f32(1.0) / np.power(f32(10000.0), np.arange(0, dim, 2, dtype=f32) / f32(dim))).astype(f32)
    f = np.arange(length, dtype=f32)[:, None] * inv[None, :]
    return np.repeat(np.sin(f), 2, axis=-1), np.repeat(np.cos(f), 2, axis=-1)


def kernel(**inputs):
    import ml_dtypes
    import concourse.bacc as _bacc
    from concourse.bass_utils import run_bass_kernel_spmd as _run

    w = {k: np.asarray(v) for k, v in inputs.items()}
    c = np.ascontiguousarray

    def chunks(m):
        return c(m.reshape(-1, P, m.shape[-1]).transpose(1, 0, 2))

    arr = {"x": c(w["x"].transpose(1, 0, 2)), "ctx": c(w["ctx_512"].transpose(1, 0, 2)),
           "ctxT": c(w["ctx_512"].reshape(NB * P, DCTX).T)}
    arr["L0_xattn_Wq"] = c(w["L0_xattn_Wq"].reshape(H0, K0, D).transpose(1, 0, 2))
    arr["L0_xattn_w_kc_q"] = c(w["L0_xattn_w_kc_q"].transpose(1, 0, 2))
    arr["L0_xattn_w_kc_kv"] = c(w["L0_xattn_w_kc_kv"].transpose(1, 0, 2))
    arr["L0_xattn_W_qr"] = c(w["L0_xattn_W_qr"].transpose(2, 0, 1))
    arr["L0_xattn_W_kr"] = c(w["L0_xattn_W_kr"].transpose(2, 0, 1))
    arr["L0_xattn_Wo"] = c(w["L0_xattn_Wo"].reshape(D, H0, K0).transpose(2, 1, 0))
    arr["L0_ffn_gate_w"] = chunks(w["L0_ffn_gate_w"])
    arr["L0_ffn_fc1_w"] = c(w["L0_ffn_fc1_w"].reshape(NE, DC, P, INTER).transpose(2, 0, 1, 3))
    arr["L0_ffn_fc2_w"] = c(w["L0_ffn_fc2_w"].reshape(NE, IC, P, D).transpose(2, 0, 1, 3))

    arr["L0_ffn_fc1_b"] = c(w["L0_ffn_fc1_b"].reshape(NE, IC, P).transpose(2, 0, 1))
    arr["L0_ffn_fc2_b"] = c(w["L0_ffn_fc2_b"])
    arr["L0_ffn_alpha"] = c(np.broadcast_to(w["L0_ffn_alpha"], (P, NE)))
    arr["L1_xattn_Wq"] = chunks(w["L1_xattn_Wq"].T)
    arr["L1_xattn_Wkv"] = c(w["L1_xattn_Wkv_expand"].T)
    arr["L1_xattn_Wout"] = chunks(w["L1_xattn_Wout"].T)
    arr["L1_ffn_w_gate"], arr["L1_ffn_w_up"] = c(w["L1_ffn_w_gate"]), c(w["L1_ffn_w_up"])
    arr["L1_ffn_w_down"] = chunks(w["L1_ffn_w_down"])
    di = w["L1_ffn_down_reorder_index"]
    whole = FF // P * P
    arr["idx_a"] = c(di[:whole].reshape(-1, P).T)
    arr["idx_b"] = c(di[whole:].reshape(-1, 1))
    arr["before"] = c(np.broadcast_to(np.tril(np.ones((NE, NE), np.float32), -1), (P, NE, NE)))

    sq, cq = rope_tables(P, DQ0)
    sk, ck = rope_tables(P, DCTX)
    two = (HALF, 2, GB, P)
    arr["rope_c"] = c(np.broadcast_to(cq.T.reshape(2, HALF, P).transpose(1, 0, 2)[:, :, None, :], two))
    ssw = np.stack([sq.T[HALF:], -sq.T[:HALF]], axis=1)
    arr["rope_s"] = c(np.broadcast_to(ssw[:, :, None, :], two))
    arr["ropek_c"] = c(ck)
    arr["ropek_s"] = c(np.concatenate([-sk[:, :DCTX // 2], sk[:, DCTX // 2:]], axis=1))
    arr["ident"] = np.eye(P, dtype=np.float32)
    arr["identb"] = np.eye(P).astype(ml_dtypes.bfloat16)
    causal = np.tril(np.ones((P, P), bool))
    arr["mask"] = c(np.broadcast_to(np.where(causal, 0.0, MASKED)[:, None, :], (P, 4, P)).astype(ml_dtypes.bfloat16))

    nc = _bacc.Bacc("TRN2", target_bir_lowering=False, num_devices=1)
    aps = {k: nc.dram_tensor(f"in_{k}", v.shape, mybir.dt.from_np(v.dtype), kind="ExternalInput").ap()
           for k, v in arr.items()}
    out = nc.dram_tensor("out_x", (P, NB, D), F32, kind="ExternalOutput").ap()
    build(nc, aps, out)
    r = _run(nc, [{f"in_{k}": v for k, v in arr.items()}], core_ids=[0])
    return c(r.results[0]["out_x"].transpose(1, 0, 2))
```

```python
from contextlib import ExitStack

import numpy as np

import concourse.bass as bass
from concourse import mybir

ALU = mybir.AluOpType
ACT = mybir.ActivationFunctionType
AX = mybir.AxisListType
F32 = mybir.dt.float32
BF16 = mybir.dt.bfloat16
U32 = mybir.dt.uint32
F32R = mybir.dt.float32r

P = 128
NB = 16
D = 256
DC = D // P
DCTX = 64
H0, K0, DQ0, R0 = 16, 128, 192, 64
HALF = DQ0 // 2
NPAIR = H0 // 2
NE, TOPK = 8, 2
INTER = 256
IC = INTER // P
H1, HD1 = 16, 16
V1 = HD1 + 1
FF = 704
FCH = [(c * P, min(P, FF - c * P)) for c in range(-(-FF // P))]
FP8_MAX = 448.0
LN_EPS = 1e-5
MASKED = -3.0e38

GB = 2
GT = GB * P
NG = NB // GB
GB2 = 4
T2 = GB2 * P
NG2 = NB // GB2
SIGN_EXP = 0x7F800000
ROUND_FP8 = 1.5 * 2.0 ** 20


def build(nc, a, out):
    with ExitStack() as ctx:
        def sb(name, shape, dt=F32):
            return ctx.enter_context(nc.sbuf_tensor(name, shape, dt))

        def sem(name):
            return ctx.enter_context(nc.semaphore(name))

        x = sb("x", [P, NB, D])
        xnT = sb("xnT", [P, 2, DC, NB * P])
        raw = sb("raw", [P, 16384])
        wc = sb("wc", [P, DC, H0, DQ0])
        wc_flat = wc[:].rearrange("p c h q -> p (c h q)")
        kvaug = sb("kvaug", [P, NB, DCTX + 1])
        ctxT = sb("ctxT", [DCTX, NB * P])
        rope_c = sb("rope_c", [HALF, 2, GB, P])
        rope_s = sb("rope_s", [HALF, 2, GB, P])
        ident = sb("ident", [P, P])
        identb = sb("identb", [P, P], BF16)
        mask = sb("mask", [P, 4, P], BF16)
        mv = sb("mv", [P, NB, 2])
        st6 = sb("st6", [P, NB, 6])
        rstd = sb("rstd", [P, NB])
        unread = sb("unread", [P, 1])
        epst = sb("epst", [P, NB])
        veps = sb("veps", [P, NB])
        mhalf = sb("mhalf", [P, NB])
        logits = sb("logits", [P, NB, NE])

        gatew = sb("gatew", [P, DC, NE])
        ropek_c = sb("ropek_c", [P, DCTX])
        ropek_s = sb("ropek_s", [P, DCTX])
        NF = len(FCH)
        idx_a = sb("idx_a", [P, NF - 1], mybir.dt.int32)
        idx_b = sb("idx_b", [FCH[-1][1], 1], mybir.dt.int32)
        with ExitStack() as early:
            def sb_early(name, shape):
                return early.enter_context(nc.sbuf_tensor(name, shape, F32))

            wqk = sb_early("wqk", [HALF, H0, 2, R0])
            wvo = sb_early("wvo", [P, NPAIR, D])
            kvT = sb_early("kvT", [P, NB * P])
            work = sb_early("work", [P, 7168])
        wgu_hi = sb("wgu_hi", [P, DC, 2 * FF], F32R)
        wgu_lo = sb("wgu_lo", [P, DC, 2 * FF], F32R)
        wd_hi = sb("wd_hi", [P, NF, D], F32R)
        wd_lo = sb("wd_lo", [P, NF, D], F32R)
        qxT = sb("qxT", [P, 2, DC, P], F32R)
        qtT = sb("qtT", [P, NF, P], F32R)

        def carve(region, at, parts, shape, dt=F32):
            n = int(np.prod(shape))
            if dt == BF16:
                v = region[0:parts, at:at + (n + 1) // 2].bitcast(BF16)
                v = v[:, 0:n]
            else:
                v = region[0:parts, at:at + n]
            names = "abcd"[:len(shape)]
            if len(shape) > 1:
                v = v.rearrange(f"p ({' '.join(names)}) -> p {' '.join(names)}",
                                **{k: s for k, s in zip(names[1:], shape[1:])})
            return v

        r_wq = carve(raw, 0, P, [H0, D])
        r_wkcq = carve(raw, 4096, P, [H0, DQ0])
        r_wqrT = carve(raw, 7168, R0, [H0, DQ0])
        r_wkrT = carve(raw, 10240, R0, [H0, DCTX])
        r_wkckv = carve(raw, 11264, P, [H0, DCTX])
        r_woT = carve(raw, 12288, P, [H0, D])
        xn_all = carve(work, 0, P, [NB, D])
        ctx_n = carve(work, 4096, P, [NB, DCTX])
        kvd = carve(work, 5120, P, [NB, 2, DCTX])
        t1 = carve(raw, 8192, HALF, [2, 512])
        t2 = carve(raw, 9216, HALF, [2, 512])
        roped = carve(raw, 10240, HALF, [2, 2, 512])
        qT = carve(raw, 12288, P, [2, GT])
        kvTg = carve(raw, 12800, P, [GT])
        prob = carve(raw, 13056, P, [2, 4, P])
        probT = carve(raw, 14080, P, [2, 4, P])
        ctxh = carve(raw, 15104, P, [2, GB, P])
        nmax = carve(raw, 15616, P, [2, 4])
        rsum = carve(raw, 15624, P, [2, 4])
        xn2 = carve(work, 0, P, [GB, D])
        ctxhT = carve(work, 512, P, [NPAIR, GT])
        xgT = carve(work, 2560, P, [DC, GT])
        fc1 = carve(raw, 0, P, [NE, DC, INTER])
        fc2 = carve(raw, 4096, P, [NE, IC, D])

        hT = carve(raw, 8192, P, [2, IC, T2])
        xn4 = carve(raw, 10240, P, [GB2, D])
        combT = carve(raw, 11264, NE, [T2])
        combg = carve(raw, 11776, P, [GB2, NE])
        expl = carve(work, 0, P, [NB, NE])
        above = carve(work, 128, P, [NB, NE, NE])
        tied = carve(work, 1152, P, [NB, NE, NE])
        rank = carve(work, 2176, P, [NB, NE])
        lmax = carve(work, 2304, P, [NB])
        comb = carve(work, 2432, P, [NB, NE])
        before = carve(work, 2560, P, [NE, NE])
        alpha = carve(work, 2624, P, [NE])
        fc1b = carve(work, 2632, P, [NE, IC])
        fc2b = carve(work, 2656, NE, [D])
        wq1 = carve(raw, 0, P, [DC, D])
        wqm = carve(raw, 512, P, [DC, DC, 2, P])
        wkv1 = carve(raw, 1536, DCTX, [2 * D])
        wout1 = carve(raw, 2048, P, [DC, D])
        vaug = carve(raw, 2560, P, [NB, H1, V1])
        q3 = carve(raw, 6912, P, [2, 2, DC, GT])
        k3 = carve(raw, 8960, P, [2, DC, GT])
        prob3 = carve(raw, 9984, P, [4, 4, P])
        probT3 = carve(raw, 12032, P, [2, 4, P])
        ctx3 = carve(raw, 13056, P, [D])
        ctx3T = carve(raw, 13312, P, [DC, P])
        nmax3 = carve(raw, 13568, P, [4, 4])
        rsum3 = carve(raw, 13584, P, [H1])
        qx_all = carve(raw, 13604, P, [NB, D], BF16)
        xn5 = carve(raw, 15652, P, [D])
        m5 = carve(raw, 15908, P, [D])
        sx_all = carve(raw, 16164, P, [NB])
        st5 = carve(raw, 16180, P, [6])
        mv5 = carve(raw, 16186, P, [2])
        ve5 = carve(raw, 16188, P, [2])
        s5 = carve(raw, 16190, P, [2])
        wgu_n = carve(wc_flat, 0, P, [2 * NF, D])
        wd_n = carve(wc_flat, 3072, P, [DC, FF])
        wm = carve(wc_flat, 4480, P, [3 * D])
        ws = carve(wc_flat, 5248, P, [2 * NF + DC])
        wr = carve(wc_flat, 5264, P, [2 * NF + DC])
        tsl = carve(raw, 0, P, [FF])
        tt = carve(raw, 704, P, [FF])
        tv = carve(raw, 1408, P, [2, FF])
        tm = carve(raw, 2816, P, [FF])
        qt = carve(raw, 3520, P, [2, FF], BF16)
        sxg = carve(raw, 4224, P, [4])
        st = carve(raw, 4228, P, [4, 2])

        ps = ctx.enter_context(nc.psum_tensor("ps", [P, 8, 512], F32))

        def bank(i):
            return ps[:, i, :]

        def bank16(i):
            return ps[:, i, :].bitcast(BF16)

        ld_x, ld_w, ld_c, ld_f = sem("ld_x"), sem("ld_w"), sem("ld_c"), sem("ld_f")
        ld_f1 = sem("ld_f1")
        phase_end = sem("phase_end")
        stored = sem("stored")
        dve_step = sem("dve_step")
        act_step = sem("act_step")
        pool_step = sem("pool_step")
        ln_stats, ln_rstd = sem("ln_stats"), sem("ln_rstd")
        kv_ready = sem("kv_ready")
        xn_ready = sem("xn_ready")
        norm_r, ln_a = sem("norm_r"), sem("ln_a")
        prep_mm, prep_act, prep_dve = sem("prep_mm"), sem("prep_act"), sem("prep_dve")
        q_mm, q_scaled, q_roped = sem("q_mm"), sem("q_scaled"), sem("q_roped")
        b_mm, b_out = sem("b_mm"), sem("b_out")
        kv_copied = sem("kv_copied")
        s_mm, s_max, s_exp = sem("s_mm"), sem("s_max"), sem("s_exp")
        t_mm, t_out = sem("t_mm"), sem("t_out")
        o_mm, o_out = sem("o_mm"), sem("o_out")
        u_mm, u_out = sem("u_mm"), sem("u_out")
        y_mm, y_add = sem("y_mm"), sem("y_add")
        l_stats, l_rstd, l_xn, l_mm, l_out = (sem("l_stats"), sem("l_rstd"), sem("l_xn"), sem("l_mm"),
                                              sem("l_out"))
        g_mm, g_out = sem("g_mm"), sem("g_out")

        ld_2, ld_3, ld_i, ld_g = sem("ld_2"), sem("ld_3"), sem("ld_i"), sem("ld_g")
        ld_d = sem("ld_d")
        gate_exp, gate_max, comb_ready = sem("gate_exp"), sem("gate_max"), sem("comb_ready")
        h_mm, h_out, f_mm, f_acc, f_cp = sem("h_mm"), sem("h_out"), sem("f_mm"), sem("f_acc"), sem("f_cp")
        n_a, n_stats, n_eps, n_rstd, n_xn, n_mm, n_out = (sem("n_a"), sem("n_stats"), sem("n_eps"), sem("n_rstd"),
                                                          sem("n_xn"), sem("n_mm"), sem("n_out"))
        w3_ready, v3_mm, v3_out = sem("w3_ready"), sem("v3_mm"), sem("v3_out")
        pj_mm, pj_out = sem("pj_mm"), sem("pj_out")
        s3_mm, s3_max, s3_exp, t3_mm, t3_out = (sem("s3_mm"), sem("s3_max"), sem("s3_exp"), sem("t3_mm"),
                                                sem("t3_out"))
        o3_mm, o3_r, o3_out, u3_mm, u3_out, y3_mm, y3_add = (sem("o3_mm"), sem("o3_r"), sem("o3_out"),
                                                             sem("u3_mm"), sem("u3_out"), sem("y3_mm"),
                                                             sem("y3_add"))
        pad_set = sem("pad_set")
        w4_mm, w4_hi, w4_lo = sem("w4_mm"), sem("w4_hi"), sem("w4_lo")
        w4_quant = sem("w4_quant")
        x5 = sem("x5")
        x5_stats, x5_eps, x5_rstd, x5_mm, x5_out = (sem("x5_stats"), sem("x5_eps"), sem("x5_rstd"),
                                                    sem("x5_mm"), sem("x5_out"))
        sxg_ready = sem("sxg_ready")
        gate_mm, up_mm, silu_out, t_prod, t_max, t_scale, t_recip, t_scaled = (
            sem("gate_mm"), sem("up_mm"), sem("silu_out"), sem("t_prod"), sem("t_max"), sem("t_scale"),
            sem("t_recip"), sem("t_scaled"))
        t_expo, t_magic, t_sum, t5_q, t5_mm, t5_out, y5_mm, x5_done = (
            sem("t_expo"), sem("t_magic"), sem("t_sum"), sem("t5_q"), sem("t5_mm"), sem("t5_out"),
            sem("y5_mm"), sem("x5_done"))

        counts = {}

        def wait(eng, s, v):
            if isinstance(v, int) and v <= 0:
                return
            eng.wait_ge(s, v)

        def wait_apart(eng, s, v):
            if isinstance(v, int):
                eng.wait_ge(s, v)
                return
            eng.wait_ge(s, v)
            nc.vector.memset(unread[:], 0.0)

        def then_next(eng, ins, s, key):
            counts[key] = counts.get(key, 0) + 1
            ins.then_inc(s, 1)
            eng.wait_ge(s, counts[key])

        def barrier(eng, n, engines=5):
            eng.drain().then_inc(phase_end, 1)
            eng.wait_ge(phase_end, engines * n)

        def stage(g, i, lag, steps, groups=NG):
            if isinstance(g, int):
                f = g * steps + i - lag
                if f < 0 or f >= groups * steps:
                    return None
                return f // steps, f % steps
            back = -((i - lag) // steps)
            return g - back, (i - lag) % steps

        def pipeline(eng, groups, steps, body):
            for i in range(steps):
                body(0, i)
            with eng.Fori(1, groups) as g:
                for i in range(steps):
                    body(g, i)
            for i in range(steps):
                body(groups, i)

        B_LAG, S_LAG, T_LAG, O_LAG, U_LAG = 1, 2, 3, 4, 5
        Y_AT, L_AT, G_AT = 5, 6, 7
        STEPS2, BIAS_AT, LN_AT = NE + 2, NE, NE + 1
        STEPS3, NG3 = 16, 4
        S3, T3, O3, U3, Y3 = 4, 6, 8, 9, 10
        W_TURNS = 2 * DC * 2 + NF // 2
        STEPS4, NG4 = 4, 4
        GU4, Q4, Y4 = 1, 2, 3
        QB, BB, SB, TB, OB, MB = (0, 1), 2, 3, 5, 6, 7

        CONSTS = [("ctx", ctx_n), ("ctxT", ctxT[:]), ("ropek_c", ropek_c[:]), ("ropek_s", ropek_s[:]),
                  ("ident", ident[:]), ("rope_c", rope_c[:]), ("rope_s", rope_s[:]),
                  ("L0_ffn_gate_w", gatew[:]), ("identb", identb[:]), ("mask", mask[:])]
        N_CONST = len(CONSTS)

        block = ctx.enter_context(nc.Block())

        @block.sync
        def _(sp):
            sp.dma_start(x[:], a["x"]).then_inc(ld_x, 16)
            sp.dma_start(r_wq, a["L0_xattn_Wq"]).then_inc(ld_w, 16)
            sp.dma_start(r_wkcq, a["L0_xattn_w_kc_q"]).then_inc(ld_w, 16)
            sp.dma_start(r_wqrT, a["L0_xattn_W_qr"]).then_inc(ld_w, 16)
            sp.dma_start(r_wkrT, a["L0_xattn_W_kr"]).then_inc(ld_w, 16)
            sp.dma_start(r_wkckv, a["L0_xattn_w_kc_kv"]).then_inc(ld_w, 16)
            sp.dma_start(r_woT, a["L0_xattn_Wo"]).then_inc(ld_w, 16)
            sp.dma_start(idx_a[:], a["idx_a"]).then_inc(ld_i, 16)
            sp.dma_start(idx_b[:], a["idx_b"]).then_inc(ld_i, 16)
            barrier(sp, 1)
            sp.dma_start(fc1, a["L0_ffn_fc1_w"]).then_inc(ld_f1, 16)
            sp.dma_start(fc2, a["L0_ffn_fc2_w"]).then_inc(ld_f1, 16)
            barrier(sp, 2)
            sp.dma_start(wd_n, a["L1_ffn_w_down"]).then_inc(ld_d, 16)
            for name, dst in (("before", before), ("L0_ffn_alpha", alpha), ("L0_ffn_fc1_b", fc1b),
                              ("L0_ffn_fc2_b", fc2b)):
                sp.dma_start(dst, a[name]).then_inc(ld_2, 16)
            barrier(sp, 3)
            for name, dst in (("L1_xattn_Wq", wq1), ("L1_xattn_Wkv", wkv1), ("L1_xattn_Wout", wout1)):
                sp.dma_start(dst, a[name]).then_inc(ld_3, 16)
            barrier(sp, 4)
            with sp.Fori(0, NG4) as g:
                sp.wait_ge(x5_done, (g + 1) * STEPS4)
                sp.dma_start(out[:, bass.ds(g * STEPS4, STEPS4), :],
                             x[:, bass.ds(g * STEPS4, STEPS4), :]).then_inc(stored, 16)
            sp.wait_ge(stored, 16 * NG4)

        PREP_WC, PREP_QK, PREP_VO, PREP_KV, PREP_LN = H0, H0 // 4, NPAIR // 2, NB // 4, NB // 2
        PREP = PREP_WC + PREP_QK + PREP_VO + PREP_KV + PREP_LN

        def prep_out(n):
            b = bank(n % 8)
            if n < PREP_WC:
                return b[:, 0:DC * DQ0].rearrange("p (c q) -> p c q", c=DC), wc[:, :, n, :]
            n -= PREP_WC
            if n < PREP_QK:
                return (b[0:HALF, :].rearrange("p (h a d) -> p h a d", h=4, a=2), wqk[:, 4 * n:4 * n + 4])
            n -= PREP_QK
            if n < PREP_VO:
                return b.rearrange("p (h o) -> p h o", h=2), wvo[:, 2 * n:2 * n + 2, :]
            n -= PREP_VO
            if n < PREP_KV:
                return b, kvT[:, 512 * n:512 * n + 512]
            n -= PREP_KV
            return (b.rearrange("p (c t) -> p c t", c=DC), xnT[:, 1, :, GT * n:GT * n + GT])

        def turned(u):
            if u < 4 * DC:
                j, hc, part = u // 4, u // 2 % DC, u % 2
                at, n = (0, 512) if part == 0 else (512, FF - 512)
                cols = slice(j * FF + at, j * FF + at + n)
                return wgu_hi[:, hc, cols], wgu_lo[:, hc, cols], bank(7)[:, 0:n]
            k = 2 * (u - 4 * DC)
            if FCH[k + 1][1] == P:
                b = bank(7).rearrange("p (k d) -> p k d", k=2)
                return wd_hi[:, k:k + 2], wd_lo[:, k:k + 2], b
            return wd_hi[:, k], wd_lo[:, k], bank(7)[:, 0:D]

        LAST_ROWS = FCH[-1][1]
        last_turn = (wd_hi[0:LAST_ROWS, NF - 1], wd_lo[0:LAST_ROWS, NF - 1], bank(7)[0:LAST_ROWS, D:2 * D])

        @block.tensor
        def _(pe):
            mm = nc.tensor.matmul
            pe.wait_ge(ld_c, 16 * N_CONST)
            pe.wait_ge(ld_w, 16 * 6)
            for n in range(PREP):
                if n >= 8:
                    pe.wait_ge(prep_dve if n % 2 else prep_act, (n - 8) // 2 + 1)
                to, _ = prep_out(n)
                if n < PREP_WC:
                    for c in range(DC):
                        last = mm(to[:, c, :], r_wq[:, n, c * P:(c + 1) * P], r_wkcq[:, n, :])
                elif n < PREP_WC + PREP_QK:
                    for k in range(4):
                        h = 4 * (n - PREP_WC) + k
                        for half in range(2):
                            last = mm(to[:, k, half, :], r_wqrT[:, h, half * HALF:(half + 1) * HALF],
                                      r_wkrT[:, h, :])
                elif n < PREP_WC + PREP_QK + PREP_VO:
                    for k in range(2):
                        for odd in range(2):
                            h = 4 * (n - PREP_WC - PREP_QK) + 2 * k + odd
                            last = mm(to[64 * odd:64 * odd + 64, k, :], r_wkckv[:, h, :], r_woT[:, h, :])
                elif n < PREP - PREP_LN:
                    for k in range(4):
                        b = 4 * (n - PREP_WC - PREP_QK - PREP_VO) + k
                        pe.wait_ge(kv_ready, 2)
                        last = nc.tensor.transpose(to[:, k * P:(k + 1) * P],
                                                   kvd[:, b].rearrange("p a d -> p (a d)"), ident[:])
                else:
                    g = n - (PREP - PREP_LN)
                    pe.wait_ge(xn_ready, GB * (g + 1))
                    for k in range(GB):
                        for c in range(DC):
                            last = nc.tensor.transpose(to[:, c, k * P:(k + 1) * P],
                                                       xn_all[:, GB * g + k, c * P:(c + 1) * P], ident[:])
                last.then_inc(prep_mm, 1)
            barrier(pe, 1)

            def query(g, i, h):
                s = stage(g, i, 0, NPAIR)
                if s is None:
                    return
                grp, p = s
                f = NPAIR * grp + p
                wait(pe, q_scaled, 2 * f + h - 1)
                o = bank(QB[h])[0:HALF, :]
                for half in range(2):
                    for c in range(DC):
                        last = mm(o[:, half * GT:(half + 1) * GT],
                                  wc[:, c, 2 * p + h, half * HALF:(half + 1) * HALF],
                                  xnT[:, 1, c, bass.ds(grp * GT, GT)], start=(c == 0), stop=(c == DC - 1))
                last.then_inc(q_mm, 1)

            def to_rank(g, i):
                s = stage(g, i, B_LAG, NPAIR)
                if s is None:
                    return
                grp, p = s
                f = NPAIR * grp + p
                pe.wait_ge(q_roped, 2 * f + 2)
                wait(pe, b_out, f)
                for h in range(2):
                    for half in range(2):
                        last = mm(bank(BB)[64 * h:64 * h + 64, 0:GT], wqk[:, 2 * p + h, half, :],
                                  roped[:, p % 2, h, half * GT:(half + 1) * GT],
                                  start=(half == 0), stop=(half == 1))
                last.then_inc(b_mm, 1)

            def scores(g, i):
                s = stage(g, i, S_LAG, NPAIR)
                if s is None:
                    return
                grp, p = s
                f = NPAIR * grp + p
                pe.wait_ge(b_out, f + 1)
                if p == 0:
                    pe.wait_ge(kv_copied, grp + 1)
                wait(pe, s_exp, f)
                for h in range(2):
                    for b in range(GB):
                        last = mm(bank(SB + h)[:, b * P:(b + 1) * P],
                                  qT[64 * h:64 * h + 64, p % 2, b * P:(b + 1) * P],
                                  kvTg[64 * h:64 * h + 64, b * P:(b + 1) * P])
                last.then_inc(s_mm, 1)

            def transpose_p(g, i):
                s = stage(g, i, T_LAG, NPAIR)
                if s is None:
                    return
                grp, p = s
                f = NPAIR * grp + p
                pe.wait_ge(s_exp, f + 1)
                wait(pe, t_out, f)
                for k in range(4):
                    last = nc.tensor.transpose(bank(TB)[:, k * P:(k + 1) * P], prob[:, p % 2, k, :], ident[:])
                last.then_inc(t_mm, 1)

            def mix(g, i):
                s = stage(g, i, O_LAG, NPAIR)
                if s is None:
                    return
                grp, p = s
                f = NPAIR * grp + p
                pe.wait_ge(t_out, f + 1)
                wait(pe, o_out, f)
                for h in range(2):
                    for b in range(GB):
                        k = 2 * h + b
                        last = mm(bank(OB)[:, k * (DCTX + 1):(k + 1) * (DCTX + 1)], probT[:, p % 2, k, :],
                                  kvaug[:, bass.ds(grp * GB + b, 1), :].rearrange("p a d -> p (a d)"))
                last.then_inc(o_mm, 1)

            def transpose_c(g, i):
                s = stage(g, i, U_LAG, NPAIR)
                if s is None:
                    return
                grp, p = s
                f = NPAIR * grp + p
                pe.wait_ge(o_out, f + 1)
                wait(pe, u_out, f)
                if p == 0:
                    wait(pe, y_add, grp)
                if p == 1:
                    wait(pe, l_out, grp)
                if p == 2:
                    wait(pe, g_out, grp)
                for b in range(GB):
                    last = nc.tensor.transpose(bank(MB)[:, b * P:(b + 1) * P], ctxh[:, p % 2, b, :], ident[:])
                last.then_inc(u_mm, 1)

            def close_group(g, i):
                s = stage(g, 0, 1, NPAIR)
                if s is None or i not in (Y_AT, L_AT, G_AT):
                    return
                grp = s[0]
                more = not isinstance(g, int) or g < NG
                if i == Y_AT:
                    pe.wait_ge(u_out, NPAIR * (grp + 1))
                    for b in range(GB):
                        for p in range(NPAIR):
                            last = mm(bank(MB)[:, b * D:(b + 1) * D], ctxhT[:, p, b * P:(b + 1) * P],
                                      wvo[:, p, :], start=(p == 0), stop=(p == NPAIR - 1))
                    last.then_inc(y_mm, 1)
                if i == L_AT:
                    pe.wait_ge(l_xn, grp + 1)
                    pe.wait_ge(u_out, NPAIR * (grp + 1) + more)
                    pe.wait_ge(y_add, grp + 1)
                    for b in range(GB):
                        for c in range(DC):
                            last = nc.tensor.transpose(bank(MB)[:, c * GT + b * P:c * GT + (b + 1) * P],
                                                       xn2[:, b, c * P:(c + 1) * P], ident[:])
                    last.then_inc(l_mm, 1)
                if i == G_AT:
                    pe.wait_ge(l_out, grp + 1)
                    pe.wait_ge(u_out, NPAIR * (grp + 1) + 2 * more)
                    for b in range(GB):
                        for c in range(DC):
                            last = mm(bank(MB)[:, b * NE:(b + 1) * NE], xgT[:, c, b * P:(b + 1) * P],
                                      gatew[:, c, :], start=(c == 0), stop=(c == DC - 1))
                    last.then_inc(g_mm, 1)

            def body(g, i):
                query(g, i, 0)
                scores(g, i)
                close_group(g, i)
                query(g, i, 1)
                transpose_p(g, i)
                mix(g, i)
                transpose_c(g, i)
                to_rank(g, i)

            pipeline(pe, NG, NPAIR, body)
            barrier(pe, 2)

            pe.wait_ge(ld_f1, 32)
            pe.wait_ge(ld_2, 64)

            def up(g, i):
                s = stage(g, i, 0, STEPS2, NG2)
                if s is None or i > BIAS_AT:
                    return
                grp, e = s
                n = (NE + 1) * grp + e
                wait(pe, h_out, n if e < 2 else n - 1)
                if e == BIAS_AT:
                    pe.wait_ge(f_cp, grp + 1)
                    for b in range(GB2):
                        last = nc.tensor.transpose(bank(0)[0:NE, b * P:(b + 1) * P], combg[:, b, :], ident[:])
                else:
                    for m in range(IC):
                        for c in range(DC):
                            last = mm(bank(2 * (e % 2) + m), fc1[:, e, c, m * P:(m + 1) * P],
                                      xnT[:, 0, c, bass.ds(grp * T2, T2)], start=(c == 0), stop=(c == DC - 1))
                last.then_inc(h_mm, 1)

            def down(g, i):
                s = stage(g, i, 1, STEPS2, NG2)
                if s is None or s[1] > BIAS_AT:
                    return
                grp, e = s
                n = (NE + 1) * grp + e
                pe.wait_ge(h_out, n + 1)
                wait(pe, f_acc, n - (0 if e == 0 else 1))
                for b in range(GB2):
                    o = bank(4 + 2 * (e % 2) + b // 2)[:, (b % 2) * D:(b % 2 + 1) * D]
                    if e == BIAS_AT:
                        last = mm(o, combT[:, b * P:(b + 1) * P], fc2b)
                    else:
                        for m in range(IC):
                            last = mm(o, hT[:, e % 2, m, b * P:(b + 1) * P], fc2[:, e, m, :],
                                      start=(m == 0), stop=(m == IC - 1))
                last.then_inc(f_mm, 1)

            def next_x(g, i):
                s = stage(g, 0, 1, STEPS2, NG2)
                if s is None or i != LN_AT:
                    return
                grp = s[0]
                pe.wait_ge(n_xn, grp + 1)
                if not isinstance(g, int) or g < NG2:
                    pe.wait_ge(h_out, (NE + 1) * (grp + 1) + NE)
                else:
                    pe.wait_ge(n_out, grp)
                for c in range(DC):
                    for b in range(GB2):
                        last = nc.tensor.transpose(bank(2 + c)[:, b * P:(b + 1) * P],
                                                   xn4[:, b, c * P:(c + 1) * P], ident[:])
                last.then_inc(n_mm, 1)

            def body2(g, i):
                up(g, i)
                next_x(g, i)
                down(g, i)

            pipeline(pe, NG2, STEPS2, body2)
            barrier(pe, 3)

            pe.wait_ge(ld_3, 48)
            for n in range(NB // 2):
                wait(pe, v3_out, n - 7)
                for b in range(2):
                    last = mm(bank(n % 8)[:, b * D:(b + 1) * D], ctxT[:, (2 * n + b) * P:(2 * n + b + 1) * P],
                              wkv1[:, D:2 * D])
                last.then_inc(v3_mm, 1)
            pe.wait_ge(w3_ready, 1)
            pe.wait_ge(v3_out, NB // 2)

            def project(g, i):
                s = stage(g, i, 0, STEPS3, NG3)
                if s is None or i % 8 > 2:
                    return
                grp, u = s[0], i % 8
                half = 2 * grp + i // 8
                wait(pe, pj_out, 3 * half + u)
                tok = bass.ds(half * GT, GT)
                for ct in range(DC):
                    o = bank(6)[:, ct * GT:(ct + 1) * GT]
                    if u == 2:
                        last = mm(o, wkv1[:, ct * P:(ct + 1) * P], ctxT[:, tok])
                    else:
                        for c in range(DC):
                            last = mm(o, wqm[:, c, ct, u, :], xnT[:, 1, c, tok], start=(c == 0), stop=(c == DC - 1))
                last.then_inc(pj_mm, 1)

            def scores3(g, i):
                s = stage(g, i, S3, STEPS3, NG3)
                if s is None:
                    return
                grp, k = s
                f, half, b, w = STEPS3 * grp + k, 2 * grp + k // 8, k // 4 % 2, k % 4
                if k % 8 == 0:
                    pe.wait_ge(pj_out, 3 * half + 3)
                wait(pe, s3_exp, f - 3)
                mm(bank(w), identb[:], mask[:].rearrange("p k l -> p (k l)"), start=True, stop=False)
                r = slice(32 * w, 32 * w + 32)
                t = slice(b * P, (b + 1) * P)
                for ct in range(DC):
                    for e in range(2):
                        o = 2 * ct + e
                        last = mm(bank(w)[:, o * P:(o + 1) * P], q3[r, k // 8, e, ct, t], k3[r, k // 8, ct, t],
                                  start=False, stop=(o == 3))
                last.then_inc(s3_mm, 1)

            def transpose3(g, i):
                s = stage(g, i, T3, STEPS3, NG3)
                if s is None:
                    return
                grp, k = s
                f = STEPS3 * grp + k
                pe.wait_ge(s3_exp, f + 1)
                wait(pe, t3_out, f)
                for o in range(4):
                    last = nc.tensor.transpose(bank(4)[:, o * P:(o + 1) * P], prob3[:, k % 4, o, :], ident[:])
                last.then_inc(t3_mm, 1)

            def mix3(g, i):
                s = stage(g, i, O3, STEPS3, NG3)
                if s is None:
                    return
                grp, k = s
                f, b, w = STEPS3 * grp + k, 4 * grp + k // 4, k % 4
                pe.wait_ge(t3_out, f + 1)
                if w == 0:
                    wait(pe, o3_out, b)
                for ct in range(DC):
                    for e in range(2):
                        h = 8 * ct + 2 * w + e
                        last = mm(bank(5)[:, h * V1:(h + 1) * V1], probT3[:, k % 2, 2 * ct + e, :],
                                  vaug[:, bass.ds(b, 1), h, :].rearrange("p a d -> p (a d)"))
                last.then_inc(o3_mm, 1)

            def turn_weights(g, i):
                if not isinstance(g, int) or g > 0 or i >= W_TURNS:
                    return
                pe.wait_ge(w4_quant, 1)
                wait(pe, w4_lo, i)
                if i < 4 * DC:
                    j, hc, part = i // 4, i // 2 % DC, i % 2
                    for k in range(4 * part, min(NF, 4 * part + 4)):
                        n = FCH[k][1]
                        o = (k - 4 * part) * P
                        last = nc.tensor.transpose(bank(7)[:, o:o + n], wgu_n[0:n, NF * j + k, hc * P:(hc + 1) * P],
                                                   ident[0:n, 0:n])
                else:
                    for q in range(2):
                        at, n = FCH[2 * (i - 4 * DC) + q]
                        for c in range(DC):
                            last = nc.tensor.transpose(bank(7)[0:n, q * D + c * P:q * D + (c + 1) * P],
                                                       wd_n[:, c, at:at + n], ident[:])
                last.then_inc(w4_mm, 1)

            def project_out(g, i):
                s = stage(g, i, U3, STEPS3, NG3)
                if s is not None and s[1] % 4 == 3:
                    b = 4 * s[0] + s[1] // 4
                    pe.wait_ge(o3_out, b + 1)
                    wait(pe, y3_add, b)
                    pe.wait_ge(w4_lo, W_TURNS)
                    for c in range(DC):
                        last = nc.tensor.transpose(bank(7)[:, c * P:(c + 1) * P], ctx3[:, c * P:(c + 1) * P], ident[:])
                    last.then_inc(u3_mm, 1)
                s = stage(g, i, Y3, STEPS3, NG3)
                if s is not None and s[1] % 4 == 3:
                    b = 4 * s[0] + s[1] // 4
                    pe.wait_ge(u3_out, b + 1)
                    for c in range(DC):
                        last = mm(bank(7)[:, D:2 * D], ctx3T[:, c, :], wout1[:, c, :],
                                  start=(c == 0), stop=(c == DC - 1))
                    last.then_inc(y3_mm, 1)

            def body3(g, i):
                project(g, i)
                scores3(g, i)
                turn_weights(g, i)
                mix3(g, i)
                transpose3(g, i)
                project_out(g, i)

            pipeline(pe, NG3, STEPS3, body3)
            barrier(pe, 4)

            def x_turned(g, i):
                s = stage(g, i, 0, STEPS4, NG4)
                if s is None:
                    return
                f = STEPS4 * s[0] + s[1]
                wait(pe, x5_out, f)
                for c in range(DC):
                    last = nc.tensor.transpose(bank16(4)[:, c * P:(c + 1) * P],
                                               qx_all[:, bass.ds(f, 1), c * P:(c + 1) * P]
                                               .rearrange("p a d -> p (a d)"), identb[:])
                last.then_inc(x5_mm, 1)

            def gate_up(g, i):
                s = stage(g, i, GU4, STEPS4, NG4)
                if s is None:
                    return
                grp, k = s
                f = STEPS4 * grp + k
                pe.wait_ge(x5_out, f + 1)
                wait(pe, silu_out, f)
                for o in range(4):
                    if o == 2:
                        last.then_inc(gate_mm, 1)
                        wait(pe, t_prod, f)
                    cols = slice(o * (FF // 2), (o + 1) * (FF // 2))
                    for c in range(DC):
                        mm(bank(o)[:, 0:FF // 2], qxT[:, k % 2, c, :], wgu_hi[:, c, cols],
                           start=(c == 0), stop=False)
                        last = mm(bank(o)[:, 0:FF // 2], qxT[:, k % 2, c, :], wgu_lo[:, c, cols],
                                  start=False, stop=(c == DC - 1))
                last.then_inc(up_mm, 1)

            def t_turned(g, i):
                s = stage(g, i, Y4, STEPS4, NG4)
                if s is None:
                    return
                grp, k = s
                f = STEPS4 * grp + k
                pe.wait_ge(t5_q, f + 1)
                wait(pe, t5_out, f)
                for c, (at, n) in enumerate(FCH):
                    last = nc.tensor.transpose(bank16(5)[0:n, c * P:(c + 1) * P], qt[:, k % 2, at:at + n], identb[:])
                last.then_inc(t5_mm, 1)

            def y_down(g, i):
                s = stage(g, i, Y4, STEPS4, NG4)
                if s is None:
                    return
                grp, k = s
                f = STEPS4 * grp + k
                pe.wait_ge(t5_out, f + 1)
                wait(pe, x5_done, f)
                for c, (at, n) in enumerate(FCH):
                    mm(bank(6)[:, 0:D], qtT[0:n, c, :], wd_hi[0:n, c, :], start=(c == 0), stop=False)
                    last = mm(bank(6)[:, 0:D], qtT[0:n, c, :], wd_lo[0:n, c, :],
                              start=False, stop=(c == NF - 1))
                last.then_inc(y5_mm, 1)

            def body4(g, i):
                gate_up(g, i)
                t_turned(g, i)
                x_turned(g, i)
                y_down(g, i)

            pipeline(pe, NG4, STEPS4, body4)

        @block.scalar
        def _(act):
            def copy(o, i):
                return nc.scalar.activation(o, i, ACT.Copy)

            for name, dst in CONSTS:
                act.dma_start(dst, a[name]).then_inc(ld_c, 16)
            for n in range(0, PREP, 2):
                act.wait_ge(prep_mm, n + 1)
                src, dst = prep_out(n)
                copy(dst, src).then_inc(prep_act, 1)
            barrier(act, 1)

            def exps(g, i):
                s = stage(g, i, S_LAG, NPAIR)
                if s is None:
                    return
                grp, p = s
                f = NPAIR * grp + p
                act.wait_ge(s_max, f + 1)
                wait(act, t_mm, f - 1)
                for k in range(4):
                    last = nc.scalar.activation(prob[:, p % 2, k, :],
                                                bank(SB + k // 2)[:, (k % 2) * P:(k % 2 + 1) * P],
                                                ACT.Exp, bias=nmax[:, p % 2, k:k + 1])
                last.then_inc(s_exp, 1)

            def probs_out(g, i):
                s = stage(g, i, T_LAG, NPAIR)
                if s is None:
                    return
                grp, p = s
                f = NPAIR * grp + p
                act.wait_ge(t_mm, f + 1)
                wait(act, o_mm, f - 1)
                copy(probT[:, p % 2].rearrange("p k t -> p (k t)"), bank(TB)).then_inc(t_out, 1)

            def ctx_out(g, i):
                s = stage(g, i, U_LAG, NPAIR)
                if s is None:
                    return
                grp, p = s
                f = NPAIR * grp + p
                act.wait_ge(u_mm, f + 1)
                if p == 0:
                    wait(act, y_mm, grp)
                copy(ctxhT[:, p, :], bank(MB)[:, 0:GT]).then_inc(u_out, 1)

            def close_group(g, i):
                s = stage(g, 0, 1, NPAIR)
                if s is None:
                    return
                grp = s[0]
                if i == L_AT:
                    act.wait_ge(l_mm, grp + 1)
                    src = bank(MB).rearrange("p (c t) -> p c t", c=DC)
                    copy(xgT[:, :, :], src)
                    copy(xnT[:, 0, :, bass.ds(grp * GT, GT)], src).then_inc(l_out, 1)
                if i == G_AT:
                    act.wait_ge(g_mm, grp + 1)
                    copy(logits[:, bass.ds(grp * GB, GB), :],
                         bank(MB)[:, 0:GB * NE].rearrange("p (b e) -> p b e", b=GB)).then_inc(g_out, 1)

            def q_out(g, i):
                s = stage(g, i, B_LAG, NPAIR)
                if s is None:
                    return
                grp, p = s
                f = NPAIR * grp + p
                act.wait_ge(b_mm, f + 1)
                wait(act, s_mm, f - 1)
                copy(qT[:, p % 2, :], bank(BB)[:, 0:GT]).then_inc(b_out, 1)

            def group_kv(g, i):
                s = stage(g, i, S_LAG, NPAIR)
                if s is None or s[1] != 0:
                    return
                grp = s[0]
                wait(act, s_mm, NPAIR * grp)
                copy(kvTg, kvT[:, bass.ds(grp * GT, GT)]).then_inc(kv_copied, 1)

            def body(g, i):
                group_kv(g, i)
                exps(g, i)
                close_group(g, i)
                probs_out(g, i)
                ctx_out(g, i)
                q_out(g, i)

            pipeline(act, NG, NPAIR, body)
            barrier(act, 2)

            act.wait_ge(gate_max, 1)
            nc.scalar.activation(expl, expl, ACT.Exp).then_inc(gate_exp, 1)
            act.wait_ge(ld_2, 64)

            def gelu(g, i):
                s = stage(g, i, 0, STEPS2, NG2)
                if s is None or i > BIAS_AT:
                    return
                grp, e = s
                n = (NE + 1) * grp + e
                act.wait_ge(h_mm, n + 1)
                if e == BIAS_AT:
                    wait(act, f_mm, n - NE)
                    copy(combT, bank(0)[0:NE, :]).then_inc(h_out, 1)
                    return
                wait(act, f_mm, n - 1 if e >= 2 else n - 2)
                for m in range(IC):
                    last = nc.scalar.activation(hT[:, e % 2, m, :], bank(2 * (e % 2) + m), ACT.Gelu,
                                                bias=fc1b[:, e, m:m + 1])
                last.then_inc(h_out, 1)

            def next_x(g, i):
                s = stage(g, 0, 1, STEPS2, NG2)
                if s is None or i != LN_AT:
                    return
                grp = s[0]
                act.wait_ge(n_mm, grp + 1)
                for c in range(DC):
                    last = copy(xnT[:, 1, c, bass.ds(grp * T2, T2)], bank(2 + c))
                last.then_inc(n_out, 1)

            def body2(g, i):
                gelu(g, i)
                next_x(g, i)

            pipeline(act, NG2, STEPS2, body2)
            barrier(act, 3)

            act.wait_ge(w3_ready, 1)
            for n in range(NB // 2):
                act.wait_ge(v3_mm, n + 1)
                for b in range(2):
                    last = copy(vaug[:, 2 * n + b, :, 0:HD1],
                                bank(n % 8)[:, b * D:(b + 1) * D].rearrange("p (h d) -> p h d", h=H1))
                last.then_inc(v3_out, 1)

            def project(g, i):
                s = stage(g, i, 0, STEPS3, NG3)
                if s is None or i % 8 > 2:
                    return
                grp, u = s[0], i % 8
                half = 2 * grp + i // 8
                act.wait_ge(pj_mm, 3 * half + u + 1)
                wait(act, s3_mm, 8 * (half - 1))
                dst = k3[:, i // 8] if u == 2 else q3[:, i // 8, u]
                copy(dst.rearrange("p c t -> p (c t)"), bank(6)).then_inc(pj_out, 1)

            def exps3(g, i):
                s = stage(g, i, S3, STEPS3, NG3)
                if s is None:
                    return
                grp, k = s
                f = STEPS3 * grp + k
                act.wait_ge(s3_max, f + 1)
                wait(act, t3_mm, f - 3)
                for o in range(4):
                    last = nc.scalar.activation(prob3[:, k % 4, o, :], bank(k % 4)[:, o * P:(o + 1) * P],
                                                ACT.Exp, bias=nmax3[:, k % 4, o:o + 1])
                last.then_inc(s3_exp, 1)

            def weights_hi(g, i):
                if not isinstance(g, int) or g > 0 or i >= W_TURNS:
                    return
                act.wait_ge(w4_mm, i + 1)
                hi, _, src = turned(i)
                if i == W_TURNS - 1:
                    copy(hi, src)
                    hi, _, src = last_turn
                copy(hi, src).then_inc(w4_hi, 1)

            def ctx_out3(g, i):
                s = stage(g, i, U3, STEPS3, NG3)
                if s is None or s[1] % 4 != 3:
                    return
                b = 4 * s[0] + s[1] // 4
                act.wait_ge(u3_mm, b + 1)
                wait(act, y3_mm, b)
                copy(ctx3T.rearrange("p c t -> p (c t)"), bank(7)[:, 0:D]).then_inc(u3_out, 1)

            def body3(g, i):
                project(g, i)
                exps3(g, i)
                weights_hi(g, i)
                ctx_out3(g, i)

            pipeline(act, NG3, STEPS3, body3)
            barrier(act, 4)

            def x_turned(g, i):
                s = stage(g, i, 0, STEPS4, NG4)
                if s is None:
                    return
                grp, k = s
                f = STEPS4 * grp + k
                act.wait_ge(x5_mm, f + 1)
                wait(act, up_mm, f - 1)
                copy(qxT[:, k % 2].rearrange("p c t -> p (c t)"), bank16(4)[:, 0:D]).then_inc(x5_out, 1)

            def silu(g, i):
                s = stage(g, i, GU4, STEPS4, NG4)
                if s is None:
                    return
                grp, k = s
                f = STEPS4 * grp + k
                if k == 0:
                    act.wait_ge(sxg_ready, grp + 1)
                act.wait_ge(gate_mm, f + 1)
                wait(act, t_prod, f)
                nc.scalar.activation(tsl.rearrange("p (k n) -> p k n", k=2), ps[:, 0:2, 0:FF // 2], ACT.Silu,
                                     scale=sxg[:, k:k + 1]).then_inc(silu_out, 1)

            def scale_t(g, i):
                s = stage(g, i, GU4, STEPS4, NG4)
                if s is None:
                    return
                grp, k = s
                f = STEPS4 * grp + k
                act.wait_ge(t_recip, f + 1)
                wait(act, t5_q, f - 1)
                nc.scalar.activation(tv[:, k % 2, :], tt, ACT.Copy, scale=st[:, k, 1:2]).then_inc(t_scaled, 1)

            def t_turned(g, i):
                s = stage(g, i, Y4, STEPS4, NG4)
                if s is None:
                    return
                grp, k = s
                f = STEPS4 * grp + k
                act.wait_ge(t5_mm, f + 1)
                wait(act, y5_mm, f)
                copy(qtT[:, 0:NF - 1, :].rearrange("p c t -> p (c t)"), bank16(5)[:, 0:(NF - 1) * P])
                copy(qtT[0:LAST_ROWS, NF - 1, :],
                     bank16(5)[0:LAST_ROWS, (NF - 1) * P:NF * P]).then_inc(t5_out, 1)

            def body4(g, i):
                silu(g, i)
                t_turned(g, i)
                x_turned(g, i)
                scale_t(g, i)

            pipeline(act, NG4, STEPS4, body4)

        @block.vector
        def _(dve):
            V = nc.vector

            def step(ins):
                then_next(dve, ins, dve_step, "dve")

            V.memset(mhalf[:], -0.5)
            V.memset(epst[:], LN_EPS)
            V.memset(kvaug[:, :, DCTX:DCTX + 1], 1.0)
            dve.wait_ge(ld_x, 16)
            for b in range(NB):
                V.bn_stats(st6[:, b, :], x[:, b, :])
            step(V.memset(veps[:], 0.0))
            for b in range(NB):
                last = V.bn_aggr(mv[:, b, :], st6[:, b, :])
            step(last)
            V.tensor_scalar(veps[:], mv[:, :, 1], LN_EPS, None, ALU.add).then_inc(ln_stats, 1)
            dve.wait_ge(ld_c, 16 * N_CONST)
            hc = DCTX // 2
            cb = ropek_c[:].unsqueeze(1).to_broadcast([P, NB, DCTX])
            tmp = kvd[:, :, 1, :]
            V.tensor_tensor(kvaug[:, :, 0:DCTX], ctx_n, cb, ALU.mult)
            V.tensor_tensor(tmp[:, :, 0:hc], ctx_n[:, :, hc:DCTX],
                            ropek_s[:, 0:hc].unsqueeze(1).to_broadcast([P, NB, hc]), ALU.mult)
            step(V.tensor_tensor(tmp[:, :, hc:DCTX], ctx_n[:, :, 0:hc],
                                 ropek_s[:, hc:DCTX].unsqueeze(1).to_broadcast([P, NB, hc]), ALU.mult))
            step(V.tensor_tensor(kvaug[:, :, 0:DCTX], kvaug[:, :, 0:DCTX], tmp, ALU.add))
            V.tensor_copy(kvd[:, :, 0, :], kvaug[:, :, 0:DCTX]).then_inc(kv_ready, 1)
            V.tensor_copy(kvd[:, :, 1, :], kvaug[:, :, 0:DCTX]).then_inc(kv_ready, 1)
            dve.wait_ge(ln_rstd, 1)
            for b in range(NB):
                V.tensor_scalar(xn_all[:, b, :], x[:, b, :], mv[:, b, 0:1], rstd[:, b:b + 1],
                                ALU.subtract, ALU.mult).then_inc(xn_ready, 1)
            for n in range(1, PREP, 2):
                dve.wait_ge(prep_mm, n + 1)
                src, dst = prep_out(n)
                V.tensor_copy(dst, src).then_inc(prep_dve, 1)
            barrier(dve, 1)

            rc = rope_c[:].rearrange("p a b t -> p (a b t)")
            rs = rope_s[:].rearrange("p a b t -> p (a b t)")

            def rope(g, i, h):
                s = stage(g, i, 0, NPAIR)
                if s is None:
                    return
                grp, p = s
                f = NPAIR * grp + p
                dve.wait_ge(q_mm, 2 * f + h + 1)
                wait(dve, q_roped, 2 * f + h - 1)
                q = bank(QB[h])[0:HALF, :]
                V.tensor_tensor(t1[:, h, :], q, rc, ALU.mult)
                V.tensor_tensor(t2[:, h, :], q, rs, ALU.mult).then_inc(q_scaled, 1)

            def row_max(g, i):
                s = stage(g, i, S_LAG, NPAIR)
                if s is None:
                    return
                grp, p = s
                f = NPAIR * grp + p
                dve.wait_ge(s_mm, f + 1)
                wait(dve, s_exp, f - 1)
                V.tensor_reduce(nmax[:, p % 2, :].rearrange("p (h b) -> p h b", h=2),
                                ps[:, SB:SB + 2, 0:GT].rearrange("p h (b l) -> p h b l", b=GB),
                                AX.X, ALU.max, negate=True).then_inc(s_max, 1)

            def normalise(g, i):
                s = stage(g, i, O_LAG, NPAIR)
                if s is None:
                    return
                grp, p = s
                f = NPAIR * grp + p
                dve.wait_ge(o_mm, f + 1)
                wait(dve, u_mm, f - 1)
                o = bank(OB)[:, 0:4 * (DCTX + 1)].rearrange("p (k d) -> p k d", k=4)
                V.reciprocal(rsum[:, p % 2, :], o[:, :, DCTX]).then_inc(norm_r, 1)
                dve.wait_ge(norm_r, f + 1)
                for h in range(2):
                    last = V.tensor_tensor(ctxh[:, p % 2, :, 64 * h:64 * h + 64], o[:, 2 * h:2 * h + 2, 0:DCTX],
                                           rsum[:, p % 2, 2 * h:2 * h + 2].unsqueeze(2)
                                           .to_broadcast([P, GB, DCTX]), ALU.mult)
                last.then_inc(o_out, 1)

            def close_group(g, i):
                s = stage(g, 0, 1, NPAIR)
                if s is None or i != Y_AT:
                    return
                grp = s[0]
                dve.wait_ge(y_mm, grp + 1)
                xg = x[:, bass.ds(grp * GB, GB), :]
                V.tensor_tensor(xg, xg, bank(MB).rearrange("p (b d) -> p b d", b=GB), ALU.add).then_inc(y_add, 1)
                wait_apart(dve, y_add, grp + 1)
                layernorm(grp, 1)

            def layernorm(grp, phase):
                for b in range(GB):
                    last = V.bn_stats(st6[:, b, :], x[:, bass.ds(grp * GB + b, 1), :].rearrange("p a d -> p (a d)"))
                last.then_inc(ln_a, 1)
                wait_apart(dve, ln_a, grp + 1)
                for b in range(GB):
                    last = V.bn_aggr(mv[:, b, :], st6[:, b, :])
                last.then_inc(l_stats, 1)
                dve.wait_ge(l_rstd, grp + 1)
                for b in range(GB):
                    last = V.tensor_scalar(xn2[:, b, :], x[:, bass.ds(grp * GB + b, 1), :]
                                           .rearrange("p a d -> p (a d)"), mv[:, b, 0:1], rstd[:, b:b + 1],
                                           ALU.subtract, ALU.mult)
                last.then_inc(l_xn, 1)

            def body(g, i):
                rope(g, i, 0)
                row_max(g, i)
                rope(g, i, 1)
                normalise(g, i)
                close_group(g, i)

            pipeline(dve, NG, NPAIR, body)
            barrier(dve, 2)

            dve.wait_ge(ld_2, 64)
            step(V.tensor_reduce(lmax, logits[:], AX.X, ALU.max))
            V.tensor_tensor(expl, logits[:], lmax.unsqueeze(2).to_broadcast([P, NB, NE]),
                            ALU.subtract).then_inc(gate_max, 1)
            dve.wait_ge(gate_exp, 1)
            every = [P, NB, NE, NE]
            mine = expl.unsqueeze(3).to_broadcast(every)
            other = expl.unsqueeze(2).to_broadcast(every)
            V.tensor_tensor(above, other, mine, ALU.is_gt)
            step(V.tensor_tensor(tied, other, mine, ALU.is_equal))
            step(V.tensor_tensor(tied, tied, before.unsqueeze(1).to_broadcast(every), ALU.mult))
            step(V.tensor_tensor(above, above, tied, ALU.add))
            step(V.tensor_reduce(rank, above, AX.X, ALU.add))
            step(V.tensor_scalar(rank, rank, TOPK - 0.5, None, ALU.is_lt))
            step(V.tensor_tensor(rank, rank, expl, ALU.mult))
            step(V.tensor_reduce(lmax, rank, AX.X, ALU.add))
            step(V.reciprocal(lmax, lmax))
            step(V.tensor_tensor(rank, rank, lmax.unsqueeze(2).to_broadcast([P, NB, NE]), ALU.mult))
            V.tensor_tensor(comb, rank, alpha.unsqueeze(1).to_broadcast([P, NB, NE]), ALU.mult)\
                .then_inc(comb_ready, 1)
            dve.wait_ge(comb_ready, 1)

            def group_comb(g, i):
                s = stage(g, i, 0, STEPS2, NG2)
                if s is None or i != 1:
                    return
                grp = s[0]
                wait(dve, h_mm, (NE + 1) * grp)
                wait(dve, f_acc, (NE + 1) * grp)
                V.tensor_copy(combg, comb[:, bass.ds(grp * GB2, GB2), :]).then_inc(f_cp, 1)

            def accumulate(g, i):
                s = stage(g, i, 1, STEPS2, NG2)
                if s is None or s[1] > BIAS_AT:
                    return
                grp, e = s
                n = (NE + 1) * grp + e
                dve.wait_ge(f_mm, n + 1)
                wait(dve, f_acc, n)
                if e == 0:
                    dve.wait_ge(f_cp, grp + 1)
                for b in range(GB2):
                    xb = x[:, bass.ds(grp * GB2 + b, 1), :].rearrange("p a d -> p (a d)")
                    y = bank(4 + 2 * (e % 2) + b // 2)[:, (b % 2) * D:(b % 2 + 1) * D]
                    if e == BIAS_AT:
                        last = V.tensor_tensor(xb, xb, y, ALU.add)
                    else:
                        last = V.scalar_tensor_tensor(xb, y, combg[:, b, e:e + 1], xb, ALU.mult, ALU.add)
                last.then_inc(f_acc, 1)

            def layernorm2(g, i):
                s = stage(g, 0, 1, STEPS2, NG2)
                if s is None or i != 1:
                    return
                grp = s[0]
                wait_apart(dve, f_acc, (NE + 1) * (grp + 1))
                for b in range(GB2):
                    last = V.bn_stats(st6[:, b, :], x[:, bass.ds(grp * GB2 + b, 1), :].rearrange("p a d -> p (a d)"))
                last.then_inc(n_a, 1)
                wait_apart(dve, n_a, grp + 1)
                for b in range(GB2):
                    last = V.bn_aggr(mv[:, b, :], st6[:, b, :])
                last.then_inc(n_stats, 1)
                dve.wait_ge(n_rstd, grp + 1)
                for b in range(GB2):
                    last = V.tensor_scalar(xn4[:, b, :], x[:, bass.ds(grp * GB2 + b, 1), :]
                                           .rearrange("p a d -> p (a d)"), mv[:, b, 0:1], rstd[:, b:b + 1],
                                           ALU.subtract, ALU.mult)
                last.then_inc(n_xn, 1)

            for j in range(2):
                last = V.memset(wgu_n[LAST_ROWS:P, NF * j + NF - 1, :], 1.0)
            last.then_inc(pad_set, 1)

            def quantise_weights(q, part):
                k, w = (slice(3 * q, 3 * q + 3), wgu_n[:, 3 * q:3 * q + 3, :]) if q < 4 else \
                    (slice(2 * NF + q - 4, 2 * NF + q - 3), wd_n[:, q - 4:q - 3, :])
                rows, width = w.shape[1], w.shape[2]
                m = wm[:, 0:rows * width].rearrange("p (k d) -> p k d", k=rows)
                if part == 0:
                    step(V.tensor_reduce(ws[:, k], w, AX.X, ALU.max, apply_absolute_value=True))
                    step(V.tensor_scalar(ws[:, k], ws[:, k], 1.0 / FP8_MAX, None, ALU.mult))
                    step(V.reciprocal(wr[:, k], ws[:, k]))
                    step(V.tensor_tensor(w, w, wr[:, k].unsqueeze(2).to_broadcast([P, rows, width]), ALU.mult))
                elif part == 1:
                    step(V.tensor_scalar(m.bitcast(U32), w.bitcast(U32), SIGN_EXP, None, ALU.bitwise_and))
                    step(V.tensor_scalar(m, m, 2.0 ** -6, ROUND_FP8, ALU.max, ALU.mult))
                    step(V.tensor_tensor(w, w, m, ALU.add))
                else:
                    step(V.tensor_tensor(w, w, m, ALU.subtract))
                    last = V.tensor_tensor(w, w, ws[:, k].unsqueeze(2).to_broadcast([P, rows, width]), ALU.mult)
                    if q == 5:
                        last.then_inc(w4_quant, 1)

            def weights(g, i):
                if not isinstance(g, int) or g > 0 or i == 0:
                    return
                if i == 1:
                    dve.wait_ge(ld_g, 16 * 2 * NF)
                    dve.wait_ge(ld_d, 16)
                    dve.wait_ge(pad_set, 1)
                for n in (2 * (i - 1), 2 * i - 1):
                    quantise_weights(n // 3, n % 3)

            def body2(g, i):
                group_comb(g, i)
                layernorm2(g, i)
                accumulate(g, i)
                weights(g, i)

            pipeline(dve, NG2, STEPS2, body2)
            barrier(dve, 3)

            V.memset(vaug, 1.0)
            step(V.memset(wqm, 0.0))
            dve.wait_ge(ld_3, 48)
            for c in range(DC):
                for ct in range(DC):
                    for e in range(2):
                        pick = wqm[:, c, ct, e, :].rearrange("p (w e d) -> p w e d", w=4, e=2)[:, :, e, :]
                        src = wq1[:, c, ct * P:(ct + 1) * P].rearrange("p (w e d) -> p w e d", w=4, e=2)[:, :, e, :]
                        last = V.tensor_scalar(pick, src, float(HD1) ** -0.5, None, ALU.mult)
            last.then_inc(w3_ready, 1)

            def row_max3(g, i):
                s = stage(g, i, S3, STEPS3, NG3)
                if s is None:
                    return
                grp, k = s
                f = STEPS3 * grp + k
                dve.wait_ge(s3_mm, f + 1)
                wait(dve, s3_exp, f - 3)
                V.tensor_reduce(nmax3[:, k % 4, :], bank(k % 4).rearrange("p (o l) -> p o l", o=4),
                                AX.X, ALU.max, negate=True).then_inc(s3_max, 1)

            def probs_out3(g, i):
                s = stage(g, i, T3, STEPS3, NG3)
                if s is None:
                    return
                grp, k = s
                f = STEPS3 * grp + k
                dve.wait_ge(t3_mm, f + 1)
                wait(dve, o3_mm, f - 1)
                V.tensor_copy(probT3[:, k % 2].rearrange("p o t -> p (o t)"), bank(4)).then_inc(t3_out, 1)

            def normalise3(g, i):
                s = stage(g, i, O3, STEPS3, NG3)
                if s is None or s[1] % 4 != 3:
                    return
                b = 4 * s[0] + s[1] // 4
                dve.wait_ge(o3_mm, 4 * (b + 1))
                wait(dve, u3_mm, b)
                o = bank(5)[:, 0:H1 * V1].rearrange("p (h d) -> p h d", h=H1)
                V.reciprocal(rsum3, o[:, :, HD1]).then_inc(o3_r, 1)
                dve.wait_ge(o3_r, b + 1)
                V.tensor_tensor(ctx3.rearrange("p (h d) -> p h d", h=H1), o[:, :, 0:HD1],
                                rsum3.unsqueeze(2).to_broadcast([P, H1, HD1]), ALU.mult).then_inc(o3_out, 1)

            def add3(g, i):
                s = stage(g, i, Y3, STEPS3, NG3)
                if s is None or s[1] % 4 != 3:
                    return
                b = 4 * s[0] + s[1] // 4
                dve.wait_ge(y3_mm, b + 1)
                xb = x[:, bass.ds(b, 1), :].rearrange("p a d -> p (a d)")
                V.tensor_tensor(xb, xb, bank(7)[:, D:2 * D], ALU.add).then_inc(y3_add, 1)

            def weights_lo(g, i):
                if not isinstance(g, int) or g > 0 or i >= W_TURNS:
                    return
                dve.wait_ge(w4_hi, i + 1)
                hi, lo, src = turned(i)
                if i == W_TURNS - 1:
                    V.tensor_tensor(lo, src, hi.bitcast(F32), ALU.subtract)
                    hi, lo, src = last_turn
                V.tensor_tensor(lo, src, hi.bitcast(F32), ALU.subtract).then_inc(w4_lo, 1)

            def quantise_x(g, i):
                for part in range(4):
                    s = stage(g, i, Y3 + part, STEPS3, NG3)
                    if s is None or s[1] % 4 != 3:
                        continue
                    b = 4 * s[0] + s[1] // 4

                    def link(ins, nth, then=dve.wait_ge):
                        ins.then_inc(x5, 1)
                        then(x5, 9 * b + nth)

                    xb = x[:, bass.ds(b, 1), :].rearrange("p a d -> p (a d)")
                    if part == 0:
                        wait_apart(dve, y3_add, b + 1)
                        link(V.bn_stats(st5, xb), 1, lambda sm, v: wait_apart(dve, sm, v))
                        V.bn_aggr(mv5, st5).then_inc(x5_stats, 1)
                    if part == 1:
                        dve.wait_ge(x5_rstd, b + 1)
                        link(V.tensor_scalar(xn5, xb, mv5[:, 0:1], ve5[:, 1:2], ALU.subtract, ALU.mult), 2)
                        link(V.tensor_reduce(s5[:, 0:1], xn5, AX.X, ALU.max, apply_absolute_value=True), 3)
                    if part == 2:
                        link(V.tensor_scalar(s5[:, 0:1], s5[:, 0:1], 1.0 / FP8_MAX, None, ALU.mult), 4)
                        link(V.reciprocal(s5[:, 1:2], s5[:, 0:1]), 5)
                        link(V.tensor_scalar(xn5, xn5, s5[:, 1:2], None, ALU.mult), 6)
                        link(V.tensor_scalar(m5.bitcast(U32), xn5.bitcast(U32), SIGN_EXP, None, ALU.bitwise_and), 7)
                    if part == 3:
                        link(V.tensor_scalar(m5, m5, 2.0 ** -6, ROUND_FP8, ALU.max, ALU.mult), 8)
                        link(V.tensor_tensor(xn5, xn5, m5, ALU.add), 9)
                        V.tensor_tensor(qx_all[:, bass.ds(b, 1), :].rearrange("p a d -> p (a d)"), xn5, m5,
                                        ALU.subtract)
                        V.tensor_copy(sx_all[:, bass.ds(b, 1)], s5[:, 0:1])

            def body3(g, i):
                row_max3(g, i)
                weights_lo(g, i)
                normalise3(g, i)
                probs_out3(g, i)
                add3(g, i)
                quantise_x(g, i)

            pipeline(dve, NG3, STEPS3, body3)
            barrier(dve, 4)

            def seq_of(g, i, lag):
                s = stage(g, i, lag, STEPS4, NG4)
                return None if s is None else (STEPS4 * s[0] + s[1], s[1])

            def product(g, i, piece):
                s = seq_of(g, i, GU4)
                if s is None:
                    return
                f, k = s
                if piece == 0:
                    dve.wait_ge(up_mm, f + 1)
                    dve.wait_ge(silu_out, f + 1)
                    wait(dve, t_scaled, f)
                    V.scalar_tensor_tensor(tt.rearrange("p (k n) -> p k n", k=2), ps[:, 2:4, 0:FF // 2],
                                           sxg[:, k:k + 1], tsl.rearrange("p (k n) -> p k n", k=2),
                                           ALU.mult, ALU.mult).then_inc(t_prod, 1)
                if piece == 1:
                    dve.wait_ge(t_prod, f + 1)
                    V.tensor_reduce(st[:, k, 0:1], tt, AX.X, ALU.max, apply_absolute_value=True).then_inc(t_max, 1)
                if piece == 2:
                    dve.wait_ge(t_max, f + 1)
                    V.tensor_scalar(st[:, k, 0:1], st[:, k, 0:1], 1.0 / FP8_MAX, None, ALU.mult).then_inc(t_scale, 1)
                    dve.wait_ge(t_scale, f + 1)
                    V.reciprocal(st[:, k, 1:2], st[:, k, 0:1]).then_inc(t_recip, 1)

            def quantise_t(g, i, piece):
                s = seq_of(g, i, Q4)
                if s is None:
                    return
                f, k = s
                v = tv[:, k % 2, :]
                if piece == 0:
                    dve.wait_ge(t_scaled, f + 1)
                    wait(dve, t5_q, f)
                    V.tensor_scalar(tm.bitcast(U32), v.bitcast(U32), SIGN_EXP, None,
                                    ALU.bitwise_and).then_inc(t_expo, 1)
                if piece == 1:
                    dve.wait_ge(t_expo, f + 1)
                    V.tensor_scalar(tm, tm, 2.0 ** -6, ROUND_FP8, ALU.max, ALU.mult).then_inc(t_magic, 1)
                if piece == 2:
                    dve.wait_ge(t_magic, f + 1)
                    V.tensor_tensor(v, v, tm, ALU.add).then_inc(t_sum, 1)
                if piece == 3:
                    dve.wait_ge(t_sum, f + 1)
                    wait(dve, t5_mm, f - 1)
                    V.tensor_tensor(qt[:, k % 2, :], v, tm, ALU.subtract).then_inc(t5_q, 1)

            def add_ffn(g, i):
                s = seq_of(g, i, Y4)
                if s is None:
                    return
                f, k = s
                xb = x[:, bass.ds(f, 1), :].rearrange("p a d -> p (a d)")
                dve.wait_ge(y5_mm, f + 1)
                V.scalar_tensor_tensor(xb, bank(6)[:, 0:D], st[:, k, 0:1], xb, ALU.mult, ALU.add)\
                    .then_inc(x5_done, 1)

            def group_scales(g, i):
                s = stage(g, i, 0, STEPS4, NG4)
                if s is None or s[1] != 0:
                    return
                wait(dve, t_prod, STEPS4 * s[0])
                V.tensor_copy(sxg, sx_all[:, bass.ds(STEPS4 * s[0], STEPS4)]).then_inc(sxg_ready, 1)
                dve.wait_ge(sxg_ready, s[0] + 1)

            def body4(g, i):
                quantise_t(g, i, 0)
                quantise_t(g, i, 1)
                product(g, i, 0)
                group_scales(g, i)
                product(g, i, 1)
                quantise_t(g, i, 2)
                product(g, i, 2)
                quantise_t(g, i, 3)
                add_ffn(g, i)

            pipeline(dve, NG4, STEPS4, body4)

        @block.gpsimd
        def _(pool):
            G = nc.gpsimd
            pool.wait_ge(ln_stats, 1)
            G.tensor_tensor(rstd[:], veps[:], mhalf[:], ALU.pow).then_inc(ln_rstd, 1)
            barrier(pool, 1)

            def add_rope(g, i, h):
                s = stage(g, i, 0, NPAIR)
                if s is None:
                    return
                grp, p = s
                f = NPAIR * grp + p
                pool.wait_ge(q_scaled, 2 * f + h + 1)
                wait(pool, b_mm, f - 1)
                for half in range(2):
                    lo, other = half * GT, (1 - half) * GT
                    last = G.tensor_tensor(roped[:, p % 2, h, lo:lo + GT], t1[:, h, lo:lo + GT],
                                           t2[:, h, other:other + GT], ALU.add)
                last.then_inc(q_roped, 1)

            def rsqrt_var(g, i):
                s = stage(g, 0, 1, NPAIR)
                if s is None or i != Y_AT:
                    return
                grp = s[0]
                wait(pool, l_stats, grp + 1)
                G.tensor_tensor(veps[:, 0:GB], mv[:, 0:GB, 1], epst[:, 0:GB], ALU.add).then_inc(pool_step, 1)
                pool.wait_ge(pool_step, grp + 1)
                G.tensor_tensor(rstd[:, 0:GB], veps[:, 0:GB], mhalf[:, 0:GB], ALU.pow).then_inc(l_rstd, 1)

            def body(g, i):
                add_rope(g, i, 0)
                rsqrt_var(g, i)
                add_rope(g, i, 1)

            pipeline(pool, NG, NPAIR, body)
            barrier(pool, 2)

            def rsqrt2(g, i):
                s = stage(g, 0, 1, STEPS2, NG2)
                if s is None or i != 1:
                    return
                grp = s[0]
                wait(pool, n_stats, grp + 1)
                G.tensor_tensor(veps[:, 0:GB2], mv[:, 0:GB2, 1], epst[:, 0:GB2], ALU.add).then_inc(n_eps, 1)
                pool.wait_ge(n_eps, grp + 1)
                G.tensor_tensor(rstd[:, 0:GB2], veps[:, 0:GB2], mhalf[:, 0:GB2], ALU.pow).then_inc(n_rstd, 1)

            pool.wait_ge(ld_i, 32)
            for j, name in enumerate(("L1_ffn_w_gate", "L1_ffn_w_up")):
                for k, (at, n) in enumerate(FCH):
                    ix = idx_a[:, k:k + 1] if k < NF - 1 else idx_b[:]
                    if k == NF - 1:
                        pool.wait_ge(pad_set, 1)
                    G.indirect_dma_start(
                        out=wgu_n[0:n, NF * j + k, :], out_offset=None, in_=a[name],
                        in_offset=bass.IndirectOffsetOnAxis(ap=ix.bitcast(U32), axis=0)).then_inc(ld_g, 16)

            pipeline(pool, NG2, STEPS2, rsqrt2)
            barrier(pool, 3)

            def rsqrt_x(g, i):
                s = stage(g, i, Y3, STEPS3, NG3)
                if s is None or s[1] % 4 != 3:
                    return
                b = 4 * s[0] + s[1] // 4
                pool.wait_ge(x5_stats, b + 1)
                G.tensor_tensor(ve5[:, 0:1], mv5[:, 1:2], epst[:, 0:1], ALU.add).then_inc(x5_eps, 1)
                pool.wait_ge(x5_eps, b + 1)
                G.tensor_tensor(ve5[:, 1:2], ve5[:, 0:1], mhalf[:, 0:1], ALU.pow).then_inc(x5_rstd, 1)

            pipeline(pool, NG3, STEPS3, rsqrt_x)
            barrier(pool, 4)


def rope_tables(length, dim):
    f32 = np.float32
    inv = (f32(1.0) / np.power(f32(10000.0), np.arange(0, dim, 2, dtype=f32) / f32(dim))).astype(f32)
    f = np.arange(length, dtype=f32)[:, None] * inv[None, :]
    return np.repeat(np.sin(f), 2, axis=-1), np.repeat(np.cos(f), 2, axis=-1)


def kernel(**inputs):
    import ml_dtypes
    import concourse.bacc as _bacc
    from concourse.bass_utils import run_bass_kernel_spmd as _run

    w = {k: np.asarray(v) for k, v in inputs.items()}
    c = np.ascontiguousarray

    def chunks(m):
        return c(m.reshape(-1, P, m.shape[-1]).transpose(1, 0, 2))

    arr = {"x": c(w["x"].transpose(1, 0, 2)), "ctx": c(w["ctx_512"].transpose(1, 0, 2)),
           "ctxT": c(w["ctx_512"].reshape(NB * P, DCTX).T)}
    arr["L0_xattn_Wq"] = c(w["L0_xattn_Wq"].reshape(H0, K0, D).transpose(1, 0, 2))
    arr["L0_xattn_w_kc_q"] = c(w["L0_xattn_w_kc_q"].transpose(1, 0, 2))
    arr["L0_xattn_w_kc_kv"] = c(w["L0_xattn_w_kc_kv"].transpose(1, 0, 2))
    arr["L0_xattn_W_qr"] = c(w["L0_xattn_W_qr"].transpose(2, 0, 1))
    arr["L0_xattn_W_kr"] = c(w["L0_xattn_W_kr"].transpose(2, 0, 1))
    arr["L0_xattn_Wo"] = c(w["L0_xattn_Wo"].reshape(D, H0, K0).transpose(2, 1, 0))
    arr["L0_ffn_gate_w"] = chunks(w["L0_ffn_gate_w"])
    arr["L0_ffn_fc1_w"] = c(w["L0_ffn_fc1_w"].reshape(NE, DC, P, INTER).transpose(2, 0, 1, 3))
    arr["L0_ffn_fc2_w"] = c(w["L0_ffn_fc2_w"].reshape(NE, IC, P, D).transpose(2, 0, 1, 3))

    arr["L0_ffn_fc1_b"] = c(w["L0_ffn_fc1_b"].reshape(NE, IC, P).transpose(2, 0, 1))
    arr["L0_ffn_fc2_b"] = c(w["L0_ffn_fc2_b"])
    arr["L0_ffn_alpha"] = c(np.broadcast_to(w["L0_ffn_alpha"], (P, NE)))
    arr["L1_xattn_Wq"] = chunks(w["L1_xattn_Wq"].T)
    arr["L1_xattn_Wkv"] = c(w["L1_xattn_Wkv_expand"].T)
    arr["L1_xattn_Wout"] = chunks(w["L1_xattn_Wout"].T)
    arr["L1_ffn_w_gate"], arr["L1_ffn_w_up"] = c(w["L1_ffn_w_gate"]), c(w["L1_ffn_w_up"])
    arr["L1_ffn_w_down"] = chunks(w["L1_ffn_w_down"])
    di = w["L1_ffn_down_reorder_index"]
    whole = FF // P * P
    arr["idx_a"] = c(di[:whole].reshape(-1, P).T)
    arr["idx_b"] = c(di[whole:].reshape(-1, 1))
    arr["before"] = c(np.broadcast_to(np.tril(np.ones((NE, NE), np.float32), -1), (P, NE, NE)))

    sq, cq = rope_tables(P, DQ0)
    sk, ck = rope_tables(P, DCTX)
    two = (HALF, 2, GB, P)
    arr["rope_c"] = c(np.broadcast_to(cq.T.reshape(2, HALF, P).transpose(1, 0, 2)[:, :, None, :], two))
    ssw = np.stack([sq.T[HALF:], -sq.T[:HALF]], axis=1)
    arr["rope_s"] = c(np.broadcast_to(ssw[:, :, None, :], two))
    arr["ropek_c"] = c(ck)
    arr["ropek_s"] = c(np.concatenate([-sk[:, :DCTX // 2], sk[:, DCTX // 2:]], axis=1))
    arr["ident"] = np.eye(P, dtype=np.float32)
    arr["identb"] = np.eye(P).astype(ml_dtypes.bfloat16)
    causal = np.tril(np.ones((P, P), bool))
    arr["mask"] = c(np.broadcast_to(np.where(causal, 0.0, MASKED)[:, None, :], (P, 4, P)).astype(ml_dtypes.bfloat16))

    nc = _bacc.Bacc("TRN2", target_bir_lowering=False, num_devices=1)
    aps = {k: nc.dram_tensor(f"in_{k}", v.shape, mybir.dt.from_np(v.dtype), kind="ExternalInput").ap()
           for k, v in arr.items()}
    out = nc.dram_tensor("out_x", (P, NB, D), F32, kind="ExternalOutput").ap()
    build(nc, aps, out)
    r = _run(nc, [{f"in_{k}": v for k, v in arr.items()}], core_ids=[0])
    return c(r.results[0]["out_x"].transpose(1, 0, 2))
```

```python
from contextlib import ExitStack

import numpy as np

import concourse.bass as bass
from concourse import mybir

ALU = mybir.AluOpType
ACT = mybir.ActivationFunctionType
AX = mybir.AxisListType
F32 = mybir.dt.float32
BF16 = mybir.dt.bfloat16
U32 = mybir.dt.uint32
F32R = mybir.dt.float32r

P = 128
NB = 16
D = 256
DC = D // P
DCTX = 64
H0, K0, DQ0, R0 = 16, 128, 192, 64
HALF = DQ0 // 2
NPAIR = H0 // 2
NE, TOPK = 8, 2
INTER = 256
IC = INTER // P
H1, HD1 = 16, 16
V1 = HD1 + 1
FF = 704
FCH = [(c * P, min(P, FF - c * P)) for c in range(-(-FF // P))]
FP8_MAX = 448.0
LN_EPS = 1e-5
MASKED = -3.0e38
QUERY_SCALE = float(HD1) ** -0.5

GB = 2
GT = GB * P
NG = NB // GB
GB2 = 4
T2 = GB2 * P
NG2 = NB // GB2
SIGN_EXP = 0x7F800000
ROUND_FP8 = 1.5 * 2.0 ** 20


def build(nc, a, out):
    with ExitStack() as ctx:
        def sb(name, shape, dt=F32):
            return ctx.enter_context(nc.sbuf_tensor(name, shape, dt))

        def sem(name):
            return ctx.enter_context(nc.semaphore(name))

        x = sb("x", [P, NB, D])
        xn_hi = sb("xn_hi", [P, DC, NB * P], F32R)
        xn_lo = sb("xn_lo", [P, DC, NB * P], F32R)
        ident = sb("ident", [P, P])
        identb = sb("identb", [P, P], BF16)
        mask = sb("mask", [P, 4, P], BF16)
        mv = sb("mv", [P, NB, 2])
        st6 = sb("st6", [P, NB, 6])
        rstd = sb("rstd", [P, NB])
        unread = sb("unread", [P, 1])
        unread_act = sb("unread_act", [P, 1])
        unread_pool = sb("unread_pool", [P, 1])
        epst = sb("epst", [P, NB])
        veps = sb("veps", [P, NB])
        mhalf = sb("mhalf", [P, NB])
        logits = sb("logits", [P, NB, NE])

        gatew = sb("gatew", [P, DC, NE])
        ropek_c = sb("ropek_c", [P, DCTX])
        ropek_s = sb("ropek_s", [P, DCTX])
        NF = len(FCH)
        idx_a = sb("idx_a", [P, NF - 1], mybir.dt.int32)
        idx_b = sb("idx_b", [FCH[-1][1], 1], mybir.dt.int32)
        arena = sb("arena", [P, 19232])
        with ExitStack() as first:
            def sb1(name, shape, dt=F32):
                return first.enter_context(nc.sbuf_tensor(name, shape, dt))

            wc_hi = sb1("wc_hi", [P, DC, H0, DQ0], F32R)
            wc_lo = sb1("wc_lo", [P, DC, H0, DQ0], F32R)
            wqk = sb1("wqk", [HALF, H0, 2, R0])
            wvo = sb1("wvo", [P, NPAIR, D])
            kvT = sb1("kvT", [P, NB * P])
            kv = sb1("kv", [P, NB, DCTX])
            kvg = sb1("kvg", [P, GB, DCTX])
            rope_c = sb1("rope_c", [HALF, 2, GB, P])
            rope_s = sb1("rope_s", [HALF, 2, GB, P])
        with ExitStack() as second:
            def sb2(name, shape):
                return second.enter_context(nc.sbuf_tensor(name, shape, F32R))

            fc1_hi, fc1_lo = sb2("fc1_hi", [P, NE, DC, INTER]), sb2("fc1_lo", [P, NE, DC, INTER])
            fc2_hi, fc2_lo = sb2("fc2_hi", [P, NE, IC, D]), sb2("fc2_lo", [P, NE, IC, D])
            hT_hi, hT_lo = sb2("hT_hi", [P, 2, IC, T2]), sb2("hT_lo", [P, 2, IC, T2])
        wgu_hi = sb("wgu_hi", [P, DC, 2 * FF], F32R)
        wgu_lo = sb("wgu_lo", [P, DC, 2 * FF], F32R)
        wd_hi = sb("wd_hi", [P, NF, D], F32R)
        wd_lo = sb("wd_lo", [P, NF, D], F32R)
        wqm_hi = sb("wqm_hi", [P, DC, DC, 2, P], F32R)
        wqm_lo = sb("wqm_lo", [P, DC, DC, 2, P], F32R)
        qxT = sb("qxT", [P, 2, DC, P], F32R)
        qtT = sb("qtT", [P, NF, P], F32R)
        late = sb("late", [P, 6184])

        def carve(region, at, parts, shape, dt=F32):
            n = int(np.prod(shape))
            if dt == BF16:
                v = region[0:parts, at:at + (n + 1) // 2].bitcast(BF16)
                v = v[:, 0:n]
            else:
                v = region[0:parts, at:at + n]
            names = "abcd"[:len(shape)]
            if len(shape) > 1:
                v = v.rearrange(f"p ({' '.join(names)}) -> p {' '.join(names)}",
                                **{k: s for k, s in zip(names[1:], shape[1:])})
            return v

        raw = arena
        r_wq = carve(raw, 0, P, [H0, D])
        r_wkcq = carve(raw, 4096, P, [H0, DQ0])
        r_wqrT = carve(raw, 7168, P, [NPAIR, DQ0])
        r_wkrT = carve(raw, 8704, P, [NPAIR, DCTX])
        r_wkckv = carve(raw, 9216, P, [H0, DCTX])
        r_woT = carve(raw, 10240, P, [H0, D])
        xn_all = carve(raw, 14336, P, [NB // 2, D])
        kvd = carve(raw, 16384, P, [NB, 2, DCTX])
        t1 = carve(raw, 8192, HALF, [2, 512])
        t2 = carve(raw, 9216, HALF, [2, 512])
        roped = carve(raw, 10240, HALF, [2, 2, 512])
        qT = carve(raw, 12288, P, [2, GT])
        kvTg = carve(raw, 12800, P, [GT])
        prob = carve(raw, 13056, P, [4, 4, P])
        probT = carve(raw, 15104, P, [2, 4, P])
        nmax = carve(raw, 16128, P, [2, 4])
        rsum = carve(raw, 16136, P, [2, 4])
        rinv = carve(raw, 16144, P, [2, 4])
        xn2 = carve(raw, 16160, P, [GB, D])
        ctxhT = carve(raw, 16672, P, [NPAIR, GT])
        xgT = carve(raw, 18720, P, [DC, GT])
        fc1 = carve(raw, 0, P, [NE, DC, INTER])
        fc2 = carve(raw, 4096, P, [NE, IC, D])

        hT = carve(raw, 8448, P, [IC, T2])
        xn4 = carve(raw, 9472, P, [GB2, D])
        combT = carve(raw, 10496, NE, [T2])
        combg = carve(raw, 11008, P, [GB2, NE])
        expl = carve(raw, 11040, P, [NB, NE])
        above = carve(raw, 11168, P, [NB, NE, NE])
        tied = carve(raw, 12192, P, [NB, NE, NE])
        rank = carve(raw, 13216, P, [NB, NE])
        lmax = carve(raw, 13344, P, [NB])
        comb = carve(raw, 13360, P, [NB, NE])
        before = carve(raw, 13488, P, [NE, NE])
        alpha = carve(raw, 13552, P, [NE])
        fc1b = carve(raw, 13560, P, [NE, IC])
        fc2b = carve(raw, 13576, NE, [D])
        wkv1 = carve(raw, 0, DCTX, [2 * D])
        wout1 = carve(raw, 512, P, [DC, D])
        wqm = carve(raw, 1024, P, [DC, DC, 2, P])
        ctxT = carve(raw, 2048, DCTX, [NB * P])
        vaug = carve(raw, 4096, P, [NB, H1, V1])
        q3 = carve(raw, 8448, P, [2, 2, DC, GT])
        k3 = carve(raw, 10496, P, [2, DC, GT])
        probT3 = carve(raw, 11520, P, [2, 4, P])
        ctx3 = carve(raw, 12544, P, [D])
        ctx3T = carve(raw, 12800, P, [DC, P])
        nmax3 = carve(raw, 13056, P, [4, 4])
        rsum3 = carve(raw, 13072, P, [H1])
        prob3 = carve(late, 2600, P, [4, 4, P])
        vseq = carve(late, 4648, P, [2, H1, 32])
        mixed = carve(late, 5672, P, [4, P])
        qx_all = carve(late, 0, P, [NB, D], BF16)
        xn5 = carve(late, 2048, P, [D])
        m5 = carve(late, 2304, P, [D])
        sx_all = carve(late, 2560, P, [NB])
        st5 = carve(late, 2576, P, [6])
        mv5 = carve(late, 2582, P, [2])
        ve5 = carve(late, 2584, P, [2])
        s5 = carve(late, 2586, P, [2])
        wgu_n = carve(raw, 13956, P, [2 * NF, D])
        wd_n = carve(raw, 17028, P, [DC, FF])
        wm = carve(raw, 18436, P, [3 * D])
        ws = carve(raw, 19204, P, [2 * NF + DC])
        wr = carve(raw, 19218, P, [2 * NF + DC])
        tsl = carve(raw, 0, P, [FF])
        tt = carve(raw, 704, P, [FF])
        tv = carve(raw, 1408, P, [2, FF])
        tm = carve(raw, 2816, P, [FF])
        qt = carve(raw, 3520, P, [2, FF], BF16)
        sxg = carve(raw, 4224, P, [4])
        st = carve(raw, 4228, P, [4, 2])

        ps = ctx.enter_context(nc.psum_tensor("ps", [P, 8, 512], F32))

        def bank(i):
            return ps[:, i, :]

        def bank16(i):
            return ps[:, i, :].bitcast(BF16)

        ld_x, ld_w, ld_wb, ld_c = sem("ld_x"), sem("ld_w"), sem("ld_wb"), sem("ld_c")
        ld_f1 = sem("ld_f1")
        phase_end = sem("phase_end")
        stored = sem("stored")
        dve_step = sem("dve_step")
        pool_step = sem("pool_step")
        ln_stats, ln_rstd = sem("ln_stats"), sem("ln_rstd")
        kv_ready = sem("kv_ready")
        xn_ready = sem("xn_ready")
        norm_r, ln_a = sem("norm_r"), sem("ln_a")
        prep_mm, prep_hi, prep_lo, prep_whole = sem("prep_mm"), sem("prep_hi"), sem("prep_lo"), sem("prep_whole")
        ld_xb = sem("ld_xb")
        kv_step, kvg_copied, p_norm = sem("kv_step"), sem("kvg_copied"), sem("p_norm")
        ld_ctx, ld_w2, l_lo = sem("ld_ctx"), sem("ld_w2"), sem("l_lo")
        h_hi, fc_hi1, fc_lo1 = sem("h_hi"), sem("fc_hi1"), sem("fc_lo1")
        fc_hi, fc_lo, h_lo, n_hi, wqm_split = (sem("fc_hi"), sem("fc_lo"), sem("h_lo"), sem("n_hi"), sem("wqm_split"))
        q_mm, q_scaled, q_roped = sem("q_mm"), sem("q_scaled"), sem("q_roped")
        b_mm, b_out = sem("b_mm"), sem("b_out")
        kv_copied = sem("kv_copied")
        s_mm, s_max, s_exp = sem("s_mm"), sem("s_max"), sem("s_exp")
        t_mm, t_out = sem("t_mm"), sem("t_out")
        o_mm, o_out = sem("o_mm"), sem("o_out")
        y_mm, y_add = sem("y_mm"), sem("y_add")
        l_stats, l_rstd, l_xn, l_mm, l_out = (sem("l_stats"), sem("l_rstd"), sem("l_xn"), sem("l_mm"),
                                              sem("l_out"))
        g_mm, g_out = sem("g_mm"), sem("g_out")

        ld_2, ld_3, ld_i = sem("ld_2"), sem("ld_3"), sem("ld_i")
        ld_g = [sem(f"ld_g{q}") for q in range(4)]
        ld_d = sem("ld_d")
        gate_exp, gate_max, comb_ready = sem("gate_exp"), sem("gate_max"), sem("comb_ready")
        h_mm, h_out, f_mm, f_acc, f_cp = sem("h_mm"), sem("h_out"), sem("f_mm"), sem("f_acc"), sem("f_cp")
        n_a, n_stats, n_eps, n_rstd, n_xn, n_mm, n_out = (sem("n_a"), sem("n_stats"), sem("n_eps"), sem("n_rstd"),
                                                          sem("n_xn"), sem("n_mm"), sem("n_out"))
        w3_ready, v3_mm, v3_out = sem("w3_ready"), sem("v3_mm"), sem("v3_out")
        pj_mm, pj_out = sem("pj_mm"), sem("pj_out")
        s3_mm, s3_max, s3_exp, t3_mm, t3_out = (sem("s3_mm"), sem("s3_max"), sem("s3_exp"), sem("t3_mm"),
                                                sem("t3_out"))
        o3_mm, o3_r, o3_out, u3_mm, u3_out, y3_mm, y3_add = (sem("o3_mm"), sem("o3_r"), sem("o3_out"),
                                                             sem("u3_mm"), sem("u3_out"), sem("y3_mm"),
                                                             sem("y3_add"))
        vseq_set, vseq_ready, m3_out, r3_mm = (sem("vseq_set"), sem("vseq_ready"), sem("m3_out"), sem("r3_mm"))
        pad_set = sem("pad_set")
        w4_mm, w4_hi, w4_lo = sem("w4_mm"), sem("w4_hi"), sem("w4_lo")
        w4_quant = sem("w4_quant")
        x5 = sem("x5")
        x5_stats, x5_eps, x5_rstd, x5_mm, x5_out = (sem("x5_stats"), sem("x5_eps"), sem("x5_rstd"),
                                                    sem("x5_mm"), sem("x5_out"))
        sxg_ready, qx_ready = sem("sxg_ready"), sem("qx_ready")
        gate_mm, up_mm, silu_out, t_prod, t_max, t_scale, t_recip, t_scaled = (
            sem("gate_mm"), sem("up_mm"), sem("silu_out"), sem("t_prod"), sem("t_max"), sem("t_scale"),
            sem("t_recip"), sem("t_scaled"))
        t_expo, t_magic, t_sum, t5_q, t5_mm, t5_out, y5_mm, x5_done = (
            sem("t_expo"), sem("t_magic"), sem("t_sum"), sem("t5_q"), sem("t5_mm"), sem("t5_out"),
            sem("y5_mm"), sem("x5_done"))

        counts = {}

        def wait(eng, s, v):
            if isinstance(v, int) and v <= 0:
                return
            eng.wait_ge(s, v)

        def wait_apart(eng, s, v):
            if isinstance(v, int):
                eng.wait_ge(s, v)
                return
            eng.wait_ge(s, v)
            nc.vector.memset(unread[:], 0.0)

        def then_next(eng, ins, s, key):
            counts[key] = counts.get(key, 0) + 1
            ins.then_inc(s, 1)
            eng.wait_ge(s, counts[key])

        def barrier(eng, n, engines=5):
            eng.drain().then_inc(phase_end, 1)
            eng.wait_ge(phase_end, engines * n)

        def stage(g, i, lag, steps, groups=NG):
            if isinstance(g, int):
                f = g * steps + i - lag
                if f < 0 or f >= groups * steps:
                    return None
                return f // steps, f % steps
            back = -((i - lag) // steps)
            return g - back, (i - lag) % steps

        def pipeline(eng, groups, steps, body):
            for i in range(steps):
                body(0, i)
            with eng.Fori(1, groups) as g:
                for i in range(steps):
                    body(g, i)
            for i in range(steps):
                body(groups, i)

        B_LAG, S_LAG, N_LAG, T_LAG, O_LAG = 1, 2, 3, 4, 5
        Y_AT, L_AT, G_AT = 5, 7, 7
        STEPS2, BIAS_AT, LN_AT = NE + 2, NE, NE + 1
        STEPS3, NG3 = 16, 4
        S3, T3, O3, R3, U3, Y3 = 4, 6, 8, 9, 10, 11
        W_TURNS = 2 * DC * 2 + NF // 2
        STEPS4, NG4 = 4, 4
        GU4, Q4, T4, Y4 = 1, 2, 3, 4
        QB, BB, SB, TB, OB, MB = (0, 1), 2, 3, 5, 6, 7

        FIRST = [("ctx", kv[:]), ("ropek_c", ropek_c[:]), ("ropek_s", ropek_s[:]), ("ident", ident[:])]
        WEIGHTS2 = [("L0_xattn_W_qr", r_wqrT), ("L0_xattn_W_kr", r_wkrT), ("L0_xattn_w_kc_kv", r_wkckv),
                    ("L0_xattn_Wo", r_woT)]
        CONSTS = [("rope_c", rope_c[:]), ("rope_s", rope_s[:]), ("L0_ffn_gate_w", gatew[:]),
                  ("identb", identb[:]), ("mask", mask[:])]

        block = ctx.enter_context(nc.Block())

        @block.sync
        def _(sp):
            for half in range(2):
                b = slice(half * NB // 2, (half + 1) * NB // 2)
                sp.dma_start(x[:, b, :], a["x"][:, b, :]).then_inc(ld_xb if half else ld_x, 16)
            for half, ld in enumerate((ld_w, ld_wb)):
                h = slice(half * H0 // 2, (half + 1) * H0 // 2)
                sp.dma_start(r_wq[:, h, :], a["L0_xattn_Wq"][:, h, :]).then_inc(ld, 16)
                sp.dma_start(r_wkcq[:, h, :], a["L0_xattn_w_kc_q"][:, h, :]).then_inc(ld, 16)
            for name, dst in WEIGHTS2:
                sp.dma_start(dst, a[name]).then_inc(ld_w2, 16)
            for name, dst in CONSTS:
                sp.dma_start(dst, a[name]).then_inc(ld_c, 16)
            sp.dma_start(idx_a[:], a["idx_a"]).then_inc(ld_i, 16)
            sp.dma_start(idx_b[:], a["idx_b"]).then_inc(ld_i, 16)
            barrier(sp, 1)
            sp.dma_start(fc1, a["L0_ffn_fc1_w"]).then_inc(ld_f1, 16)
            sp.dma_start(fc2, a["L0_ffn_fc2_w"]).then_inc(ld_f1, 16)
            barrier(sp, 2)
            for name, dst in (("before", before), ("L0_ffn_alpha", alpha), ("L0_ffn_fc1_b", fc1b),
                              ("L0_ffn_fc2_b", fc2b)):
                sp.dma_start(dst, a[name]).then_inc(ld_2, 16)
            sp.dma_start(wd_n, a["L1_ffn_w_down"]).then_inc(ld_d, 16)
            sp.wait_ge(fc_lo, NE)
            sp.wait_ge(fc_lo1, NE)
            for name, dst in (("L1_xattn_Wq", wqm), ("L1_xattn_Wkv", wkv1), ("L1_xattn_Wout", wout1),
                              ("ctxT", ctxT)):
                sp.dma_start(dst, a[name]).then_inc(ld_3, 16)
            barrier(sp, 3)
            with sp.Fori(0, NG4) as g:
                sp.wait_ge(x5_done, (g + 1) * STEPS4 + 1)
                sp.dma_start(out[:, bass.ds(g * STEPS4, STEPS4), :],
                             x[:, bass.ds(g * STEPS4, STEPS4), :]).then_inc(stored, 16)
            sp.wait_ge(stored, 16 * NG4)

        PREP = ([("wc", h) for h in range(H0 // 2)] + [("x", g) for g in range(NB // 2)]
                + [("wc", h) for h in range(H0 // 2, H0)] + [("qk", n) for n in range(H0 // 4)]
                + [("vo", n) for n in range(NPAIR // 2)] + [("kv", n) for n in range(NB // 4)])

        def is_split(n):
            return PREP[n][0] in ("x", "wc")

        def uses(n, split):
            return sum(is_split(m) == split for m in range(n + 1))

        def prep_out(n):
            b = bank(n % 8)
            kind, m = PREP[n]
            if kind == "wc":
                return (b[:, 0:DC * DQ0].rearrange("p (c q) -> p c q", c=DC), wc_hi[:, :, m, :], wc_lo[:, :, m, :])
            if kind == "x":
                t = slice(GT * m, GT * m + GT)
                return b.rearrange("p (c t) -> p c t", c=DC), xn_hi[:, :, t], xn_lo[:, :, t]
            if kind == "qk":
                return (b[0:HALF, :].rearrange("p (h a d) -> p h a d", h=4, a=2),
                        wqk[:, 8 * (m // 2):8 * (m // 2) + 8].rearrange("p (h e) a d -> p e h a d", e=2)[:, m % 2], None)
            if kind == "vo":
                return b.rearrange("p (h o) -> p h o", h=2), wvo[:, 2 * m:2 * m + 2, :], None
            return b, kvT[:, 512 * m:512 * m + 512], None

        def turned(u):
            if u < 4 * DC:
                j, hc, part = u // 4, u // 2 % DC, u % 2
                at, n = (0, 512) if part == 0 else (512, FF - 512)
                cols = slice(j * FF + at, j * FF + at + n)
                return wgu_hi[:, hc, cols], wgu_lo[:, hc, cols], bank(7)[:, 0:n]
            k = 2 * (u - 4 * DC)
            if FCH[k + 1][1] == P:
                b = bank(7).rearrange("p (k d) -> p k d", k=2)
                return wd_hi[:, k:k + 2], wd_lo[:, k:k + 2], b
            return wd_hi[:, k], wd_lo[:, k], bank(7)[:, 0:D]

        LAST_ROWS = FCH[-1][1]
        last_turn = (wd_hi[0:LAST_ROWS, NF - 1], wd_lo[0:LAST_ROWS, NF - 1], bank(7)[0:LAST_ROWS, D:2 * D])

        @block.tensor
        def _(pe):
            mm = nc.tensor.matmul

            def mm3(o, w_hi, w_lo, m_hi, m_lo, start, stop):
                mm(o, w_hi, m_lo, start=start, stop=False)
                mm(o, w_lo, m_hi, start=False, stop=False)
                return mm(o, w_hi, m_hi, start=False, stop=stop)

            pe.wait_ge(ld_ctx, 16 * len(FIRST))
            for n, (kind, m) in enumerate(PREP):
                if n >= 8:
                    split = is_split(n - 8)
                    pe.wait_ge(prep_lo if split else prep_whole, uses(n - 8, split))
                to = prep_out(n)[0]
                if kind == "x":
                    pe.wait_ge(xn_ready, GB * (m + 1))
                    for k in range(GB):
                        for c in range(DC):
                            last = nc.tensor.transpose(to[:, c, k * P:(k + 1) * P],
                                                       xn_all[:, (GB * m + k) % (NB // 2), c * P:(c + 1) * P],
                                                       ident[:])
                elif kind == "wc":
                    pe.wait_ge(ld_w if m < H0 // 2 else ld_wb, 32)
                    for c in range(DC):
                        last = mm(to[:, c, :], r_wq[:, m, c * P:(c + 1) * P], r_wkcq[:, m, :])
                elif kind == "qk":
                    pe.wait_ge(ld_w2, 16 * len(WEIGHTS2))
                    for k in range(4):
                        h = 8 * (m // 2) + m % 2 + 2 * k
                        r = slice(64 * (h % 2), 64 * (h % 2) + 64)
                        for half in range(2):
                            last = mm(to[:, k, half, :], r_wqrT[r, h // 2, half * HALF:(half + 1) * HALF],
                                      r_wkrT[r, h // 2, :])
                elif kind == "vo":
                    for k in range(2):
                        for odd in range(2):
                            h = 4 * m + 2 * k + odd
                            last = mm(to[64 * odd:64 * odd + 64, k, :], r_wkckv[:, h, :], r_woT[:, h, :])
                else:
                    pe.wait_ge(kv_ready, 2)
                    for k in range(4):
                        last = nc.tensor.transpose(to[:, k * P:(k + 1) * P],
                                                   kvd[:, 4 * m + k].rearrange("p a d -> p (a d)"), ident[:])
                last.then_inc(prep_mm, 1)
            barrier(pe, 1)

            pe.wait_ge(ld_c, 16 * len(CONSTS))
            def query(g, i, h):
                s = stage(g, i, 0, NPAIR)
                if s is None:
                    return
                grp, p = s
                f = NPAIR * grp + p
                wait(pe, q_scaled, 2 * f + h - 1)
                o = bank(QB[h])[0:HALF, :]
                for half in range(2):
                    for c in range(DC):
                        w = (c, 2 * p + h, slice(half * HALF, (half + 1) * HALF))
                        tok = bass.ds(grp * GT, GT)
                        last = mm3(o[:, half * GT:(half + 1) * GT], wc_hi[:, *w], wc_lo[:, *w],
                                   xn_hi[:, c, tok], xn_lo[:, c, tok], c == 0, c == DC - 1)
                last.then_inc(q_mm, 1)

            def to_rank(g, i):
                s = stage(g, i, B_LAG, NPAIR)
                if s is None:
                    return
                grp, p = s
                f = NPAIR * grp + p
                pe.wait_ge(q_roped, 2 * f + 2)
                wait(pe, b_out, f)
                for h in range(2):
                    for half in range(2):
                        last = mm(bank(BB)[64 * h:64 * h + 64, 0:GT], wqk[:, 2 * p + h, half, :],
                                  roped[:, p % 2, h, half * GT:(half + 1) * GT],
                                  start=(half == 0), stop=(half == 1))
                last.then_inc(b_mm, 1)

            def scores(g, i):
                s = stage(g, i, S_LAG, NPAIR)
                if s is None:
                    return
                grp, p = s
                f = NPAIR * grp + p
                pe.wait_ge(b_out, f + 1)
                if p == 0:
                    pe.wait_ge(kv_copied, grp + 1)
                wait(pe, s_exp, f)
                for b in range(GB):
                    for h in range(2):
                        last = mm(bank(SB + h)[:, b * P:(b + 1) * P],
                                  qT[64 * h:64 * h + 64, p % 2, b * P:(b + 1) * P],
                                  kvTg[64 * h:64 * h + 64, b * P:(b + 1) * P])
                last.then_inc(s_mm, 1)

            def transpose_p(g, i):
                s = stage(g, i, T_LAG, NPAIR)
                if s is None:
                    return
                grp, p = s
                f = NPAIR * grp + p
                pe.wait_ge(p_norm, f + 1)
                wait(pe, t_out, f)
                for k in range(4):
                    last = nc.tensor.transpose(bank(TB)[:, k * P:(k + 1) * P], prob[:, p % 4, k, :], ident[:])
                last.then_inc(t_mm, 1)

            def mix(g, i):
                s = stage(g, i, O_LAG, NPAIR)
                if s is None:
                    return
                grp, p = s
                f = NPAIR * grp + p
                pe.wait_ge(t_out, f + 1)
                if p == 0:
                    pe.wait_ge(kvg_copied, grp + 1)
                wait(pe, o_out, f)
                for b in range(GB):
                    for h in range(2):
                        last = mm(bank(OB)[64 * h:64 * h + 64, b * P:(b + 1) * P], kvg[:, b, :],
                                  probT[:, p % 2, 2 * h + b, :])
                last.then_inc(o_mm, 1)

            def close_group(g, i, last_part):
                s = stage(g, 0, 1, NPAIR)
                pairs = {Y_AT: range(NPAIR)}
                if isinstance(g, int) and g == NG:
                    pairs = {1: range(4), 3: range(4, 6), Y_AT: range(6, NPAIR)}
                if s is None or not (i in pairs or i in (L_AT, G_AT)):
                    return
                grp = s[0]
                if i in pairs and not last_part:
                    pe.wait_ge(o_out, NPAIR * grp + pairs[i].stop)
                    if pairs[i].start == 0:
                        pe.wait_ge(g_out, grp + 1)
                    for b in range(GB):
                        for p in range(NPAIR) if b == GB - 1 and i == Y_AT else pairs[i] if b == 0 else ():
                            last = mm(bank(MB)[:, b * D:(b + 1) * D], ctxhT[:, p, b * P:(b + 1) * P],
                                      wvo[:, p, :], start=(p == 0), stop=(p == NPAIR - 1))
                    if i == Y_AT:
                        last.then_inc(y_mm, 1)
                if i == L_AT and not last_part:
                    pe.wait_ge(l_xn, grp + 1)
                    pe.wait_ge(y_add, grp + 1)
                    for b in range(GB):
                        for c in range(DC):
                            last = nc.tensor.transpose(bank(MB)[:, c * GT + b * P:c * GT + (b + 1) * P],
                                                       xn2[:, b, c * P:(c + 1) * P], ident[:])
                    last.then_inc(l_mm, 1)
                if i == G_AT and last_part:
                    pe.wait_ge(l_out, grp + 1)
                    for b in range(GB):
                        for c in range(DC):
                            last = mm(bank(MB)[:, b * NE:(b + 1) * NE], xgT[:, c, b * P:(b + 1) * P],
                                      gatew[:, c, :], start=(c == 0), stop=(c == DC - 1))
                    last.then_inc(g_mm, 1)

            def body(g, i):
                query(g, i, 0)
                scores(g, i)
                close_group(g, i, False)
                query(g, i, 1)
                transpose_p(g, i)
                mix(g, i)
                to_rank(g, i)
                close_group(g, i, True)

            pipeline(pe, NG, NPAIR, body)
            barrier(pe, 2)


            def up(g, i):
                s = stage(g, i, 0, STEPS2, NG2)
                if s is None or i > BIAS_AT:
                    return
                grp, e = s
                if e == 0:
                    wait(pe, h_out, grp)
                elif e == 1:
                    wait(pe, n_out, grp)
                else:
                    pe.wait_ge(h_hi, IC * (NE * grp + e - 1))
                if isinstance(g, int) and e < NE:
                    pe.wait_ge(fc_lo1, e + 1)
                if e == BIAS_AT:
                    pe.wait_ge(f_cp, grp + 1)
                    for b in range(GB2):
                        last = nc.tensor.transpose(bank(0)[0:NE, b * P:(b + 1) * P], combg[:, b, :], ident[:])
                else:
                    for m in range(IC):
                        for c in range(DC):
                            w, tok = (e, c, slice(m * P, (m + 1) * P)), bass.ds(grp * T2, T2)
                            last = mm3(bank(2 * (e % 2) + m), fc1_hi[:, *w], fc1_lo[:, *w],
                                       xn_hi[:, c, tok], xn_lo[:, c, tok], c == 0, c == DC - 1)
                last.then_inc(h_mm, 1)

            def down(g, i):
                s = stage(g, i, 1, STEPS2, NG2)
                if s is None or s[1] > BIAS_AT:
                    return
                grp, e = s
                n = (NE + 1) * grp + e
                if e == BIAS_AT:
                    pe.wait_ge(h_out, grp + 1)
                else:
                    pe.wait_ge(h_lo, IC * (NE * grp + e + 1))
                    if isinstance(g, int) and g == 0:
                        pe.wait_ge(fc_lo, e + 1)
                wait(pe, f_acc, n - (0 if e == 0 else 1))
                for b in range(GB2):
                    o = bank(4 + 2 * (e % 2) + b // 2)[:, (b % 2) * D:(b % 2 + 1) * D]
                    if e == BIAS_AT:
                        if b == 0:
                            pe.wait_ge(ld_2, 64)
                        last = mm(o, combT[:, b * P:(b + 1) * P], fc2b)
                    else:
                        for m in range(IC):
                            h = (e % 2, m, slice(b * P, (b + 1) * P))
                            last = mm3(o, hT_hi[:, *h], hT_lo[:, *h], fc2_hi[:, e, m, :], fc2_lo[:, e, m, :],
                                       m == 0, m == IC - 1)
                last.then_inc(f_mm, 1)

            def next_x(g, i):
                s = stage(g, 0, 1, STEPS2, NG2)
                if s is None or i != LN_AT:
                    return
                grp = s[0]
                pe.wait_ge(n_xn, grp + 1)
                if not isinstance(g, int) or g < NG2:
                    pe.wait_ge(h_hi, IC * NE * (grp + 2))
                else:
                    pe.wait_ge(n_out, grp + 1)
                for c in range(DC):
                    for b in range(GB2):
                        last = nc.tensor.transpose(bank(2 + c)[:, b * P:(b + 1) * P],
                                                   xn4[:, b, c * P:(c + 1) * P], ident[:])
                last.then_inc(n_mm, 1)

            def values(g, i):
                if not isinstance(g, int) or g != NG2 or i != 0:
                    return
                pe.wait_ge(ld_3, 64)
                pe.wait_ge(h_out, NG2)
                for n in range(NB // 2):
                    wait(pe, v3_out, n - 1)
                    for b in range(2):
                        last = mm(bank(n % 2)[:, b * D:(b + 1) * D], ctxT[:, (2 * n + b) * P:(2 * n + b + 1) * P],
                                  wkv1[:, D:2 * D])
                    last.then_inc(v3_mm, 1)

            def body2(g, i):
                up(g, i)
                next_x(g, i)
                down(g, i)
                values(g, i)

            pipeline(pe, NG2, STEPS2, body2)
            barrier(pe, 3)

            pe.wait_ge(wqm_split, 2)

            def project(g, i):
                s = stage(g, i, 0, STEPS3, NG3)
                if s is None or i % 8 > 2:
                    return
                grp, u = s[0], i % 8
                half = 2 * grp + i // 8
                wait(pe, pj_out, 3 * half + u)
                tok = bass.ds(half * GT, GT)
                for ct in range(DC):
                    o = bank(6)[:, ct * GT:(ct + 1) * GT]
                    if u == 2:
                        last = mm(o, wkv1[:, ct * P:(ct + 1) * P], ctxT[:, tok])
                    else:
                        for c in range(DC):
                            last = mm3(o, wqm_hi[:, c, ct, u, :], wqm_lo[:, c, ct, u, :],
                                       xn_hi[:, c, tok], xn_lo[:, c, tok], c == 0, c == DC - 1)
                last.then_inc(pj_mm, 1)

            def scores3(g, i):
                s = stage(g, i, S3, STEPS3, NG3)
                if s is None:
                    return
                grp, k = s
                f, half, b, w = STEPS3 * grp + k, 2 * grp + k // 8, k // 4 % 2, k % 4
                if k % 8 == 0:
                    pe.wait_ge(pj_out, 3 * half + 3)
                wait(pe, s3_exp, f - 3)
                mm(bank(w), identb[:], mask[:].rearrange("p k l -> p (k l)"), start=True, stop=False)
                r = slice(32 * w, 32 * w + 32)
                t = slice(b * P, (b + 1) * P)
                for ct in range(DC):
                    for e in range(2):
                        o = 2 * ct + e
                        last = mm(bank(w)[:, o * P:(o + 1) * P], q3[r, k // 8, e, ct, t], k3[r, k // 8, ct, t],
                                  start=False, stop=(o == 3))
                last.then_inc(s3_mm, 1)

            def transpose3(g, i):
                s = stage(g, i, T3, STEPS3, NG3)
                if s is None:
                    return
                grp, k = s
                f = STEPS3 * grp + k
                pe.wait_ge(s3_exp, f + 1)
                wait(pe, t3_out, f)
                for o in range(4):
                    last = nc.tensor.transpose(bank(4)[:, o * P:(o + 1) * P], prob3[:, k % 4, o, :], ident[:])
                last.then_inc(t3_mm, 1)

            def mix3(g, i):
                s = stage(g, i, O3, STEPS3, NG3)
                if s is None:
                    return
                grp, k = s
                f, b, w = STEPS3 * grp + k, 4 * grp + k // 4, k % 4
                pe.wait_ge(t3_out, f + 1)
                if w == 0:
                    pe.wait_ge(vseq_ready, b + 1)
                    wait(pe, m3_out, b)
                for o in range(4):
                    h = 8 * (o // 2) + 2 * w + o % 2
                    last = mm(bank(5)[32 * o:32 * o + 32, w * P:(w + 1) * P], vseq[:, k // 4 % 2, h, :],
                              probT3[:, k % 2, o, :])
                last.then_inc(o3_mm, 1)

            def turn_back(g, i):
                s = stage(g, i, R3, STEPS3, NG3)
                if s is None or s[1] % 4 != 3:
                    return
                b = 4 * s[0] + s[1] // 4
                pe.wait_ge(m3_out, b + 1)
                wait(pe, y3_add, b)
                if isinstance(g, int):
                    pe.wait_ge(w4_lo, W_TURNS)
                for w in range(4):
                    last = nc.tensor.transpose(bank(7)[:, w * P:(w + 1) * P], mixed[:, w, :], ident[:])
                last.then_inc(r3_mm, 1)

            def turn_weights(g, i):
                if not isinstance(g, int) or g > 0 or i >= W_TURNS:
                    return
                pe.wait_ge(w4_quant, 1)
                wait(pe, w4_lo, i)
                if i < 4 * DC:
                    j, hc, part = i // 4, i // 2 % DC, i % 2
                    for k in range(4 * part, min(NF, 4 * part + 4)):
                        n = FCH[k][1]
                        o = (k - 4 * part) * P
                        last = nc.tensor.transpose(bank(7)[:, o:o + n], wgu_n[0:n, NF * j + k, hc * P:(hc + 1) * P],
                                                   ident[0:n, 0:n])
                else:
                    for q in range(2):
                        at, n = FCH[2 * (i - 4 * DC) + q]
                        for c in range(DC):
                            last = nc.tensor.transpose(bank(7)[0:n, q * D + c * P:q * D + (c + 1) * P],
                                                       wd_n[:, c, at:at + n], ident[:])
                last.then_inc(w4_mm, 1)

            def project_out(g, i):
                s = stage(g, i, U3, STEPS3, NG3)
                if s is not None and s[1] % 4 == 3:
                    b = 4 * s[0] + s[1] // 4
                    pe.wait_ge(o3_out, b + 1)
                    for c in range(DC):
                        last = nc.tensor.transpose(bank(7)[:, c * P:(c + 1) * P], ctx3[:, c * P:(c + 1) * P], ident[:])
                    last.then_inc(u3_mm, 1)
                s = stage(g, i, Y3, STEPS3, NG3)
                if s is not None and s[1] % 4 == 3:
                    b = 4 * s[0] + s[1] // 4
                    pe.wait_ge(u3_out, b + 1)
                    for c in range(DC):
                        last = mm(bank(7)[:, D:2 * D], ctx3T[:, c, :], wout1[:, c, :],
                                  start=(c == 0), stop=(c == DC - 1))
                    last.then_inc(y3_mm, 1)

            def body3(g, i):
                project(g, i)
                scores3(g, i)
                turn_weights(g, i)
                mix3(g, i)
                turn_back(g, i)
                transpose3(g, i)
                project_out(g, i)

            pipeline(pe, NG3, STEPS3, body3)

            pe.wait_ge(s3_exp, STEPS3 * NG3)
            pe.wait_ge(t3_out, STEPS3 * NG3)
            pe.wait_ge(m3_out, NB)
            pe.wait_ge(pj_out, 3 * NB // GB)

            def x_turned(g, i):
                s = stage(g, i, 0, STEPS4, NG4)
                if s is None:
                    return
                f = STEPS4 * s[0] + s[1]
                pe.wait_ge(qx_ready, f + 1)
                wait(pe, x5_out, f)
                for c in range(DC):
                    last = nc.tensor.transpose(bank16(4)[:, c * P:(c + 1) * P],
                                               qx_all[:, bass.ds(f, 1), c * P:(c + 1) * P]
                                               .rearrange("p a d -> p (a d)"), identb[:])
                last.then_inc(x5_mm, 1)

            def gate_up(g, i):
                s = stage(g, i, GU4, STEPS4, NG4)
                if s is None:
                    return
                grp, k = s
                f = STEPS4 * grp + k
                pe.wait_ge(x5_out, f + 1)
                wait(pe, silu_out, f)
                for o in range(4):
                    if o == 2:
                        last.then_inc(gate_mm, 1)
                        wait(pe, t_prod, f)
                    cols = slice(o * (FF // 2), (o + 1) * (FF // 2))
                    for c in range(DC):
                        mm(bank(o)[:, 0:FF // 2], qxT[:, k % 2, c, :], wgu_hi[:, c, cols],
                           start=(c == 0), stop=False)
                        last = mm(bank(o)[:, 0:FF // 2], qxT[:, k % 2, c, :], wgu_lo[:, c, cols],
                                  start=False, stop=(c == DC - 1))
                last.then_inc(up_mm, 1)

            def t_turned(g, i):
                s = stage(g, i, T4, STEPS4, NG4)
                if s is None:
                    return
                grp, k = s
                f = STEPS4 * grp + k
                pe.wait_ge(t5_q, f + 1)
                wait(pe, t5_out, f)
                for c, (at, n) in enumerate(FCH):
                    last = nc.tensor.transpose(bank16(5)[0:n, c * P:(c + 1) * P], qt[:, k % 2, at:at + n], identb[:])
                last.then_inc(t5_mm, 1)

            def y_down(g, i):
                s = stage(g, i, Y4, STEPS4, NG4)
                if s is None:
                    return
                grp, k = s
                f = STEPS4 * grp + k
                pe.wait_ge(t5_out, f + 1)
                pe.wait_ge(x5_done, f + 1)
                for c, (at, n) in enumerate(FCH):
                    mm(bank(6)[:, 0:D], qtT[0:n, c, :], wd_hi[0:n, c, :], start=(c == 0), stop=False)
                    last = mm(bank(6)[:, 0:D], qtT[0:n, c, :], wd_lo[0:n, c, :],
                              start=False, stop=(c == NF - 1))
                last.then_inc(y5_mm, 1)

            def body4(g, i):
                gate_up(g, i)
                x_turned(g, i)
                y_down(g, i)
                t_turned(g, i)

            pipeline(pe, NG4, STEPS4, body4)

        @block.scalar
        def _(act):
            def copy(o, i):
                return nc.scalar.activation(o, i, ACT.Copy)

            for name, dst in FIRST:
                act.dma_start(dst, a[name]).then_inc(ld_ctx, 16)
            for n in range(len(PREP)):
                if n == NB // 2 + H0:
                    act.wait_ge(kv_step, 3)
                    for twice in range(2):
                        copy(kvd[:, :, twice, :], kv[:]).then_inc(kv_ready, 1)
                act.wait_ge(prep_mm, n + 1)
                src, dst, _ = prep_out(n)
                copy(dst, src).then_inc(prep_hi if is_split(n) else prep_whole, 1)
            barrier(act, 1)

            def exps(g, i):
                s = stage(g, i, S_LAG, NPAIR)
                if s is None:
                    return
                grp, p = s
                f = NPAIR * grp + p
                act.wait_ge(s_max, f + 1)
                wait(act, t_mm, f - 3)
                wait(act, norm_r, f - 1)
                for k in range(4):
                    last = nc.scalar.activation(prob[:, p % 4, k, :],
                                                bank(SB + k // 2)[:, (k % 2) * P:(k % 2 + 1) * P],
                                                ACT.Exp, bias=nmax[:, p % 2, k:k + 1],
                                                accum_out=rsum[:, p % 2, k:k + 1])
                last.then_inc(s_exp, 1)

            def probs_out(g, i):
                s = stage(g, i, T_LAG, NPAIR)
                if s is None:
                    return
                grp, p = s
                f = NPAIR * grp + p
                act.wait_ge(t_mm, f + 1)
                wait(act, o_mm, f - 1)
                copy(probT[:, p % 2].rearrange("p k t -> p (k t)"), bank(TB)).then_inc(t_out, 1)

            def ctx_out(g, i):
                s = stage(g, i, O_LAG, NPAIR)
                if s is None:
                    return
                grp, p = s
                f = NPAIR * grp + p
                act.wait_ge(o_mm, f + 1)
                if p == 0:
                    wait(act, y_mm, grp)
                copy(ctxhT[:, p, :], bank(OB)[:, 0:GT]).then_inc(o_out, 1)

            def close_group(g, i, last_part):
                s = stage(g, 0, 1, NPAIR)
                if s is None:
                    if i == G_AT and last_part:
                        copy(unread_act[:], ident[:, 0:1]).then_inc(g_out, 1)
                    return
                grp = s[0]
                if i == L_AT and not last_part:
                    act.wait_ge(l_mm, grp + 1)
                    src = bank(MB).rearrange("p (c t) -> p c t", c=DC)
                    act.wait_ge(l_lo, grp + 1)
                    copy(xgT[:, :, :], src)
                    copy(xn_hi[:, :, bass.ds(grp * GT, GT)], src).then_inc(l_out, 1)
                if i == G_AT and last_part:
                    act.wait_ge(g_mm, grp + 1)
                    copy(logits[:, bass.ds(grp * GB, GB), :],
                         bank(MB)[:, 0:GB * NE].rearrange("p (b e) -> p b e", b=GB)).then_inc(g_out, 1)

            def q_out(g, i):
                s = stage(g, i, B_LAG, NPAIR)
                if s is None:
                    return
                grp, p = s
                f = NPAIR * grp + p
                act.wait_ge(b_mm, f + 1)
                wait(act, s_mm, f - 1)
                copy(qT[:, p % 2, :], bank(BB)[:, 0:GT]).then_inc(b_out, 1)

            def group_kv(g, i):
                s = stage(g, i, S_LAG, NPAIR)
                if s is None or s[1] != 0:
                    return
                grp = s[0]
                wait(act, s_mm, NPAIR * grp)
                copy(kvTg, kvT[:, bass.ds(grp * GT, GT)]).then_inc(kv_copied, 1)

            def group_ctx(g, i):
                s = stage(g, i, O_LAG, NPAIR)
                if s is None or s[1] != 0:
                    return
                wait(act, o_mm, NPAIR * s[0])
                copy(kvg[:], kv[:, bass.ds(s[0] * GB, GB), :]).then_inc(kvg_copied, 1)

            def body(g, i):
                group_kv(g, i)
                group_ctx(g, i)
                exps(g, i)
                close_group(g, i, False)
                probs_out(g, i)
                ctx_out(g, i)
                q_out(g, i)
                close_group(g, i, True)

            pipeline(act, NG, NPAIR, body)
            barrier(act, 2)

            def split_expert(e):
                if e < NE:
                    copy(fc1_hi[:, e], fc1[:, e]).then_inc(fc_hi1, 1)
                    copy(fc2_hi[:, e], fc2[:, e]).then_inc(fc_hi, 1)

            act.wait_ge(ld_f1, 32)
            split_expert(0)
            split_expert(1)
            act.wait_ge(gate_max, 1)
            nc.scalar.activation(expl, expl, ACT.Exp).then_inc(gate_exp, 1)
            act.wait_ge(ld_2, 64)

            def gelu(g, i):
                s = stage(g, i, 0, STEPS2, NG2)
                if s is None or i > BIAS_AT:
                    return
                grp, e = s
                n = (NE + 1) * grp + e
                act.wait_ge(h_mm, n + 1)
                if e == BIAS_AT:
                    wait(act, f_mm, n - NE)
                    copy(combT, bank(0)[0:NE, :]).then_inc(h_out, 1)
                    return
                wait(act, f_mm, n - 1 if e >= 2 else n - 2)
                for m in range(IC):
                    wait(act, h_lo, IC * (NE * grp + e - 1) + m + 1)
                    nc.scalar.activation(hT[:, m, :], bank(2 * (e % 2) + m), ACT.Gelu, bias=fc1b[:, e, m:m + 1])
                    nc.scalar.activation(hT_hi[:, e % 2, m, :], bank(2 * (e % 2) + m), ACT.Gelu,
                                                bias=fc1b[:, e, m:m + 1]).then_inc(h_hi, 1)
                if isinstance(g, int):
                    split_expert(e + 2)

            def next_x(g, i):
                s = stage(g, 0, 1, STEPS2, NG2)
                if s is None or i != LN_AT:
                    return
                grp = s[0]
                act.wait_ge(n_mm, grp + 1)
                for c in range(DC):
                    last = copy(xn_hi[:, c, bass.ds(grp * T2, T2)], bank(2 + c))
                last.then_inc(n_hi, 1)

            def values(g, i):
                if not isinstance(g, int) or g != NG2 or i != 0:
                    return
                act.wait_ge(w3_ready, 1)
                for n in range(NB // 2):
                    act.wait_ge(v3_mm, n + 1)
                    for b in range(2):
                        last = copy(vaug[:, 2 * n + b, :, 0:HD1],
                                    bank(n % 2)[:, b * D:(b + 1) * D].rearrange("p (h d) -> p h d", h=H1))
                    last.then_inc(v3_out, 1)

            def body2(g, i):
                gelu(g, i)
                next_x(g, i)
                values(g, i)

            pipeline(act, NG2, STEPS2, body2)
            barrier(act, 3)

            act.wait_ge(ld_3, 64)
            nc.scalar.activation(wqm_hi[:], wqm, ACT.Copy, scale=QUERY_SCALE).then_inc(wqm_split, 1)

            def project(g, i):
                s = stage(g, i, 0, STEPS3, NG3)
                if s is None or i % 8 > 2:
                    return
                grp, u = s[0], i % 8
                half = 2 * grp + i // 8
                act.wait_ge(pj_mm, 3 * half + u + 1)
                wait(act, s3_mm, 8 * (half - 1))
                dst = k3[:, i // 8] if u == 2 else q3[:, i // 8, u]
                copy(dst.rearrange("p c t -> p (c t)"), bank(6)).then_inc(pj_out, 1)

            def exps3(g, i):
                s = stage(g, i, S3, STEPS3, NG3)
                if s is None:
                    return
                grp, k = s
                f = STEPS3 * grp + k
                act.wait_ge(s3_max, f + 1)
                wait(act, t3_mm, f - 3)
                for o in range(4):
                    last = nc.scalar.activation(prob3[:, k % 4, o, :], bank(k % 4)[:, o * P:(o + 1) * P],
                                                ACT.Exp, bias=nmax3[:, k % 4, o:o + 1])
                last.then_inc(s3_exp, 1)

            def mixed_out(g, i):
                s = stage(g, i, O3, STEPS3, NG3)
                if s is None or s[1] % 4 != 3:
                    return
                b = 4 * s[0] + s[1] // 4
                act.wait_ge(o3_mm, 4 * (b + 1))
                wait(act, r3_mm, b)
                copy(mixed.rearrange("p w t -> p (w t)"), bank(5)).then_inc(m3_out, 1)

            def weights_hi(g, i):
                if not isinstance(g, int) or g > 0 or i >= W_TURNS:
                    return
                act.wait_ge(w4_mm, i + 1)
                hi, _, src = turned(i)
                if i == W_TURNS - 1:
                    copy(hi, src)
                    hi, _, src = last_turn
                copy(hi, src).then_inc(w4_hi, 1)

            def ctx_out3(g, i):
                s = stage(g, i, U3, STEPS3, NG3)
                if s is None or s[1] % 4 != 3:
                    return
                b = 4 * s[0] + s[1] // 4
                act.wait_ge(u3_mm, b + 1)
                wait(act, y3_mm, b)
                copy(ctx3T.rearrange("p c t -> p (c t)"), bank(7)[:, 0:D]).then_inc(u3_out, 1)

            def body3(g, i):
                project(g, i)
                exps3(g, i)
                mixed_out(g, i)
                weights_hi(g, i)
                ctx_out3(g, i)

            pipeline(act, NG3, STEPS3, body3)

            def x_turned(g, i):
                s = stage(g, i, 0, STEPS4, NG4)
                if s is None:
                    return
                grp, k = s
                f = STEPS4 * grp + k
                act.wait_ge(x5_mm, f + 1)
                wait(act, up_mm, f - 1)
                copy(qxT[:, k % 2].rearrange("p c t -> p (c t)"), bank16(4)[:, 0:D]).then_inc(x5_out, 1)

            def silu(g, i):
                s = stage(g, i, GU4, STEPS4, NG4)
                if s is None:
                    return
                grp, k = s
                f = STEPS4 * grp + k
                if k == 0:
                    act.wait_ge(sxg_ready, grp + 1)
                act.wait_ge(gate_mm, f + 1)
                wait(act, t_prod, f)
                nc.scalar.activation(tsl.rearrange("p (k n) -> p k n", k=2), ps[:, 0:2, 0:FF // 2], ACT.Silu,
                                     scale=sxg[:, k:k + 1]).then_inc(silu_out, 1)

            def scale_t(g, i):
                s = stage(g, i, GU4, STEPS4, NG4)
                if s is None:
                    return
                grp, k = s
                f = STEPS4 * grp + k
                act.wait_ge(t_recip, f + 1)
                wait(act, t5_q, f - 1)
                nc.scalar.activation(tv[:, k % 2, :], tt, ACT.Copy, scale=st[:, k, 1:2]).then_inc(t_scaled, 1)

            def t_turned(g, i):
                s = stage(g, i, T4, STEPS4, NG4)
                if s is None:
                    return
                grp, k = s
                f = STEPS4 * grp + k
                act.wait_ge(t5_mm, f + 1)
                wait(act, y5_mm, f)
                copy(qtT[:, 0:NF - 1, :].rearrange("p c t -> p (c t)"), bank16(5)[:, 0:(NF - 1) * P])
                copy(qtT[0:LAST_ROWS, NF - 1, :],
                     bank16(5)[0:LAST_ROWS, (NF - 1) * P:NF * P]).then_inc(t5_out, 1)

            def body4(g, i):
                silu(g, i)
                x_turned(g, i)
                t_turned(g, i)
                scale_t(g, i)

            pipeline(act, NG4, STEPS4, body4)

        @block.vector
        def _(dve):
            V = nc.vector

            def step(ins):
                then_next(dve, ins, dve_step, "dve")

            V.memset(mhalf[:], -0.5)
            V.memset(epst[:], LN_EPS)
            for b in range(NB):
                if b % (NB // 2) == 0:
                    dve.wait_ge(ld_xb if b else ld_x, 16)
                V.bn_stats(st6[:, b, :], x[:, b, :])
            step(V.memset(veps[:], 0.0))
            for b in range(NB):
                last = V.bn_aggr(mv[:, b, :], st6[:, b, :])
            step(last)
            V.tensor_scalar(veps[:], mv[:, :, 1], LN_EPS, None, ALU.add).then_inc(ln_stats, 1)

            def normalise_half(first):
                for b in range(first, first + NB // 2):
                    V.tensor_scalar(xn_all[:, b % (NB // 2), :], x[:, b, :], mv[:, b, 0:1], rstd[:, b:b + 1],
                                    ALU.subtract, ALU.mult).then_inc(xn_ready, 1)

            for n in range(len(PREP)):
                if n == H0 // 2:
                    dve.wait_ge(ln_rstd, 1)
                    normalise_half(0)
                    dve.wait_ge(prep_mm, H0 // 2 + NB // 4)
                    normalise_half(NB // 2)
                if is_split(n):
                    dve.wait_ge(prep_hi, uses(n, True))
                    src, hi, lo = prep_out(n)
                    V.tensor_tensor(lo, src, hi.bitcast(F32), ALU.subtract).then_inc(prep_lo, 1)
            barrier(dve, 1)

            dve.wait_ge(ld_c, 16 * len(CONSTS))
            rc = rope_c[:].rearrange("p a b t -> p (a b t)")
            rs = rope_s[:].rearrange("p a b t -> p (a b t)")

            def rope(g, i, h):
                s = stage(g, i, 0, NPAIR)
                if s is None:
                    return
                grp, p = s
                f = NPAIR * grp + p
                dve.wait_ge(q_mm, 2 * f + h + 1)
                wait(dve, q_roped, 2 * f + h - 1)
                q = bank(QB[h])[0:HALF, :]
                V.tensor_tensor(t1[:, h, :], q, rc, ALU.mult)
                V.tensor_tensor(t2[:, h, :], q, rs, ALU.mult).then_inc(q_scaled, 1)

            def row_max(g, i):
                s = stage(g, i, S_LAG, NPAIR)
                if s is None:
                    return
                grp, p = s
                f = NPAIR * grp + p
                dve.wait_ge(s_mm, f + 1)
                wait(dve, s_exp, f - 1)
                V.tensor_reduce(nmax[:, p % 2, :].rearrange("p (h b) -> p h b", h=2),
                                ps[:, SB:SB + 2, 0:GT].rearrange("p h (b l) -> p h b l", b=GB),
                                AX.X, ALU.max, negate=True).then_inc(s_max, 1)

            def normalise(g, i):
                s = stage(g, i, N_LAG, NPAIR)
                if s is None:
                    return
                grp, p = s
                f = NPAIR * grp + p
                dve.wait_ge(s_exp, f + 1)
                wait(dve, p_norm, f - 1)
                V.reciprocal(rinv[:, p % 2, :], rsum[:, p % 2, :]).then_inc(norm_r, 1)
                dve.wait_ge(norm_r, f + 1)
                V.tensor_tensor(prob[:, p % 4], prob[:, p % 4],
                                rinv[:, p % 2, :].unsqueeze(2).to_broadcast([P, 4, P]), ALU.mult).then_inc(p_norm, 1)

            def close_group(g, i):
                s = stage(g, 0, 1, NPAIR)
                if s is None or i not in (Y_AT, Y_AT + 1):
                    return
                grp = s[0]
                if i == Y_AT + 1:
                    layernorm(grp)
                    return
                dve.wait_ge(y_mm, grp + 1)
                xg = x[:, bass.ds(grp * GB, GB), :]
                V.tensor_tensor(xg, xg, bank(MB).rearrange("p (b d) -> p b d", b=GB), ALU.add).then_inc(y_add, 1)
                wait_apart(dve, y_add, grp + 1)
                for b in range(GB):
                    last = V.bn_stats(st6[:, b, :], x[:, bass.ds(grp * GB + b, 1), :].rearrange("p a d -> p (a d)"))
                last.then_inc(ln_a, 1)
                wait_apart(dve, ln_a, grp + 1)
                for b in range(GB):
                    last = V.bn_aggr(mv[:, b, :], st6[:, b, :])
                last.then_inc(l_stats, 1)

            def layernorm(grp):
                dve.wait_ge(l_rstd, grp + 1)
                for b in range(GB):
                    last = V.tensor_scalar(xn2[:, b, :], x[:, bass.ds(grp * GB + b, 1), :]
                                           .rearrange("p a d -> p (a d)"), mv[:, b, 0:1], rstd[:, b:b + 1],
                                           ALU.subtract, ALU.mult)
                last.then_inc(l_xn, 1)

            def body(g, i):
                rope(g, i, 0)
                row_max(g, i)
                rope(g, i, 1)
                normalise(g, i)
                close_group(g, i)

            pipeline(dve, NG, NPAIR, body)
            barrier(dve, 2)

            def expert_lo(e):
                if e < NE:
                    dve.wait_ge(fc_hi1, e + 1)
                    V.tensor_tensor(fc1_lo[:, e], fc1[:, e], fc1_hi[:, e].bitcast(F32), ALU.subtract)\
                        .then_inc(fc_lo1, 1)

            for j in range(2):
                last = V.memset(wgu_n[LAST_ROWS:P, NF * j + NF - 1, :], 1.0)
            last.then_inc(pad_set, 1)
            expert_lo(0)
            step(V.tensor_reduce(lmax, logits[:], AX.X, ALU.max))
            V.tensor_tensor(expl, logits[:], lmax.unsqueeze(2).to_broadcast([P, NB, NE]),
                            ALU.subtract).then_inc(gate_max, 1)
            dve.wait_ge(gate_exp, 1)
            every = [P, NB, NE, NE]
            mine = expl.unsqueeze(3).to_broadcast(every)
            other = expl.unsqueeze(2).to_broadcast(every)
            V.tensor_tensor(above, other, mine, ALU.is_gt)
            step(V.tensor_tensor(tied, other, mine, ALU.is_equal))
            expert_lo(1)
            dve.wait_ge(ld_2, 64)
            step(V.tensor_tensor(tied, tied, before.unsqueeze(1).to_broadcast(every), ALU.mult))
            step(V.tensor_tensor(above, above, tied, ALU.add))
            step(V.tensor_reduce(rank, above, AX.X, ALU.add))
            step(V.tensor_scalar(rank, rank, TOPK - 0.5, None, ALU.is_lt))
            step(V.tensor_tensor(rank, rank, expl, ALU.mult))
            step(V.tensor_reduce(lmax, rank, AX.X, ALU.add))
            step(V.reciprocal(lmax, lmax))
            step(V.tensor_tensor(rank, rank, lmax.unsqueeze(2).to_broadcast([P, NB, NE]), ALU.mult))
            V.tensor_tensor(comb, rank, alpha.unsqueeze(1).to_broadcast([P, NB, NE]), ALU.mult)\
                .then_inc(comb_ready, 1)
            dve.wait_ge(comb_ready, 1)

            def group_comb(g, i):
                s = stage(g, i, 0, STEPS2, NG2)
                if s is None or i != 1:
                    return
                grp = s[0]
                wait(dve, h_mm, (NE + 1) * grp)
                wait(dve, f_acc, (NE + 1) * grp)
                V.tensor_copy(combg, comb[:, bass.ds(grp * GB2, GB2), :]).then_inc(f_cp, 1)

            def accumulate(g, i):
                s = stage(g, i, 1, STEPS2, NG2)
                if s is None or s[1] > BIAS_AT:
                    return
                grp, e = s
                n = (NE + 1) * grp + e
                dve.wait_ge(f_mm, n + 1)
                wait(dve, f_acc, n)
                if e == 0:
                    dve.wait_ge(f_cp, grp + 1)
                for b in range(GB2):
                    xb = x[:, bass.ds(grp * GB2 + b, 1), :].rearrange("p a d -> p (a d)")
                    y = bank(4 + 2 * (e % 2) + b // 2)[:, (b % 2) * D:(b % 2 + 1) * D]
                    if e == BIAS_AT:
                        last = V.tensor_tensor(xb, xb, y, ALU.add)
                    else:
                        last = V.scalar_tensor_tensor(xb, y, combg[:, b, e:e + 1], xb, ALU.mult, ALU.add)
                last.then_inc(f_acc, 1)

            def layernorm2(g, i):
                s = stage(g, 0, 1, STEPS2, NG2)
                if s is None or i != 1:
                    return
                grp = s[0]
                wait_apart(dve, f_acc, (NE + 1) * (grp + 1))
                for b in range(GB2):
                    last = V.bn_stats(st6[:, b, :], x[:, bass.ds(grp * GB2 + b, 1), :].rearrange("p a d -> p (a d)"))
                last.then_inc(n_a, 1)
                wait_apart(dve, n_a, grp + 1)
                for b in range(GB2):
                    last = V.bn_aggr(mv[:, b, :], st6[:, b, :])
                last.then_inc(n_stats, 1)
                dve.wait_ge(n_rstd, grp + 1)
                for b in range(GB2):
                    last = V.tensor_scalar(xn4[:, b, :], x[:, bass.ds(grp * GB2 + b, 1), :]
                                           .rearrange("p a d -> p (a d)"), mv[:, b, 0:1], rstd[:, b:b + 1],
                                           ALU.subtract, ALU.mult)
                last.then_inc(n_xn, 1)

            def ones_of_values(g, i):
                if isinstance(g, int) and g == NG2 and i == 0:
                    dve.wait_ge(fc_lo, NE)
                    V.memset(vaug[:, :, :, HD1:V1], 1.0).then_inc(w3_ready, 1)

            def next_x_lo(g, i):
                s = stage(g, 0, 1, STEPS2, NG2)
                if i != LN_AT:
                    return
                if s is None:
                    V.memset(unread[:], 0.0).then_inc(n_out, 1)
                    return
                tok = bass.ds(s[0] * T2, T2)
                dve.wait_ge(n_hi, s[0] + 1)
                for c in range(DC):
                    last = V.tensor_tensor(xn_lo[:, c, tok], bank(2 + c), xn_hi[:, c, tok].bitcast(F32), ALU.subtract)
                last.then_inc(n_out, 1)

            def quantise_weights(q, part):
                k, w = (slice(3 * q, 3 * q + 3), wgu_n[:, 3 * q:3 * q + 3, :]) if q < 4 else \
                    (slice(2 * NF + q - 4, 2 * NF + q - 3), wd_n[:, q - 4:q - 3, :])
                rows, width = w.shape[1], w.shape[2]
                m = wm[:, 0:rows * width].rearrange("p (k d) -> p k d", k=rows)
                if part == 0:
                    step(V.tensor_reduce(ws[:, k], w, AX.X, ALU.max, apply_absolute_value=True))
                    step(V.tensor_scalar(ws[:, k], ws[:, k], 1.0 / FP8_MAX, None, ALU.mult))
                    step(V.reciprocal(wr[:, k], ws[:, k]))
                    step(V.tensor_tensor(w, w, wr[:, k].unsqueeze(2).to_broadcast([P, rows, width]), ALU.mult))
                elif part == 1:
                    step(V.tensor_scalar(m.bitcast(U32), w.bitcast(U32), SIGN_EXP, None, ALU.bitwise_and))
                    step(V.tensor_scalar(m, m, 2.0 ** -6, ROUND_FP8, ALU.max, ALU.mult))
                    step(V.tensor_tensor(w, w, m, ALU.add))
                else:
                    step(V.tensor_tensor(w, w, m, ALU.subtract))
                    last = V.tensor_tensor(w, w, ws[:, k].unsqueeze(2).to_broadcast([P, rows, width]), ALU.mult)
                    if q == 5:
                        last.then_inc(w4_quant, 1)

            def weights(g, i):
                if not isinstance(g, int) or g > 0 or i == 0:
                    return
                for n in (2 * (i - 1), 2 * i - 1):
                    if n % 3 == 0 and n < 12:
                        dve.wait_ge(ld_g[n // 3], 16 * 3)
                    if n == 12:
                        dve.wait_ge(ld_d, 16)
                    quantise_weights(n // 3, n % 3)

            def body2(g, i):
                if isinstance(g, int) and g == 0:
                    expert_lo(i + 2)
                group_comb(g, i)
                layernorm2(g, i)
                ones_of_values(g, i)
                accumulate(g, i)
                next_x_lo(g, i)
                weights(g, i)

            pipeline(dve, NG2, STEPS2, body2)
            barrier(dve, 3)

            V.memset(vseq, 0.0).then_inc(vseq_set, 1)
            dve.wait_ge(wqm_split, 1)
            V.scalar_tensor_tensor(wqm_lo[:], wqm, QUERY_SCALE, wqm_hi[:].bitcast(F32), ALU.mult, ALU.subtract)\
                .then_inc(wqm_split, 1)

            def row_max3(g, i):
                s = stage(g, i, S3, STEPS3, NG3)
                if s is None:
                    return
                grp, k = s
                f = STEPS3 * grp + k
                dve.wait_ge(s3_mm, f + 1)
                wait(dve, s3_exp, f - 3)
                V.tensor_reduce(nmax3[:, k % 4, :], bank(k % 4).rearrange("p (o l) -> p o l", o=4),
                                AX.X, ALU.max, negate=True).then_inc(s3_max, 1)

            def probs_out3(g, i):
                s = stage(g, i, T3, STEPS3, NG3)
                if s is None:
                    return
                grp, k = s
                f = STEPS3 * grp + k
                dve.wait_ge(t3_mm, f + 1)
                wait(dve, o3_mm, f - 1)
                V.tensor_copy(probT3[:, k % 2].rearrange("p o t -> p (o t)"), bank(4)).then_inc(t3_out, 1)

            def normalise3(g, i):
                s = stage(g, i, R3, STEPS3, NG3)
                if s is None or s[1] % 4 != 3:
                    return
                b = 4 * s[0] + s[1] // 4
                dve.wait_ge(r3_mm, b + 1)
                wait(dve, u3_mm, b)
                o = bank(7).rearrange("p (h d) -> p h d", d=32)
                V.reciprocal(rsum3, o[:, :, HD1]).then_inc(o3_r, 1)
                dve.wait_ge(o3_r, b + 1)
                for ct in range(DC):
                    last = V.tensor_tensor(
                        ctx3[:, ct * P:(ct + 1) * P].rearrange("p (w e d) -> p w e d", w=4, e=2),
                        o.rearrange("p (w c e) d -> p w c e d", w=4, c=2)[:, :, ct, :, 0:HD1],
                        rsum3.rearrange("p (w c e) -> p w c e", w=4, c=2)[:, :, ct].unsqueeze(3)
                        .to_broadcast([P, 4, 2, HD1]), ALU.mult)
                last.then_inc(o3_out, 1)

            def add3(g, i):
                s = stage(g, i, Y3, STEPS3, NG3)
                if s is None or s[1] % 4 != 3:
                    return
                b = 4 * s[0] + s[1] // 4
                dve.wait_ge(y3_mm, b + 1)
                xb = x[:, bass.ds(b, 1), :].rearrange("p a d -> p (a d)")
                V.tensor_tensor(xb, xb, bank(7)[:, D:2 * D], ALU.add).then_inc(y3_add, 1)

            def weights_lo(g, i):
                if not isinstance(g, int) or g > 0 or i >= W_TURNS:
                    return
                dve.wait_ge(w4_hi, i + 1)
                hi, lo, src = turned(i)
                if i == W_TURNS - 1:
                    V.tensor_tensor(lo, src, hi.bitcast(F32), ALU.subtract)
                    hi, lo, src = last_turn
                V.tensor_tensor(lo, src, hi.bitcast(F32), ALU.subtract).then_inc(w4_lo, 1)

            def quantise_x(g, i):
                for part in range(4):
                    s = stage(g, i, Y3 + part, STEPS3, NG3)
                    if s is None or s[1] % 4 != 3:
                        continue
                    b = 4 * s[0] + s[1] // 4

                    def link(ins, nth, then=dve.wait_ge):
                        ins.then_inc(x5, 1)
                        then(x5, 9 * b + nth)

                    xb = x[:, bass.ds(b, 1), :].rearrange("p a d -> p (a d)")
                    if part == 0:
                        wait_apart(dve, y3_add, b + 1)
                        link(V.bn_stats(st5, xb), 1, lambda sm, v: wait_apart(dve, sm, v))
                        V.bn_aggr(mv5, st5).then_inc(x5_stats, 1)
                    if part == 1:
                        dve.wait_ge(x5_rstd, b + 1)
                        link(V.tensor_scalar(xn5, xb, mv5[:, 0:1], ve5[:, 1:2], ALU.subtract, ALU.mult), 2)
                        link(V.tensor_reduce(s5[:, 0:1], xn5, AX.X, ALU.max, apply_absolute_value=True), 3)
                    if part == 2:
                        link(V.tensor_scalar(s5[:, 0:1], s5[:, 0:1], 1.0 / FP8_MAX, None, ALU.mult), 4)
                        link(V.reciprocal(s5[:, 1:2], s5[:, 0:1]), 5)
                        link(V.tensor_scalar(xn5, xn5, s5[:, 1:2], None, ALU.mult), 6)
                        link(V.tensor_scalar(m5.bitcast(U32), xn5.bitcast(U32), SIGN_EXP, None, ALU.bitwise_and), 7)
                    if part == 3:
                        link(V.tensor_scalar(m5, m5, 2.0 ** -6, ROUND_FP8, ALU.max, ALU.mult), 8)
                        link(V.tensor_tensor(xn5, xn5, m5, ALU.add), 9)
                        V.tensor_tensor(qx_all[:, bass.ds(b, 1), :].rearrange("p a d -> p (a d)"), xn5, m5,
                                        ALU.subtract)
                        V.tensor_copy(sx_all[:, bass.ds(b, 1)], s5[:, 0:1]).then_inc(qx_ready, 1)

            def body3(g, i):
                row_max3(g, i)
                weights_lo(g, i)
                normalise3(g, i)
                probs_out3(g, i)
                add3(g, i)
                quantise_x(g, i)

            pipeline(dve, NG3, STEPS3, body3)
            dve.wait_ge(qx_ready, NB)
            V.memset(unread[:], 0.0).then_inc(x5_done, 1)

            def seq_of(g, i, lag):
                s = stage(g, i, lag, STEPS4, NG4)
                return None if s is None else (STEPS4 * s[0] + s[1], s[1])

            def product(g, i, piece):
                s = seq_of(g, i, GU4)
                if s is None:
                    return
                f, k = s
                if piece == 0:
                    dve.wait_ge(up_mm, f + 1)
                    dve.wait_ge(silu_out, f + 1)
                    wait(dve, t_scaled, f)
                    V.scalar_tensor_tensor(tt.rearrange("p (k n) -> p k n", k=2), ps[:, 2:4, 0:FF // 2],
                                           sxg[:, k:k + 1], tsl.rearrange("p (k n) -> p k n", k=2),
                                           ALU.mult, ALU.mult).then_inc(t_prod, 1)
                if piece == 1:
                    dve.wait_ge(t_prod, f + 1)
                    V.tensor_reduce(st[:, k, 0:1], tt, AX.X, ALU.max, apply_absolute_value=True).then_inc(t_max, 1)
                if piece == 2:
                    dve.wait_ge(t_max, f + 1)
                    V.tensor_scalar(st[:, k, 0:1], st[:, k, 0:1], 1.0 / FP8_MAX, None, ALU.mult).then_inc(t_scale, 1)
                    dve.wait_ge(t_scale, f + 1)
                    V.reciprocal(st[:, k, 1:2], st[:, k, 0:1]).then_inc(t_recip, 1)

            def quantise_t(g, i, piece):
                s = seq_of(g, i, Q4)
                if s is None:
                    return
                f, k = s
                v = tv[:, k % 2, :]
                if piece == 0:
                    dve.wait_ge(t_scaled, f + 1)
                    wait(dve, t5_q, f)
                    V.tensor_scalar(tm.bitcast(U32), v.bitcast(U32), SIGN_EXP, None,
                                    ALU.bitwise_and).then_inc(t_expo, 1)
                if piece == 1:
                    dve.wait_ge(t_expo, f + 1)
                    V.tensor_scalar(tm, tm, 2.0 ** -6, ROUND_FP8, ALU.max, ALU.mult).then_inc(t_magic, 1)
                if piece == 2:
                    dve.wait_ge(t_sum, f + 1)
                    wait(dve, t5_mm, f - 1)
                    V.tensor_tensor(qt[:, k % 2, :], v, tm, ALU.subtract).then_inc(t5_q, 1)

            def add_ffn(g, i):
                s = seq_of(g, i, Y4)
                if s is None:
                    return
                f, k = s
                xb = x[:, bass.ds(f, 1), :].rearrange("p a d -> p (a d)")
                dve.wait_ge(y5_mm, f + 1)
                V.scalar_tensor_tensor(xb, bank(6)[:, 0:D], st[:, k, 0:1], xb, ALU.mult, ALU.add)\
                    .then_inc(x5_done, 1)

            def group_scales(g, i):
                s = stage(g, i, 0, STEPS4, NG4)
                if s is None or s[1] != 0:
                    return
                wait(dve, t_prod, STEPS4 * s[0])
                V.tensor_copy(sxg, sx_all[:, bass.ds(STEPS4 * s[0], STEPS4)]).then_inc(sxg_ready, 1)
                dve.wait_ge(sxg_ready, s[0] + 1)

            def body4(g, i):
                quantise_t(g, i, 0)
                quantise_t(g, i, 1)
                product(g, i, 0)
                group_scales(g, i)
                product(g, i, 1)
                product(g, i, 2)
                quantise_t(g, i, 2)
                add_ffn(g, i)

            pipeline(dve, NG4, STEPS4, body4)

        @block.gpsimd
        def _(pool):
            G = nc.gpsimd
            pool.wait_ge(ln_stats, 1)
            G.tensor_tensor(rstd[:], veps[:], mhalf[:], ALU.pow).then_inc(ln_rstd, 1)
            pool.wait_ge(ld_ctx, 16 * len(FIRST))
            hc = DCTX // 2
            tmp = kvd[:, :, 1, :]
            G.tensor_tensor(tmp[:, :, 0:hc], kv[:, :, hc:DCTX],
                            ropek_s[:, 0:hc].unsqueeze(1).to_broadcast([P, NB, hc]), ALU.mult)
            G.tensor_tensor(tmp[:, :, hc:DCTX], kv[:, :, 0:hc],
                            ropek_s[:, hc:DCTX].unsqueeze(1).to_broadcast([P, NB, hc]), ALU.mult)\
                .then_inc(kv_step, 1)
            pool.wait_ge(kv_step, 1)
            G.tensor_tensor(kv[:], kv[:], ropek_c[:].unsqueeze(1).to_broadcast([P, NB, DCTX]), ALU.mult).then_inc(kv_step, 1)
            pool.wait_ge(kv_step, 2)
            G.tensor_tensor(kv[:], kv[:], tmp, ALU.add).then_inc(kv_step, 1)
            barrier(pool, 1)

            def add_rope(g, i, h):
                s = stage(g, i, 0, NPAIR)
                if s is None:
                    return
                grp, p = s
                f = NPAIR * grp + p
                pool.wait_ge(q_scaled, 2 * f + h + 1)
                wait(pool, b_mm, f - 1)
                for half in range(2):
                    lo, other = half * GT, (1 - half) * GT
                    last = G.tensor_tensor(roped[:, p % 2, h, lo:lo + GT], t1[:, h, lo:lo + GT],
                                           t2[:, h, other:other + GT], ALU.add)
                last.then_inc(q_roped, 1)

            def rsqrt_var(g, i):
                s = stage(g, 0, 1, NPAIR)
                if s is None or i != Y_AT:
                    return
                grp = s[0]
                wait(pool, l_stats, grp + 1)
                G.tensor_tensor(veps[:, 0:GB], mv[:, 0:GB, 1], epst[:, 0:GB], ALU.add).then_inc(pool_step, 1)
                pool.wait_ge(pool_step, grp + 1)
                G.tensor_tensor(rstd[:, 0:GB], veps[:, 0:GB], mhalf[:, 0:GB], ALU.pow).then_inc(l_rstd, 1)

            def x_lo(g, i):
                s = stage(g, 0, 1, NPAIR)
                if i != G_AT:
                    return
                if s is None:
                    G.memset(unread_pool[:], 0.0).then_inc(l_lo, 1)
                    return
                tok = bass.ds(s[0] * GT, GT)
                wait(pool, l_out, s[0] + 1)
                G.tensor_tensor(xn_lo[:, :, tok], xgT, xn_hi[:, :, tok].bitcast(F32), ALU.subtract).then_inc(l_lo, 1)

            def body(g, i):
                add_rope(g, i, 0)
                add_rope(g, i, 1)
                rsqrt_var(g, i)
                x_lo(g, i)

            pipeline(pool, NG, NPAIR, body)
            barrier(pool, 2)

            def rsqrt2(g, i):
                s = stage(g, 0, 1, STEPS2, NG2)
                if s is None or i != 1:
                    return
                grp = s[0]
                wait(pool, n_stats, grp + 1)
                G.tensor_tensor(veps[:, 0:GB2], mv[:, 0:GB2, 1], epst[:, 0:GB2], ALU.add).then_inc(n_eps, 1)
                pool.wait_ge(n_eps, grp + 1)
                G.tensor_tensor(rstd[:, 0:GB2], veps[:, 0:GB2], mhalf[:, 0:GB2], ALU.pow).then_inc(n_rstd, 1)

            def gather(n):
                j, k = n // NF, n % NF
                ix = idx_a[:, k:k + 1] if k < NF - 1 else idx_b[:]
                if k == NF - 1:
                    pool.wait_ge(pad_set, 1)
                G.indirect_dma_start(
                    out=wgu_n[0:FCH[k][1], n, :], out_offset=None,
                    in_=a[("L1_ffn_w_gate", "L1_ffn_w_up")[j]],
                    in_offset=bass.IndirectOffsetOnAxis(ap=ix.bitcast(U32), axis=0)).then_inc(ld_g[n // 3], 16)

            def gathers(g, i):
                if not isinstance(g, int) or g > 0 or i > 3:
                    return
                if i == 0:
                    gather(6)
                    gather(7)
                    gather(8)
                else:
                    gather(8 + i)

            def expert_lo(e):
                if e < NE:
                    pool.wait_ge(fc_hi, e + 1)
                    G.tensor_tensor(fc2_lo[:, e], fc2[:, e], fc2_hi[:, e].bitcast(F32), ALU.subtract).then_inc(fc_lo, 1)

            def activations_lo(g, i):
                s = stage(g, i, 0, STEPS2, NG2)
                if s is None or i >= NE:
                    return
                grp, e = s
                n = (NE + 1) * grp + e
                wait(pool, f_mm, n - 1 if e >= 2 else n - 2)
                for m in range(IC):
                    pool.wait_ge(h_hi, IC * (NE * grp + e) + m + 1)
                    G.tensor_tensor(hT_lo[:, e % 2, m, :], hT[:, m, :], hT_hi[:, e % 2, m, :].bitcast(F32),
                                    ALU.subtract).then_inc(h_lo, 1)
                if isinstance(g, int):
                    expert_lo(e + 1)

            def body2(g, i):
                activations_lo(g, i)
                gathers(g, i)
                rsqrt2(g, i)

            pool.wait_ge(ld_i, 32)
            expert_lo(0)
            for n in range(6):
                gather(n)
            pipeline(pool, NG2, STEPS2, body2)
            barrier(pool, 3)

            def rsqrt_x(g, i):
                s = stage(g, i, Y3, STEPS3, NG3)
                if s is None or s[1] % 4 != 3:
                    return
                b = 4 * s[0] + s[1] // 4
                pool.wait_ge(x5_stats, b + 1)
                G.tensor_tensor(ve5[:, 0:1], mv5[:, 1:2], epst[:, 0:1], ALU.add).then_inc(x5_eps, 1)
                pool.wait_ge(x5_eps, b + 1)
                G.tensor_tensor(ve5[:, 1:2], ve5[:, 0:1], mhalf[:, 0:1], ALU.pow).then_inc(x5_rstd, 1)

            def sequence_values(g, i):
                s = stage(g, i, O3 - 3, STEPS3, NG3)
                if s is None or s[1] % 4 != 0:
                    return
                b = 4 * s[0] + s[1] // 4
                wait(pool, o3_mm, 4 * (b - 1))
                G.tensor_copy(vseq[:, s[1] // 4 % 2, :, 0:V1], vaug[:, bass.ds(b, 1), :, :]
                              .rearrange("p a h d -> p (a h) d")).then_inc(vseq_ready, 1)

            def body3(g, i):
                sequence_values(g, i)
                rsqrt_x(g, i)

            pool.wait_ge(vseq_set, 1)
            pipeline(pool, NG3, STEPS3, body3)

            def round_sum(g, i):
                s = stage(g, i, Q4, STEPS4, NG4)
                if s is None:
                    return
                f, v = STEPS4 * s[0] + s[1], tv[:, s[1] % 2, :]
                wait(pool, t_magic, f + 1)
                G.tensor_tensor(v, v, tm, ALU.add).then_inc(t_sum, 1)

            pipeline(pool, NG4, STEPS4, round_sum)


def rope_tables(length, dim):
    f32 = np.float32
    inv = (f32(1.0) / np.power(f32(10000.0), np.arange(0, dim, 2, dtype=f32) / f32(dim))).astype(f32)
    f = np.arange(length, dtype=f32)[:, None] * inv[None, :]
    return np.repeat(np.sin(f), 2, axis=-1), np.repeat(np.cos(f), 2, axis=-1)


def kernel(**inputs):
    import ml_dtypes
    import concourse.bacc as _bacc
    from concourse.bass_utils import run_bass_kernel_spmd as _run

    w = {k: np.asarray(v) for k, v in inputs.items()}
    c = np.ascontiguousarray

    def chunks(m):
        return c(m.reshape(-1, P, m.shape[-1]).transpose(1, 0, 2))

    arr = {"x": c(w["x"].transpose(1, 0, 2)), "ctx": c(w["ctx_512"].transpose(1, 0, 2)),
           "ctxT": c(w["ctx_512"].reshape(NB * P, DCTX).T)}
    arr["L0_xattn_Wq"] = c(w["L0_xattn_Wq"].reshape(H0, K0, D).transpose(1, 0, 2))
    arr["L0_xattn_w_kc_q"] = c(w["L0_xattn_w_kc_q"].transpose(1, 0, 2))
    arr["L0_xattn_w_kc_kv"] = c(w["L0_xattn_w_kc_kv"].transpose(1, 0, 2))

    def two_heads(m):
        return c(m.reshape(NPAIR, 2, m.shape[1], R0).transpose(1, 3, 0, 2).reshape(2 * R0, NPAIR, m.shape[1]))

    arr["L0_xattn_W_qr"], arr["L0_xattn_W_kr"] = two_heads(w["L0_xattn_W_qr"]), two_heads(w["L0_xattn_W_kr"])
    arr["L0_xattn_Wo"] = c(w["L0_xattn_Wo"].reshape(D, H0, K0).transpose(2, 1, 0))
    arr["L0_ffn_gate_w"] = chunks(w["L0_ffn_gate_w"])
    arr["L0_ffn_fc1_w"] = c(w["L0_ffn_fc1_w"].reshape(NE, DC, P, INTER).transpose(2, 0, 1, 3))
    arr["L0_ffn_fc2_w"] = c(w["L0_ffn_fc2_w"].reshape(NE, IC, P, D).transpose(2, 0, 1, 3))

    arr["L0_ffn_fc1_b"] = c(w["L0_ffn_fc1_b"].reshape(NE, IC, P).transpose(2, 0, 1))
    arr["L0_ffn_fc2_b"] = c(w["L0_ffn_fc2_b"])
    arr["L0_ffn_alpha"] = c(np.broadcast_to(w["L0_ffn_alpha"], (P, NE)))
    by_parity = np.zeros((P, DC, DC, 2, P // (2 * HD1), 2, HD1), np.float32)
    cols = chunks(w["L1_xattn_Wq"].T).reshape(P, DC, DC, P // (2 * HD1), 2, HD1)
    for e in range(2):
        by_parity[:, :, :, e, :, e] = cols[:, :, :, :, e]
    arr["L1_xattn_Wq"] = by_parity.reshape(P, DC, DC, 2, P)
    arr["L1_xattn_Wkv"] = c(w["L1_xattn_Wkv_expand"].T)
    arr["L1_xattn_Wout"] = chunks(w["L1_xattn_Wout"].T)
    arr["L1_ffn_w_gate"], arr["L1_ffn_w_up"] = c(w["L1_ffn_w_gate"]), c(w["L1_ffn_w_up"])
    arr["L1_ffn_w_down"] = chunks(w["L1_ffn_w_down"])
    di = w["L1_ffn_down_reorder_index"]
    whole = FF // P * P
    arr["idx_a"] = c(di[:whole].reshape(-1, P).T)
    arr["idx_b"] = c(di[whole:].reshape(-1, 1))
    arr["before"] = c(np.broadcast_to(np.tril(np.ones((NE, NE), np.float32), -1), (P, NE, NE)))

    sq, cq = rope_tables(P, DQ0)
    sk, ck = rope_tables(P, DCTX)
    two = (HALF, 2, GB, P)
    arr["rope_c"] = c(np.broadcast_to(cq.T.reshape(2, HALF, P).transpose(1, 0, 2)[:, :, None, :], two))
    ssw = np.stack([sq.T[HALF:], -sq.T[:HALF]], axis=1)
    arr["rope_s"] = c(np.broadcast_to(ssw[:, :, None, :], two))
    arr["ropek_c"] = c(ck)
    arr["ropek_s"] = c(np.concatenate([-sk[:, :DCTX // 2], sk[:, DCTX // 2:]], axis=1))
    arr["ident"] = np.eye(P, dtype=np.float32)
    arr["identb"] = np.eye(P).astype(ml_dtypes.bfloat16)
    causal = np.tril(np.ones((P, P), bool))
    arr["mask"] = c(np.broadcast_to(np.where(causal, 0.0, MASKED)[:, None, :], (P, 4, P)).astype(ml_dtypes.bfloat16))

    nc = _bacc.Bacc("TRN2", target_bir_lowering=False, num_devices=1)
    aps = {k: nc.dram_tensor(f"in_{k}", v.shape, mybir.dt.from_np(v.dtype), kind="ExternalInput").ap()
           for k, v in arr.items()}
    out = nc.dram_tensor("out_x", (P, NB, D), F32, kind="ExternalOutput").ap()
    build(nc, aps, out)
    r = _run(nc, [{f"in_{k}": v for k, v in arr.items()}], core_ids=[0])
    return c(r.results[0]["out_x"].transpose(1, 0, 2))
```
